# Optimizing a Trainium2 kernel written in Bass

```python
import numpy as np
import jax
import jax.numpy as jnp

def _softmax(x, axis=-1):
    return jax.nn.softmax(x, axis=axis)

def _gelu(x):
    return jax.nn.gelu(x, approximate=True)

def _silu(x):
    return jax.nn.silu(x)

def _sigmoid(x):
    return jax.nn.sigmoid(x)

def _layernorm(x, axis=-1, eps=1e-05):
    m = jnp.mean(x, axis=axis, keepdims=True)
    v = jnp.var(x, axis=axis, keepdims=True)
    return (x - m) / jnp.sqrt(v + eps)

def _scatter_add(tgt, idx, src, axis=0):
    return tgt.at[idx].add(src)

def _segment_sum(src, seg, n):
    return jax.ops.segment_sum(src, seg, n)
kernel_name = 'mk_xattn_ffn_d2_seqx_r8_41e3de'

def setup_inputs(seed: int=0):
    np.random.seed(seed)
    _w = jnp.asarray

    def _rec_inputs():
        import jax
        import jax.numpy as jnp
        _rk = jax.random.key(seed)
        x = 7.22e-05 + 1 * jax.random.normal(jax.random.fold_in(_rk, 1), (8, 128, 512), jnp.float32)
        _lenS = 128 - jax.random.randint(jax.random.fold_in(_rk, 7), (8,), 0, max(1, 128 // 4) + 1, jnp.int32)
        _lenS2 = 128 - jax.random.randint(jax.random.fold_in(_rk, 8), (8,), 0, max(1, 128 // 4) + 1, jnp.int32)
        _ctx_4096P = jax.random.normal(jax.random.fold_in(_rk, 11), (8, 16, 512), jnp.float32)
        _ctx_4096c = jax.random.dirichlet(jax.random.fold_in(_rk, 511), 0.3 * jnp.ones((16,), jnp.float32), (8, 128))
        _ctx_4096t = jnp.einsum('bsk,bkd->bsd', _ctx_4096c, _ctx_4096P)
        _ctx_4096t = _ctx_4096t * jax.lax.rsqrt(jnp.mean(jnp.square(_ctx_4096t)) + 1e-12) * 0.953939
        ctx_4096 = 4.13588e-05 + 0.999923 * (_ctx_4096t + 0.3 * jax.random.normal(jax.random.fold_in(_rk, 611), (8, 128, 512), jnp.float32))
        _validS = jnp.arange(128)[None, :] < _lenS[:, None]
        _validS2 = jnp.arange(128)[None, :] < _lenS2[:, None]
        _causal = jnp.tril(jnp.ones((128, 128), dtype=bool))
        mask_1x1xSxS2_bk0 = jnp.logical_not(jnp.broadcast_to(_validS2[0:1, None, None, :], (1, 1, 128, 128)))
        return (x, ctx_4096, mask_1x1xSxS2_bk0)
    x, ctx_4096, mask_1x1xSxS2_bk0 = _rec_inputs()

    def _L0_xattn_setup():
        import jax, jax.numpy as jnp
        import numpy as np
        DIM = 512
        NUM_HEADS = 32
        NUM_KV_HEADS = 8
        HEAD_DIM = DIM // NUM_HEADS
        KV_DIM = DIM // (NUM_HEADS // NUM_KV_HEADS)
        B, S = (1, 256)
        key = jax.random.key(seed)
        ks = jax.random.split(key, 7)
        w_scale = DIM ** (-0.5)
        return {'query': jax.random.normal(ks[0], (B, S, DIM), jnp.float32), 'key': jax.random.normal(ks[1], (B, S, DIM), jnp.float32), 'value': jax.random.normal(ks[2], (B, S, DIM), jnp.float32), 'Wq': jax.random.normal(ks[3], (DIM, DIM), jnp.float32) * w_scale, 'Wk': jax.random.normal(ks[4], (DIM, KV_DIM), jnp.float32) * w_scale, 'Wv': jax.random.normal(ks[5], (DIM, KV_DIM), jnp.float32) * w_scale, 'Wo': jax.random.normal(ks[6], (DIM, DIM), jnp.float32) * w_scale}
    _L0_xattn_all = _L0_xattn_setup()
    _L0_xattn_in = {k: v for k, v in _L0_xattn_all.items() if k in ('Wq', 'Wk', 'Wv', 'Wo')}
    del _L0_xattn_all

    def _L0_ffn_setup():
        import jax, jax.numpy as jnp
        import numpy as np
        BLK = 16
        FP8_MAX = 448.0
        GSCALE_DIV = 448.0 * 6.0
        SELECT = 128

        def _ste(x, q):
            return x + jax.lax.stop_gradient(q - x)

        def _fp8_block_qdq(v):
            lead, C = (v.shape[:-1], v.shape[-1])
            vb = v.reshape(*lead, C // BLK, BLK)
            s = jnp.maximum(jnp.max(jnp.abs(vb), axis=-1, keepdims=True) / FP8_MAX, 1e-08)
            q = (vb / s).astype(jnp.float8_e4m3fn).astype(jnp.float32) * s
            return _ste(vb, q).reshape(*lead, C)

        def _int4_block_qdq(w):
            out, C = w.shape
            wb = w.reshape(out, C // BLK, BLK)
            s = jnp.maximum(jnp.max(jnp.abs(wb), axis=-1, keepdims=True) / 7.0, 1e-08)
            q = jnp.round(jnp.clip(wb / s, -8.0, 7.0)) * s
            return _ste(wb, q).reshape(out, C)

        def _quant_act(x2d, reorder_index, select_num):
            g = jnp.maximum(jnp.max(jnp.abs(x2d)) / GSCALE_DIV, 1e-08)
            xr = (x2d / g)[:, reorder_index]
            n = xr.shape[1] - select_num
            normal = _fp8_block_qdq(xr[:, :n])
            outl = xr[:, n:]
            q1 = _fp8_block_qdq(outl)
            q2 = _fp8_block_qdq(outl - q1)
            A = jnp.concatenate([normal, q1, q2], axis=1)
            return (A, g)

        def _quant_w(w, reorder_index, select_num):
            wr = w[:, reorder_index]
            n = wr.shape[1] - select_num
            wq = jnp.concatenate([wr[:, :n], wr[:, n:], wr[:, n:]], axis=1)
            return _int4_block_qdq(wq)
        key = jax.random.key(seed)
        k0, k1, k2, k3 = jax.random.split(key, 4)
        B, L, H, I = (2, 256, 512, 1376)
        return {'x': jax.random.normal(k0, (B, L, H), dtype=jnp.float32), 'w_gate': jax.random.normal(k1, (I, H), dtype=jnp.float32) * 0.02, 'w_up': jax.random.normal(k2, (I, H), dtype=jnp.float32) * 0.02, 'w_down': jax.random.normal(k3, (H, I), dtype=jnp.float32) * 0.02, 'ri_in': jnp.arange(H, dtype=jnp.int32), 'ri_mid': jnp.arange(I, dtype=jnp.int32)}
    _L0_ffn_all = _L0_ffn_setup()
    _L0_ffn_in = {k: v for k, v in _L0_ffn_all.items() if k in ('w_gate', 'w_up', 'w_down', 'ri_in', 'ri_mid')}
    del _L0_ffn_all

    def _L1_xattn_setup():
        import jax, jax.numpy as jnp
        import numpy as np
        B, T, D_MODEL = (1, 256, 512)
        NUM_Q_HEADS, NUM_KV_HEADS, KEY_SIZE = (32, 8, 128)
        ATTN_MULT = 0.08838834764831845
        MAX_ATTN_VAL = 30.0

        def rotate_half(x):
            x1, x2 = jnp.split(x, 2, axis=-1)
            return jnp.concatenate((-x2, x1), axis=-1)

        def apply_rope(x):
            b, t, h, d = x.shape
            exponents = jnp.arange(0, d, 2, dtype=jnp.float32)
            inv_freq = 1.0 / 10000.0 ** (exponents / d)
            pos = jnp.arange(t, dtype=jnp.float32)
            phase = pos[:, None] * inv_freq[None, :]
            phase = jnp.tile(phase, (1, 2))[None, :, None, :]
            return (x * jnp.cos(phase) + rotate_half(x) * jnp.sin(phase)).astype(x.dtype)
        key = jax.random.key(seed)
        ks = jax.random.split(key, 8)
        query = jax.random.normal(ks[0], (B, T, D_MODEL), dtype=jnp.float32)
        kk = jax.random.normal(ks[1], (B, T, D_MODEL), dtype=jnp.float32)
        vv = jax.random.normal(ks[2], (B, T, D_MODEL), dtype=jnp.float32)
        mask = jnp.tril(jnp.ones((T, T), dtype=bool))[None, None, :, :]
        s = 0.02
        Wq = jax.random.normal(ks[3], (D_MODEL, NUM_Q_HEADS * KEY_SIZE), dtype=jnp.float32) * s
        Wk = jax.random.normal(ks[4], (D_MODEL, NUM_KV_HEADS * KEY_SIZE), dtype=jnp.float32) * s
        Wv = jax.random.normal(ks[5], (D_MODEL, NUM_KV_HEADS * KEY_SIZE), dtype=jnp.float32) * s
        Wo = jax.random.normal(ks[6], (NUM_Q_HEADS * KEY_SIZE, D_MODEL), dtype=jnp.float32) * s
        return {'query': query, 'key': kk, 'value': vv, 'mask': mask, 'Wq': Wq, 'Wk': Wk, 'Wv': Wv, 'Wo': Wo}
    _L1_xattn_all = _L1_xattn_setup()
    _L1_xattn_in = {k: v for k, v in _L1_xattn_all.items() if k in ('Wq', 'Wk', 'Wv', 'Wo')}
    del _L1_xattn_all

    def _L1_ffn_setup():
        import jax, jax.numpy as jnp
        import numpy as np

        def _block_dequantize_mixed(packed, scale, mask):
            q_lo = packed & 15
            q_hi = packed >> 4 & 15
            q = jnp.stack([q_lo, q_hi], axis=-1).reshape(packed.shape[0], -1)
            scale_eff = scale.astype(jnp.float32) * jnp.where(mask[:, None], 1.0, 0.5)
            return (q.astype(jnp.float32) - 8.0) * scale_eff
        key = jax.random.key(seed)
        k1, k2, k3, k4, k5 = jax.random.split(key, 5)
        B, S, IN, OUT, G = (8, 256, 512, 512, 32)
        NB = OUT * IN // G
        x = jax.random.normal(k1, (B, S, IN), dtype=jnp.float32)
        weight_packed = jax.random.randint(k2, (NB, G // 2), 0, 32, dtype=jnp.int32)
        weight_scale = (jax.random.uniform(k3, (NB, 1)) * 0.02).astype(jnp.float16)
        weight_var_mask = jax.random.randint(k4, (NB,), 0, 2) > 0
        bias = jax.random.normal(k5, (OUT,), dtype=jnp.float32)
        return {'x': x, 'weight_packed': weight_packed, 'weight_scale': weight_scale, 'weight_var_mask': weight_var_mask, 'bias': bias}
    _L1_ffn_all = _L1_ffn_setup()
    _L1_ffn_in = {k: v for k, v in _L1_ffn_all.items() if k in ('weight_packed', 'weight_scale', 'weight_var_mask', 'bias')}
    del _L1_ffn_all
    return {'x': x, 'ctx_4096': ctx_4096, 'mask_1x1xSxS2_bk0': mask_1x1xSxS2_bk0, 'L0_xattn_Wq': _L0_xattn_in['Wq'], 'L0_xattn_Wk': _L0_xattn_in['Wk'], 'L0_xattn_Wv': _L0_xattn_in['Wv'], 'L0_xattn_Wo': _L0_xattn_in['Wo'], 'L0_ffn_w_gate': _L0_ffn_in['w_gate'], 'L0_ffn_w_up': _L0_ffn_in['w_up'], 'L0_ffn_w_down': _L0_ffn_in['w_down'], 'L0_ffn_ri_in': _L0_ffn_in['ri_in'], 'L0_ffn_ri_mid': _L0_ffn_in['ri_mid'], 'L1_xattn_Wq': _L1_xattn_in['Wq'], 'L1_xattn_Wk': _L1_xattn_in['Wk'], 'L1_xattn_Wv': _L1_xattn_in['Wv'], 'L1_xattn_Wo': _L1_xattn_in['Wo'], 'L1_ffn_weight_packed': _L1_ffn_in['weight_packed'], 'L1_ffn_weight_scale': _L1_ffn_in['weight_scale'], 'L1_ffn_weight_var_mask': _L1_ffn_in['weight_var_mask'], 'L1_ffn_bias': _L1_ffn_in['bias']}

def reference(x, ctx_4096, mask_1x1xSxS2_bk0, L0_xattn_Wq, L0_xattn_Wk, L0_xattn_Wv, L0_xattn_Wo, L0_ffn_w_gate, L0_ffn_w_up, L0_ffn_w_down, L0_ffn_ri_in, L0_ffn_ri_mid, L1_xattn_Wq, L1_xattn_Wk, L1_xattn_Wv, L1_xattn_Wo, L1_ffn_weight_packed, L1_ffn_weight_scale, L1_ffn_weight_var_mask, L1_ffn_bias):
    import jax
    import jax.numpy as jnp

    def _L0_xattn_ref(query, key, value, Wq, Wk, Wv, Wo):
        import jax, jax.numpy as jnp
        import numpy as np
        DIM = 512
        NUM_HEADS = 32
        NUM_KV_HEADS = 8
        HEAD_DIM = DIM // NUM_HEADS
        KV_DIM = DIM // (NUM_HEADS // NUM_KV_HEADS)
        B, S = (1, 256)
        b, sq, _ = query.shape
        _, sk, _ = key.shape
        rep = NUM_HEADS // NUM_KV_HEADS
        q = (query @ Wq).reshape(b, sq, NUM_HEADS, HEAD_DIM).transpose(0, 2, 1, 3)
        k = (key @ Wk).reshape(b, sk, NUM_KV_HEADS, HEAD_DIM).transpose(0, 2, 1, 3)
        v = (value @ Wv).reshape(b, sk, NUM_KV_HEADS, HEAD_DIM).transpose(0, 2, 1, 3)
        k = jnp.repeat(k, rep, axis=1)
        v = jnp.repeat(v, rep, axis=1)
        scale = HEAD_DIM ** (-0.5)
        scores = jnp.einsum('bhqd,bhkd->bhqk', q, k) * scale
        probs = jax.nn.softmax(scores, axis=-1)
        out = jnp.einsum('bhqk,bhkd->bhqd', probs, v)
        out = out.transpose(0, 2, 1, 3).reshape(b, sq, DIM)
        return out @ Wo

    def _L0_ffn_ref(x, w_gate, w_up, w_down, ri_in, ri_mid):
        import jax, jax.numpy as jnp
        import numpy as np
        BLK = 16
        FP8_MAX = 448.0
        GSCALE_DIV = 448.0 * 6.0
        SELECT = 128

        def _ste(x, q):
            return x + jax.lax.stop_gradient(q - x)

        def _fp8_block_qdq(v):
            lead, C = (v.shape[:-1], v.shape[-1])
            vb = v.reshape(*lead, C // BLK, BLK)
            s = jnp.maximum(jnp.max(jnp.abs(vb), axis=-1, keepdims=True) / FP8_MAX, 1e-08)
            q = (vb / s).astype(jnp.float8_e4m3fn).astype(jnp.float32) * s
            return _ste(vb, q).reshape(*lead, C)

        def _int4_block_qdq(w):
            out, C = w.shape
            wb = w.reshape(out, C // BLK, BLK)
            s = jnp.maximum(jnp.max(jnp.abs(wb), axis=-1, keepdims=True) / 7.0, 1e-08)
            q = jnp.round(jnp.clip(wb / s, -8.0, 7.0)) * s
            return _ste(wb, q).reshape(out, C)

        def _quant_act(x2d, reorder_index, select_num):
            g = jnp.maximum(jnp.max(jnp.abs(x2d)) / GSCALE_DIV, 1e-08)
            xr = (x2d / g)[:, reorder_index]
            n = xr.shape[1] - select_num
            normal = _fp8_block_qdq(xr[:, :n])
            outl = xr[:, n:]
            q1 = _fp8_block_qdq(outl)
            q2 = _fp8_block_qdq(outl - q1)
            A = jnp.concatenate([normal, q1, q2], axis=1)
            return (A, g)

        def _quant_w(w, reorder_index, select_num):
            wr = w[:, reorder_index]
            n = wr.shape[1] - select_num
            wq = jnp.concatenate([wr[:, :n], wr[:, n:], wr[:, n:]], axis=1)
            return _int4_block_qdq(wq)
        B, L, H = x.shape
        x2 = x.reshape(B * L, H)
        A, g = _quant_act(x2, ri_in, SELECT)
        Wg = _quant_w(w_gate, ri_in, SELECT)
        Wu = _quant_w(w_up, ri_in, SELECT)
        gate = A @ Wg.T * g
        up = A @ Wu.T * g
        h = jax.nn.silu(gate) * up
        Am, gm = _quant_act(h, ri_mid, SELECT)
        Wd = _quant_w(w_down, ri_mid, SELECT)
        y = Am @ Wd.T * gm
        return y.reshape(B, L, -1)

    def _L1_xattn_ref(query, key, value, mask, Wq, Wk, Wv, Wo):
        import jax, jax.numpy as jnp
        import numpy as np
        B, T, D_MODEL = (1, 256, 512)
        NUM_Q_HEADS, NUM_KV_HEADS, KEY_SIZE = (32, 8, 128)
        ATTN_MULT = 0.08838834764831845
        MAX_ATTN_VAL = 30.0

        def rotate_half(x):
            x1, x2 = jnp.split(x, 2, axis=-1)
            return jnp.concatenate((-x2, x1), axis=-1)

        def apply_rope(x):
            b, t, h, d = x.shape
            exponents = jnp.arange(0, d, 2, dtype=jnp.float32)
            inv_freq = 1.0 / 10000.0 ** (exponents / d)
            pos = jnp.arange(t, dtype=jnp.float32)
            phase = pos[:, None] * inv_freq[None, :]
            phase = jnp.tile(phase, (1, 2))[None, :, None, :]
            return (x * jnp.cos(phase) + rotate_half(x) * jnp.sin(phase)).astype(x.dtype)
        b, t, _ = query.shape
        d = KEY_SIZE
        h, kv_h = (NUM_Q_HEADS, NUM_KV_HEADS)
        g = h // kv_h
        q = (query @ Wq).reshape(b, t, h, d)
        k = (key @ Wk).reshape(b, t, kv_h, d)
        v = (value @ Wv).reshape(b, t, kv_h, d)
        q = apply_rope(q)
        k = apply_rope(k)
        q = q.reshape(b, t, kv_h, g, d)
        logits = jnp.einsum('btkgd,bTkd->bkgtT', q, k).astype(jnp.float32)
        logits = logits * ATTN_MULT
        logits = MAX_ATTN_VAL * jnp.tanh(logits / MAX_ATTN_VAL)
        m = mask[:, :, None, :, :]
        logits = jnp.where(m, logits, -1e+30)
        weights = jax.nn.softmax(logits, axis=-1).astype(query.dtype)
        attn = jnp.einsum('bkgtT,bTkd->btkgd', weights, v)
        attn = attn.reshape(b, t, h * d)
        return attn @ Wo

    def _L1_ffn_ref(x, weight_packed, weight_scale, weight_var_mask, bias):
        import jax, jax.numpy as jnp
        import numpy as np

        def _block_dequantize_mixed(packed, scale, mask):
            q_lo = packed & 15
            q_hi = packed >> 4 & 15
            q = jnp.stack([q_lo, q_hi], axis=-1).reshape(packed.shape[0], -1)
            scale_eff = scale.astype(jnp.float32) * jnp.where(mask[:, None], 1.0, 0.5)
            return (q.astype(jnp.float32) - 8.0) * scale_eff
        out_features = bias.shape[0]
        in_features = x.shape[-1]
        w = _block_dequantize_mixed(weight_packed, weight_scale, weight_var_mask)
        w = w.reshape(out_features, in_features)
        return jnp.einsum('bsi,oi->bso', x, w) + bias
    x = x + _L0_xattn_ref(_layernorm(x, axis=-1), ctx_4096, ctx_4096, L0_xattn_Wq, L0_xattn_Wk, L0_xattn_Wv, L0_xattn_Wo)
    x = x + _L0_ffn_ref(_layernorm(x, axis=-1), L0_ffn_w_gate, L0_ffn_w_up, L0_ffn_w_down, L0_ffn_ri_in, L0_ffn_ri_mid)
    x = x + _L1_xattn_ref(_layernorm(x, axis=-1), ctx_4096, ctx_4096, mask_1x1xSxS2_bk0, L1_xattn_Wq, L1_xattn_Wk, L1_xattn_Wv, L1_xattn_Wo)
    x = x + _L1_ffn_ref(_layernorm(x, axis=-1), L1_ffn_weight_packed, L1_ffn_weight_scale, L1_ffn_weight_var_mask, L1_ffn_bias)
    return x

_drawn_inputs = setup_inputs


def setup_inputs(seed=0):
    import zlib

    import numpy as np

    out = dict(_drawn_inputs(seed))
    spreads = {}
    factors = {}
    for name, (base, spread) in spreads.items():
        noise = np.random.default_rng([zlib.crc32(name.encode()), seed]).standard_normal(out[name].shape)
        drawn = base * np.exp(spread * noise) if base else spread * noise
        out[name] = jnp.asarray(drawn.astype(out[name].dtype))
    for name, factor in factors.items():
        out[name] = (out[name] * factor).astype(out[name].dtype)
    return out
```

```python
from contextlib import ExitStack

import numpy as np

import concourse.bass as bass
from concourse import mybir

F32 = mybir.dt.float32
F32R = mybir.dt.float32r
I32 = mybir.dt.int32
ALU = mybir.AluOpType
ACT = mybir.ActivationFunctionType
AX = mybir.AxisListType

P = 128
B = 8
D = 512
KC = D // P
EPS = 1e-5
H0, G0, E0 = 32, 8, 16
J0 = H0 // G0
PAIRS = G0 // 2
STACK = 4 * E0
VC = E0 + 1


def mm3(pe, out, ah, al, bh, bl, start, stop):
    pe.matmul(out, ah, bh, start=start, stop=False)
    pe.matmul(out, ah, bl, start=False, stop=False)
    return pe.matmul(out, al, bh, start=False, stop=stop)


def program(nc, t, stop_after):
    with ExitStack() as whole:
        held = []

        def sem(name):
            held.append(nc.alloc_semaphore(name))
            return held[-1]

        def release():
            nc.clear_and_free_semaphores(held)
            held.clear()
            nc.all_engine_barrier()

        def sb_in(stack):
            return lambda name, shape, dt=F32: stack.enter_context(nc.sbuf_tensor(name, shape, dt))

        keep = sb_in(whole)
        scratch = {n: nc.dram_tensor("w_" + n, s, F32, kind="Internal").ap()
                   for n, s in (("gate", (I0, D)), ("up", (I0, D)), ("down", (D, I0)))}
        ps = whole.enter_context(nc.psum_tensor("ps", [P, 8, 512], F32))
        ident = keep("ident", [P, P])
        X = keep("X", [P, B, D])
        stats = keep("stats", [P, B, 6])
        mv = keep("mv", [P, B, 2])
        rstd = keep("rstd", [P, B, 1])
        minus_half = keep("minus_half", [P, B, 1])
        CTh = keep("CTh", [P, KC, B * P], F32R)
        CTl = keep("CTl", [P, KC, B * P], F32R)

        with ExitStack() as layer0:
            kw = layer0_setup(nc, t, sem, sb_in(layer0), ps, ident, X, stats, mv, rstd, minus_half, CTh, CTl)
            layer0_attention(nc, sem, ps, ident, X, stats, mv, rstd, **kw)
        release()
        if stop_after >= 2:
            layer0_ffn(nc, t, sem, ps, ident, X, stats, mv, rstd, minus_half, scratch)
            release()
        if stop_after >= 3:
            with ExitStack() as attention:
                sb = sb_in(attention)
                tables, bias = sb("tables", [P, 2, J1 + 1, E1]), sb("bias", [P, P])
                XTh, XTl = sb("XTh", [P, B, KC, P], F32R), sb("XTl", [P, B, KC, P], F32R)
                layer1_tables(nc, t, sem, ps, ident, tables, bias)
                normalize_rows(nc, sem, ps, ident, X, mv, rstd, minus_half, XTh, XTl)
                layer1_attention(nc, t, sem, ps, X, stats, mv, ident, CTh, CTl, XTh, XTl, tables, bias)
        if stop_after >= 4:
            return layer1_ffn(nc, t, sem, ps, ident, X, mv, rstd, minus_half)
        if stop_after:
            return finish(nc, t, sem, X)


def finish(nc, t, sem, X):
    stored = sem("stored")
    with nc.Block() as block:
        @block.sync
        def _(sp):
            sp.dma_start(t["out"].rearrange("b p d -> p b d"), X[:]).then_inc(stored, 16)
            sp.wait_ge(stored, 16)


def layer0_setup(nc, t, sem, sb, ps, ident, X, stats, mv, rstd, minus_half, CTh, CTl):
    KT = sb("KT", [P, B, PAIRS, P], F32R)
    V = sb("V", [P, B, G0, VC])
    Wq = [sb(f"Wq{s}", [P, KC, D], F32R) for s in "hl"]
    Wo = [sb(f"Wo{s}", [P, KC, D], F32R) for s in "hl"]
    with ExitStack() as here:
        own = sb_in_stack(nc, here)
        ctx_in = own("ctx_in", [P, B, D])
        w_in = own("w_in", [P, 2, KC, D])
        wkv_in = own("wkv_in", [P, KC, 2 * P])
        Wkv = [own(f"Wkv{s}", [P, KC, 2 * P], F32R) for s in "hl"]
        KS = own("KS", [P, 2, G0, STACK], F32R)
        ctx_loaded = [sem(f"ctx_loaded{b}") for b in range(B)]
        x_loaded, wkv_loaded, w_loaded = sem("x_loaded"), sem("wkv_loaded"), sem("w_loaded")
        ident_zero, ident_ready, half_ready = sem("ident_zero"), sem("ident_ready"), sem("half_ready")
        wkv_hi, wkv_lo, w_hi, w_lo = sem("wkv_hi"), sem("wkv_lo"), sem("w_hi"), sem("w_lo")
        ct_psum, ct_hi, ct_lo = sem("ct_psum"), sem("ct_hi"), sem("ct_lo")
        kv_psum, kv_hi, kv_lo, ks_full = sem("kv_psum"), sem("kv_hi"), sem("kv_lo"), sem("ks_full")
        v_ready, v_ones = sem("v_ready"), sem("v_ones")
        kt_psum, kt_ready = sem("kt_psum"), sem("kt_ready")
        stat_ready, mv_ready, rstd_ready = sem("stat_ready"), sem("mv_ready"), sem("rstd_ready")

        tr = lambda b: ps[:, b % 2, :]
        kv = lambda b: ps[:, 2 + b % 2, 0:2 * P]
        kt = lambda b: ps[:, 4 + b % 2, :]

        with nc.Block() as block:
            @block.sync
            def _(sp):
                sp.dma_start(ctx_in[:, 0], t["ctx_4096"][0]).then_inc(ctx_loaded[0], 16)
                sp.dma_start(wkv_in[:, :, 0:P], t["L0_xattn_Wk"].rearrange("(k p) n -> p k n", p=P)).then_inc(wkv_loaded, 16)
                sp.dma_start(wkv_in[:, :, P:2 * P], t["L0_xattn_Wv"].rearrange("(k p) n -> p k n", p=P)).then_inc(wkv_loaded, 16)
                for b in range(1, B):
                    sp.dma_start(ctx_in[:, b], t["ctx_4096"][b]).then_inc(ctx_loaded[b], 16)
                sp.dma_start(X[:], t["x"].rearrange("b p d -> p b d")).then_inc(x_loaded, 16)
                sp.dma_start(w_in[:, 0], t["L0_xattn_Wq"].rearrange("(k p) n -> p k n", p=P)).then_inc(w_loaded, 16)
                sp.dma_start(w_in[:, 1], t["L0_xattn_Wo"].rearrange("(k p) n -> p k n", p=P)).then_inc(w_loaded, 16)

            @block.gpsimd
            def _(pool):
                pool.memset(ident[:], 0.0).then_inc(ident_zero, 1)
                pool.wait_ge(ident_zero, 1)
                pool.affine_select(out=ident[:], in_=ident[:], compare_op=ALU.not_equal, fill=1.0, base=0,
                                   pattern=[[-1, P]], channel_multiplier=1).then_inc(ident_ready, 1)
                pool.memset(minus_half[:], -0.5).then_inc(half_ready, 1)
                pool.memset(V[:, :, :, E0:VC], 1.0).then_inc(v_ones, 1)
                pool.wait_ge(wkv_hi, 1)
                pool.tensor_tensor(Wkv[1][:], wkv_in[:], Wkv[0][:].bitcast(F32), ALU.subtract).then_inc(wkv_lo, 1)
                for b in range(B):
                    pool.wait_ge(kv_hi, b + 1)
                    pool.wait_ge(kv_lo, b + 1)
                    v = KS[:, b % 2].bitcast(F32).rearrange("p g (a c e) -> p g a c e", a=2, c=2)
                    o = KS[:, b % 2].rearrange("p g (a c e) -> p g a c e", a=2, c=2)
                    pool.tensor_copy(o[:, :, :, 1], v[:, :, :, 0]).then_inc(ks_full, 1)
                pool.wait_ge(w_hi, 2)
                pool.tensor_tensor(Wq[1][:], w_in[:, 0], Wq[0][:].bitcast(F32), ALU.subtract).then_inc(w_lo, 1)
                pool.tensor_tensor(Wo[1][:], w_in[:, 1], Wo[0][:].bitcast(F32), ALU.subtract).then_inc(w_lo, 1)
                pool.wait_ge(mv_ready, B)
                pool.wait_ge(half_ready, 1)
                pool.tensor_tensor(rstd[:], rstd[:], minus_half[:], ALU.pow).then_inc(rstd_ready, 1)

            @block.scalar
            def _(act):
                act.wait_ge(wkv_loaded, 32)
                act.activation(Wkv[0][:], wkv_in[:], ACT.Copy).then_inc(wkv_hi, 1)

                def keys(b):
                    act.wait_ge(kv_psum, b + 1)
                    if b >= 2:
                        act.wait_ge(kt_psum, b - 1)
                    act.activation(KS[:, b % 2, :, 0:E0], kv(b)[:, 0:P].rearrange("p (g e) -> p g e", g=G0),
                                   ACT.Copy).then_inc(kv_hi, 1)
                    act.activation(V[:, b, :, 0:E0], kv(b)[:, P:2 * P].rearrange("p (g e) -> p g e", g=G0),
                                   ACT.Copy).then_inc(v_ready, 1)

                def keys_out(b):
                    act.wait_ge(kt_psum, b + 1)
                    act.activation(KT[:, b], kt(b), ACT.Copy).then_inc(kt_ready, 1)

                for b in range(B + 2):
                    if b < B:
                        act.wait_ge(ct_psum, b + 1)
                        act.activation(CTh[:, :, b * P:(b + 1) * P], tr(b).rearrange("p (k n) -> p k n", k=KC),
                                       ACT.Copy).then_inc(ct_hi, 1)
                    if 1 <= b <= B:
                        keys(b - 1)
                    if b >= 2:
                        keys_out(b - 2)
                act.wait_ge(w_loaded, 32)
                act.activation(Wq[0][:], w_in[:, 0], ACT.Copy).then_inc(w_hi, 1)
                act.activation(Wo[0][:], w_in[:, 1], ACT.Copy).then_inc(w_hi, 1)

            @block.vector
            def _(dve):
                def keys_lo(b):
                    dve.wait_ge(v_ready, b + 1)
                    if b >= 2:
                        dve.wait_ge(kt_psum, b - 1)
                    dve.tensor_tensor(KS[:, b % 2, :, 2 * E0:3 * E0], kv(b)[:, 0:P].rearrange("p (g e) -> p g e", g=G0),
                                      KS[:, b % 2, :, 0:E0].bitcast(F32), ALU.subtract).then_inc(kv_lo, 1)

                for b in range(B + 1):
                    if b < B:
                        dve.wait_ge(ct_hi, b + 1)
                        dve.tensor_tensor(CTl[:, :, b * P:(b + 1) * P], tr(b).rearrange("p (k n) -> p k n", k=KC),
                                          CTh[:, :, b * P:(b + 1) * P].bitcast(F32), ALU.subtract).then_inc(ct_lo, 1)
                    if b >= 1:
                        keys_lo(b - 1)
                dve.wait_ge(x_loaded, 16)
                for b in range(B):
                    dve.bn_stats(stats[:, b], X[:, b]).then_inc(stat_ready, 1)
                for b in range(B):
                    dve.wait_ge(stat_ready, b + 1)
                    dve.bn_aggr(mv[:, b], stats[:, b]).then_inc(stat_ready, 1)
                dve.wait_ge(stat_ready, 2 * B)
                dve.tensor_scalar(rstd[:], mv[:, :, 1:2], EPS, None, ALU.add).then_inc(mv_ready, B)

            @block.tensor
            def _(pe):
                def project(b):
                    pe.wait_ge(ct_hi, b + 1)
                    pe.wait_ge(ct_lo, b + 1)
                    if b >= 2:
                        pe.wait_ge(kv_lo, b - 1)
                        pe.wait_ge(v_ready, b - 1)
                    for k in range(KC):
                        last = mm3(pe, kv(b), CTh[:, k, b * P:(b + 1) * P], CTl[:, k, b * P:(b + 1) * P],
                                   Wkv[0][:, k], Wkv[1][:, k], k == 0, k == KC - 1)
                    last.then_inc(kv_psum, 1)

                def turn_keys(b):
                    pe.wait_ge(ks_full, b + 1)
                    if b >= 2:
                        pe.wait_ge(kt_ready, b - 1)
                    for pr in range(PAIRS):
                        last = pe.transpose(kt(b)[:, pr * P:(pr + 1) * P],
                                            KS[:, b % 2, 2 * pr:2 * pr + 2].bitcast(F32).rearrange("p g c -> p (g c)"),
                                            ident[:])
                    last.then_inc(kt_psum, 1)

                pe.wait_ge(ident_ready, 1)
                for b in range(B + 2):
                    if b < B:
                        pe.wait_ge(ctx_loaded[b], 16)
                        if b >= 2:
                            pe.wait_ge(ct_lo, b - 1)
                        for k in range(KC):
                            last = pe.transpose(tr(b)[:, k * P:(k + 1) * P], ctx_in[:, b, k * P:(k + 1) * P], ident[:])
                        last.then_inc(ct_psum, 1)
                    if b == 0:
                        pe.wait_ge(wkv_lo, 1)
                    if 1 <= b <= B:
                        project(b - 1)
                    if b >= 2:
                        turn_keys(b - 2)
    return dict(KT=KT, V=V, Wq=Wq, Wo=Wo, sb=sb)


def sb_in_stack(nc, stack):
    return lambda name, shape, dt=F32: stack.enter_context(nc.sbuf_tensor(name, shape, dt))


def layer0_attention(nc, sem, ps, ident, X, stats, mv, rstd, KT, V, Wq, Wo, sb):
    xh = sb("xh", [P, 2, D])
    XTh, XTl = sb("XTh0", [P, 2, KC, P], F32R), sb("XTl0", [P, 2, KC, P], F32R)
    QS = sb("QS", [P, 2, H0, STACK], F32R)
    QT = sb("QT", [P, 2, PAIRS, J0 * P], F32R)
    KTb = sb("KTb", [P, 2, PAIRS, P], F32R)
    Vb = sb("Vb", [P, 2, G0, VC])
    mx = sb("mx", [P, 2, 2 * J0])
    PR = sb("PR", [P, 2, 2 * J0 * P])
    PT = sb("PT", [P, 2, J0 * P])
    rden = sb("rden", [P, H0 // 2])
    O = sb("O", [P, 2, D])
    OTh, OTl = sb("OTh", [P, KC, P], F32R), sb("OTl", [P, KC, P], F32R)

    xh_ready, xt_psum, xt_hi, xt_lo = sem("a_xh_ready"), sem("a_xt_psum"), sem("a_xt_hi"), sem("a_xt_lo")
    q_psum, qs_hi, qs_lo, qs_full = sem("a_q_psum"), sem("a_qs_hi"), sem("a_qs_lo"), sem("a_qs_full")
    qt_psum, qt_ready, kv_staged = sem("a_qt_psum"), sem("a_qt_ready"), sem("a_kv_staged")
    s_psum, mx_ready, s_shifted, p_ready = sem("a_s_psum"), sem("a_mx_ready"), sem("a_s_shifted"), sem("a_p_ready")
    pt_psum, pt_ready, pv_done = sem("a_pt_psum"), sem("a_pt_ready"), sem("a_pv_done")
    rden_ready, o_ready = sem("a_rden_ready"), sem("a_o_ready")
    ot_psum, ot_hi, ot_lo = sem("a_ot_psum"), sem("a_ot_hi"), sem("a_ot_lo")
    zero, zero_ready = sb("zero", [P, 1]), sem("a_zero_ready")
    y_psum, x_added, stat_done = sem("a_y_psum"), sem("a_x_added"), sem("a_stat_done")

    psA = ps[:, 0, :]
    psB = ps[:, 1, :]
    psS = lambda n: ps[:, 2 + 2 * (n % 2):4 + 2 * (n % 2), :]
    psT = ps[:, 6, :]
    psO = ps[:, 7, 0:H0 // 2 * VC].rearrange("p (h e) -> p h e", e=VC)

    with nc.Block() as block:
        @block.tensor
        def _(pe):
            def x_and_q(b, u):
                pe.wait_ge(xh_ready, b + 1)
                if not isinstance(b, int) or b:
                    pe.wait_ge(qt_ready, b * PAIRS)
                    pe.wait_ge(ot_lo, b - 1)
                for k in range(KC):
                    last = pe.transpose(psA[:, k * P:(k + 1) * P], xh[:, u, k * P:(k + 1) * P], ident[:])
                last.then_inc(xt_psum, 1)
                pe.wait_ge(xt_hi, b + 1)
                pe.wait_ge(xt_lo, b + 1)
                if not isinstance(b, int) or b:
                    pe.wait_ge(x_added, b - 1)
                for k in range(KC):
                    last = mm3(pe, psB, XTh[:, u, k], XTl[:, u, k], Wq[0][:, k], Wq[1][:, k], k == 0, k == KC - 1)
                last.then_inc(q_psum, 1)

            def turn_q(b, u):
                pe.wait_ge(qs_full, b + 1)
                for pr in range(PAIRS):
                    need(pe, qt_ready, b * PAIRS + pr)
                    for j in range(J0):
                        src = QS[:, u, 2 * (pr * J0 + j):2 * (pr * J0 + j + 1)].bitcast(F32).rearrange("p h c -> p (h c)")
                        last = pe.transpose(psA[:, j * P:(j + 1) * P], src, ident[:])
                    last.then_inc(qt_psum, 1)

            def scores(b, u, pr):
                pe.wait_ge(qt_ready, b * PAIRS + pr + 1)
                pe.wait_ge(kv_staged, 2 * (b + 1))
                pe.wait_ge(s_shifted, b * PAIRS + pr + 1)
                out = psS(pr).rearrange("p g (j k) -> p g j k", j=J0)
                for g in range(2):
                    r = slice(g * STACK, (g + 1) * STACK)
                    for j in range(J0):
                        last = pe.matmul(out[:, g, j], QT[r, u, pr, j * P:(j + 1) * P], KTb[r, u, pr],
                                         start=True, stop=True)
                last.then_inc(s_psum, 1)

            def weigh(b, u, pr):
                pe.wait_ge(p_ready, b * PAIRS + pr + 1)
                if pr % 2 == 0:
                    need(pe, o_ready, 2 * b + pr // 2)
                for g in range(2):
                    n = (b * PAIRS + pr) * 2 + g
                    need(pe, pt_ready, n)
                    for j in range(J0):
                        last = pe.transpose(psT[:, j * P:(j + 1) * P],
                                            PR[:, pr % 2, (g * J0 + j) * P:(g * J0 + j + 1) * P], ident[:])
                    last.then_inc(pt_psum, 1)
                    pe.wait_ge(pt_ready, n + 1)
                    for j in range(J0):
                        last = pe.matmul(psO[:, ((pr % 2) * 2 + g) * J0 + j], PT[:, g, j * P:(j + 1) * P],
                                         Vb[:, u, 2 * pr + g], start=True, stop=True)
                    last.then_inc(pv_done, 1)

            def project(b, u):
                pe.wait_ge(o_ready, 2 * b + 2)
                for k in range(KC):
                    last = pe.transpose(psA[:, k * P:(k + 1) * P], O[:, u, k * P:(k + 1) * P], ident[:])
                last.then_inc(ot_psum, 1)
                pe.wait_ge(ot_hi, b + 1)
                pe.wait_ge(ot_lo, b + 1)
                for k in range(KC):
                    last = mm3(pe, psB, OTh[:, k], OTl[:, k], Wo[0][:, k], Wo[1][:, k], k == 0, k == KC - 1)
                last.then_inc(y_psum, 1)

            def body(pe, b, u, more):
                scores(b, u, 0)
                scores(b, u, 1)
                weigh(b, u, 0)
                scores(b, u, 2)
                weigh(b, u, 1)
                if more:
                    x_and_q(b + 1, 1 - u)
                scores(b, u, 3)
                weigh(b, u, 2)
                weigh(b, u, 3)
                if more:
                    turn_q(b + 1, 1 - u)
                    pe.wait_ge(qt_ready, (b + 2) * PAIRS)
                project(b, u)

            pe.sem_inc(s_shifted, 2)
            x_and_q(0, 0)
            turn_q(0, 0)
            rows_loop(body)(pe)

        @block.scalar
        def _(act):
            def x_and_q(b, u):
                act.wait_ge(xt_psum, b + 1)
                act.activation(XTh[:, u], psA.rearrange("p (k n) -> p k n", k=KC), ACT.Copy).then_inc(xt_hi, 1)
                act.wait_ge(q_psum, b + 1)
                act.activation(QS[:, u, :, 0:E0], psB.rearrange("p (h e) -> p h e", h=H0), ACT.Copy).then_inc(qs_hi, 1)

            def turn_q(b, u):
                for pr in range(PAIRS):
                    act.wait_ge(qt_psum, b * PAIRS + pr + 1)
                    act.activation(QT[:, u, pr], psA, ACT.Copy).then_inc(qt_ready, 1)

            def exps(b, pr):
                act.wait_ge(s_shifted, b * PAIRS + pr + 3)
                act.activation(PR[:, pr % 2], PR[:, pr % 2], ACT.Exp, scale=float(E0) ** -0.5).then_inc(p_ready, 1)

            def turned(b, pr):
                for g in range(2):
                    n = (b * PAIRS + pr) * 2 + g
                    act.wait_ge(pt_psum, n + 1)
                    act.wait_ge(pv_done, n + 1)
                    act.activation(PT[:, g], psT, ACT.Copy).then_inc(pt_ready, 1)

            def body(act, b, u, more):
                exps(b, 0)
                exps(b, 1)
                turned(b, 0)
                exps(b, 2)
                turned(b, 1)
                if more:
                    x_and_q(b + 1, 1 - u)
                exps(b, 3)
                turned(b, 2)
                turned(b, 3)
                if more:
                    turn_q(b + 1, 1 - u)
                act.wait_ge(ot_psum, b + 1)
                need(act, y_psum, b)
                act.activation(OTh[:], psA.rearrange("p (k n) -> p k n", k=KC), ACT.Copy).then_inc(ot_hi, 1)

            act.sem_inc(pv_done, 2)
            x_and_q(0, 0)
            turn_q(0, 0)
            rows_loop(body)(act)

        @block.gpsimd
        def _(pool):
            def stage(b, u):
                pool.tensor_copy(KTb[:, u], KT[:, b].bitcast(F32)).then_inc(kv_staged, 1)
                pool.tensor_copy(Vb[:, u], V[:, b]).then_inc(kv_staged, 1)

            def body(pool, b, u, more):
                if more:
                    need(pool, x_added, b)
                    stage(b + 1, 1 - u)
                    dup(b + 1, 1 - u)

            def dup(b, u):
                pool.wait_ge(qs_hi, b + 1)
                pool.wait_ge(qs_lo, b + 1)
                pool.tensor_tensor(QS[:, u, :, 2 * E0:4 * E0], QS[:, u, :, 0:2 * E0].bitcast(F32),
                                   bcast(bcast(zero[:, 0], H0), 2 * E0), ALU.add).then_inc(qs_full, 1)

            pool.memset(zero[:], 0.0).then_inc(zero_ready, 1)
            pool.wait_ge(zero_ready, 1)
            stage(0, 0)
            dup(0, 0)
            rows_loop(body)(pool)

        @block.vector
        def _(dve):
            def normalize(b, u):
                dve.tensor_scalar(xh[:, u], X[:, b], mv[:, b, 0:1], rstd[:, b],
                                  ALU.subtract, ALU.mult).then_inc(xh_ready, 1)

            def x_and_q(b, u):
                dve.wait_ge(xt_hi, b + 1)
                dve.tensor_tensor(XTl[:, u], psA.rearrange("p (k n) -> p k n", k=KC), XTh[:, u].bitcast(F32),
                                  ALU.subtract).then_inc(xt_lo, 1)
                dve.wait_ge(qs_hi, b + 1)
                dve.tensor_tensor(QS[:, u, :, E0:2 * E0], psB.rearrange("p (h e) -> p h e", h=H0),
                                  QS[:, u, :, 0:E0].bitcast(F32), ALU.subtract).then_inc(qs_lo, 1)

            def shift(b, pr):
                n = b * PAIRS + pr
                dve.wait_ge(s_psum, n + 1)
                s = psS(pr).rearrange("p g (j k) -> p g j k", j=J0)
                m = mx[:, pr % 2].rearrange("p (g j) -> p g j", g=2)
                dve.tensor_reduce(m, s, AX.X, ALU.max).then_inc(mx_ready, 1)
                dve.wait_ge(mx_ready, n + 1)
                need(dve, pv_done, 2 * n)
                dve.tensor_tensor(PR[:, pr % 2].rearrange("p (g j k) -> p g j k", g=2, j=J0), s,
                                  bcast(m, P),
                                  ALU.subtract).then_inc(s_shifted, 1)

            def norm(b, u, half):
                n = 2 * b + half
                dve.wait_ge(pv_done, 4 * n + 6)
                dve.reciprocal(rden[:], psO[:, :, E0]).then_inc(rden_ready, 1)
                dve.wait_ge(rden_ready, n + 1)
                dve.tensor_tensor(O[:, u, half * (D // 2):(half + 1) * (D // 2)].rearrange("p (h e) -> p h e", e=E0),
                                  psO[:, :, 0:E0], bcast(rden[:], E0), ALU.mult).then_inc(o_ready, 1)

            def body(dve, b, u, more):
                shift(b, 0)
                shift(b, 1)
                if more:
                    normalize(b + 1, 1 - u)
                shift(b, 2)
                norm(b, u, 0)
                if more:
                    x_and_q(b + 1, 1 - u)
                shift(b, 3)
                norm(b, u, 1)
                dve.wait_ge(ot_hi, b + 1)
                dve.tensor_tensor(OTl[:], psA.rearrange("p (k n) -> p k n", k=KC), OTh[:].bitcast(F32),
                                  ALU.subtract).then_inc(ot_lo, 1)
                dve.wait_ge(y_psum, b + 1)
                dve.tensor_tensor(X[:, b], psB, X[:, b], ALU.add).then_inc(x_added, 1)
                dve.wait_ge(x_added, b + 1)
                dve.bn_stats(stats[:, b], X[:, b]).then_inc(stat_done, 1)

            normalize(0, 0)
            x_and_q(0, 0)
            rows_loop(body)(dve)
            for b in range(B):
                dve.wait_ge(stat_done, b + 1)
                dve.bn_aggr(mv[:, b], stats[:, b]).then_inc(stat_done, 1)


def bcast(ap, n):
    return ap.unsqueeze(len(ap.shape)).broadcast_to([*ap.shape, n])

I0 = 1376
IT = [(r, min(P, I0 - r)) for r in range(0, I0, P)]
IC = [(c, min(512, I0 - c)) for c in range(0, I0, 512)]
BLK = 16
SELECT = 128
FP8_MAX = 448.0
INT4_MAX = 7.0
LEAST = 1e-8
ROUND_INT = 1.5 * 2.0 ** 23
EXPONENT = 0x7F800000
FP8_LEAST_NORMAL = 2.0 ** -6
FP8_STEP = 1.5 * 2.0 ** (23 - 3)


def layer0_quantize_weights(nc, t, sem, ps, ident, scratch):
    with ExitStack() as here:
        sb = sb_in_stack(nc, here)
        idx_in, idx_mid = sb("idx_in", [P, KC], I32), sb("idx_mid", [P, len(IT)], I32)
        G = {"gate": sb("Gg", [P, KC, I0]), "up": sb("Gu", [P, KC, I0]), "down": sb("Gd", [P, len(IT), D])}
        NB = 512 // BLK
        bm, sc, rs = (sb(n, [P, 2, NB]) for n in ("bm", "sc", "rs"))
        Vq = sb("Vq", [P, 4, 512])
        Wq = sb("Wqz", [P, 4, 512])
        idx_loaded, gathered = sem("idx_loaded"), {k: sem("gathered_" + k) for k in G}
        w_turned, bm_ready, sc_ready, rs_ready = sem("w_turned"), sem("bm_ready"), sem("sc_ready"), sem("rs_ready")
        v_scaled, v_clipped, v_rounded, w_ready = sem("v_scaled"), sem("v_clipped"), sem("v_rounded"), sem("w_ready")
        w_stored = [sem(f"w_stored{n}") for n in range(4)]

        units = []
        for name in ("gate", "up"):
            for r, rows in IT:
                units.append((name, [(k * P, P, G[name][:, k, r:r + rows]) for k in range(KC)], r, rows, 0))
        for r in range(0, D, P):
            for c, n in IC:
                units.append(("down", [(m - c, w, G["down"][0:w, m // P, r:r + P]) for m, w in IT if c <= m < c + n],
                              r, P, c))
        width = [sum(w for _, w, _ in u[1]) for u in units]
        bank = lambda n: ps[:, n % 4, :]

        with nc.Block() as block:
            @block.sync
            def _(sp):
                sp.dma_start(idx_in[:], t["ri_in_columns"]).then_inc(idx_loaded, 16)
                full = I0 // P
                sp.dma_start(idx_mid[:, 0:full], t["ri_mid_columns"]).then_inc(idx_loaded, 16)
                sp.dma_start(idx_mid[0:I0 - full * P, full:full + 1], t["ri_mid_rest"]).then_inc(idx_loaded, 16)
                for n, (name, parts, r, rows, c) in enumerate(units):
                    sp.wait_ge(w_ready, n + 1)
                    sp.dma_start(scratch[name][r:r + rows, c:c + width[n]], Wq[0:rows, n % 4, 0:width[n]])\
                        .then_inc(w_stored[n % 4], 16)
                for q in range(4):
                    sp.wait_ge(w_stored[q], 16 * len(range(q, len(units), 4)))

            @block.gpsimd
            def _(pool):
                pool.wait_ge(idx_loaded, 48)
                for name, src in (("gate", t["L0_ffn_w_gate"]), ("up", t["L0_ffn_w_up"])):
                    for k in range(KC):
                        pool.indirect_dma_start(G[name][:, k], None, src,
                                                bass.IndirectOffsetOnAxis(ap=idx_in[:, k:k + 1], axis=0))\
                            .then_inc(gathered[name], 16)
                for m, (_, w) in enumerate(IT):
                    pool.indirect_dma_start(G["down"][0:w, m], None, t["L0_ffn_w_down"],
                                            bass.IndirectOffsetOnAxis(ap=idx_mid[0:w, m:m + 1], axis=0))\
                        .then_inc(gathered["down"], 16)

                def clip(n):
                    rows, w = units[n][3], width[n]
                    pool.wait_ge(v_scaled, n + 1)
                    pool.tensor_scalar(Vq[0:rows, n % 4, 0:w], Vq[0:rows, n % 4, 0:w], INT4_MAX, -INT4_MAX - 1,
                                       ALU.min, ALU.max).then_inc(v_clipped, 1)

                def scale(n):
                    rows, w = units[n][3], width[n]
                    pool.wait_ge(v_rounded, n + 1)
                    if n >= 4:
                        pool.wait_ge(w_stored[n % 4], 16 * (n // 4))
                    pool.tensor_tensor(Wq[0:rows, n % 4, 0:w].rearrange("p (b e) -> p b e", e=BLK),
                                       Vq[0:rows, n % 4, 0:w].rearrange("p (b e) -> p b e", e=BLK),
                                       bcast(sc[0:rows, n % 2, 0:w // BLK], BLK), ALU.mult).then_inc(w_ready, 1)

                for n in range(len(units) + 1):
                    if n < len(units):
                        clip(n)
                    if n >= 1:
                        scale(n - 1)

            @block.vector
            def _(dve):
                def first(n):
                    rows, w = units[n][3], width[n]
                    nb = w // BLK
                    src = bank(n)[0:rows, 0:w].rearrange("p (b e) -> p b e", e=BLK)
                    dve.wait_ge(w_turned, n + 1)
                    dve.tensor_reduce(bm[0:rows, n % 2, 0:nb], src, AX.X, ALU.max, apply_absolute_value=True).then_inc(bm_ready, 1)
                    dve.wait_ge(bm_ready, n + 1)
                    if n >= 2:
                        dve.wait_ge(w_ready, n - 1)
                    dve.tensor_scalar(sc[0:rows, n % 2, 0:nb], bm[0:rows, n % 2, 0:nb], 1.0 / INT4_MAX, LEAST,
                                      ALU.mult, ALU.max).then_inc(sc_ready, 1)
                    dve.wait_ge(sc_ready, n + 1)
                    dve.reciprocal(rs[0:rows, n % 2, 0:nb], sc[0:rows, n % 2, 0:nb]).then_inc(rs_ready, 1)
                    dve.wait_ge(rs_ready, n + 1)
                    dve.tensor_tensor(Vq[0:rows, n % 4, 0:w].rearrange("p (b e) -> p b e", e=BLK), src,
                                      bcast(rs[0:rows, n % 2, 0:nb], BLK), ALU.mult).then_inc(v_scaled, 1)

                def second(n):
                    rows, w = units[n][3], width[n]
                    dve.wait_ge(v_clipped, n + 1)
                    dve.tensor_scalar(Vq[0:rows, n % 4, 0:w], Vq[0:rows, n % 4, 0:w], ROUND_INT, -ROUND_INT,
                                      ALU.add, ALU.add).then_inc(v_rounded, 1)

                for n in range(len(units) + 1):
                    if n < len(units):
                        first(n)
                    if n >= 1:
                        second(n - 1)

            @block.tensor
            def _(pe):
                pe.wait_ge(gathered["gate"], 16 * KC)
                for n, (name, parts, r, rows, c) in enumerate(units):
                    if name == "up" and r == 0:
                        pe.wait_ge(gathered["up"], 16 * KC)
                    if name == "down" and r == c == 0:
                        pe.wait_ge(gathered["down"], 16 * len(IT))
                    if n >= 4:
                        pe.wait_ge(v_scaled, n - 3)
                    for at, w, src in parts:
                        k = src.shape[0]
                        last = pe.transpose(bank(n)[0:rows, at:at + w], src, ident[0:k, 0:k])
                    last.then_inc(w_turned, 1)


def quantize_fp8(dve, link, V, E, bits):
    e = E.bitcast(I32)
    link(dve.tensor_scalar(e, V.bitcast(I32), bits, None, ALU.bitwise_and))
    link(dve.tensor_scalar(E, E, FP8_LEAST_NORMAL, FP8_STEP, ALU.max, ALU.mult))
    link(dve.tensor_tensor(V, V, E, ALU.add))
    link(dve.tensor_tensor(V, V, E, ALU.subtract))


class Chain:
    def __init__(self, eng, sem):
        self.eng, self.sem, self.base, self.n, self.per = eng, sem, 0, 0, None

    def row(self, b):
        if self.n and self.per is None:
            self.per = self.n
        if self.per is not None:
            assert self.n == self.per
            self.base = b * self.per
        self.n = 0

    def __call__(self, ins):
        self.n += 1
        ins.then_inc(self.sem, 1)
        self.eng.wait_ge(self.sem, self.base + self.n)


def blocks(ap):
    return ap.rearrange("p (b e) -> p b e", e=BLK)


def quantize_rows(dve, link, src, inv, sc, V, E, R, A, bm, g_inv, width):
    n = width - SELECT
    ob = SELECT // BLK
    link(dve.tensor_tensor(blocks(V[:, 0:width]), blocks(src), bcast(inv, BLK), ALU.mult))
    quantize_fp8(dve, link, V[:, 0:width], E[:, 0:width], EXPONENT)
    link(dve.tensor_tensor(blocks(A), blocks(V[:, 0:width]), bcast(sc, BLK), ALU.mult))
    link(dve.scalar_tensor_tensor(R, src[:, n:width], g_inv, A[:, n:width], ALU.mult, ALU.subtract))
    link(dve.tensor_reduce(bm[:, 0], blocks(R), AX.X, ALU.max, apply_absolute_value=True))
    link(dve.tensor_scalar(bm[:, 1], bm[:, 0], 1.0 / FP8_MAX, LEAST, ALU.mult, ALU.max))
    link(dve.reciprocal(bm[:, 2], bm[:, 1]))
    link(dve.tensor_tensor(blocks(V[:, 0:SELECT]), blocks(R), bcast(bm[:, 2], BLK), ALU.mult))
    quantize_fp8(dve, link, V[:, 0:SELECT], E[:, 0:SELECT], EXPONENT)
    link(dve.tensor_tensor(blocks(V[:, 0:SELECT]), blocks(V[:, 0:SELECT]), bcast(bm[:, 1], BLK), ALU.mult))
    return dve.tensor_tensor(A[:, n:width], A[:, n:width], V[:, 0:SELECT], ALU.add)


def rows_loop(body):
    def run(eng):
        body(eng, 0, 0, True)
        with eng.Fori(0, B // 2 - 1) as i:
            for u in (1, 0):
                body(eng, i * 2 + (2 - u), u, True)
        body(eng, B - 1, 1, False)
    return run


def need(eng, sem, value):
    if not isinstance(value, int) or value > 0:
        eng.wait_ge(sem, value)


def ffn0_gather_x(nc, t, sem, ps, ident, X, mv, rstd, minus_half, H, xb, g):
    with ExitStack() as here:
        sb = sb_in_stack(nc, here)
        xh = sb("g_xh", [P, 2, D])
        XTh, XTl = sb("g_XTh", [P, 2, KC, P], F32R), sb("g_XTl", [P, 2, KC, P], F32R)
        ri, rif, pid, pidf = sb("ri", [P, D], I32), sb("rif", [P, D]), sb("pid", [P, KC], I32), sb("pidf", [P, KC])
        pick = sb("pick", [P, KC, D], F32R)
        names = "ri_loaded pid_ready rif_ready pick_ready eps_added rstd_ready xh_ready xt_psum xt_hi xt_lo xg_psum xg_copied xb_ready"
        S = {n: sem("g_" + n) for n in names.split()}
        psA = lambda u: ps[:, u, :]
        psG = lambda u: ps[:, 2 + u, :]
        with nc.Block() as block:
            @block.sync
            def _(sp):
                sp.dma_start(ri[:], t["L0_ffn_ri_in"].partition_broadcast(P)).then_inc(S["ri_loaded"], 16)

            @block.gpsimd
            def _(pool):
                pool.iota(pid[:], [[P, KC]], base=0, channel_multiplier=1).then_inc(S["pid_ready"], 1)
                pool.wait_ge(S["eps_added"], 1)
                pool.tensor_tensor(rstd[:], rstd[:], minus_half[:], ALU.pow).then_inc(S["rstd_ready"], 1)

            @block.tensor
            def _(pe):
                def turn(b, u):
                    pe.wait_ge(S["xh_ready"], b + 1)
                    pe.wait_ge(S["xt_lo"], b)
                    for k in range(KC):
                        last = pe.transpose(psA(u)[:, k * P:(k + 1) * P], xh[:, u, k * P:(k + 1) * P], ident[:])
                    last.then_inc(S["xt_psum"], 1)

                def body(pe, b, u, more):
                    if more:
                        turn(b + 1, 1 - u)
                    pe.wait_ge(S["xt_hi"], b + 1)
                    pe.wait_ge(S["xt_lo"], b + 2)
                    pe.wait_ge(S["xb_ready"], b + 1)
                    for k in range(KC):
                        pe.matmul(psG(u), XTh[:, u, k], pick[:, k], start=k == 0, stop=False)
                        last = pe.matmul(psG(u), XTl[:, u, k], pick[:, k], start=False, stop=k == KC - 1)
                    last.then_inc(S["xg_psum"], 1)

                pe.sem_inc(S["xt_lo"], 1)
                pe.sem_inc(S["xb_ready"], 2)
                turn(0, 0)
                pe.wait_ge(S["pick_ready"], KC)
                rows_loop(body)(pe)

            @block.scalar
            def _(act):
                def hi(b, u):
                    act.wait_ge(S["xt_psum"], b + 1)
                    act.activation(XTh[:, u], psA(u).rearrange("p (k n) -> p k n", k=KC), ACT.Copy).then_inc(S["xt_hi"], 1)

                def body(act, b, u, more):
                    if more:
                        hi(b + 1, 1 - u)
                    act.wait_ge(S["xg_psum"], b + 1)
                    act.activation(H[:, b, 0:D], psG(u), ACT.Copy).then_inc(S["xg_copied"], 1)

                hi(0, 0)
                rows_loop(body)(act)

            @block.vector
            def _(dve):
                link = Chain(dve, sem("g_link"))
                dve.wait_ge(S["ri_loaded"], 16)
                link(dve.tensor_copy(rif[:], ri[:]))
                dve.wait_ge(S["pid_ready"], 1)
                link(dve.tensor_copy(pidf[:], pid[:]))
                for k in range(KC):
                    dve.tensor_scalar(pick[:, k], rif[:], pidf[:, k:k + 1], None, ALU.is_equal).then_inc(S["pick_ready"], 1)
                dve.tensor_scalar(rstd[:], mv[:, :, 1:2], EPS, None, ALU.add).then_inc(S["eps_added"], 1)

                def lo(b, u):
                    dve.tensor_scalar(xh[:, u], X[:, b], mv[:, b, 0:1], rstd[:, b], ALU.subtract, ALU.mult)\
                       .then_inc(S["xh_ready"], 1)
                    dve.wait_ge(S["xt_hi"], b + 1)
                    dve.tensor_tensor(XTl[:, u], psA(u).rearrange("p (k n) -> p k n", k=KC), XTh[:, u].bitcast(F32),
                                      ALU.subtract).then_inc(S["xt_lo"], 1)

                def body(dve, b, u, more):
                    if more:
                        lo(b + 1, 1 - u)
                    dve.wait_ge(S["xg_copied"], b + 1)
                    dve.tensor_reduce(xb[:, b], blocks(psG(u)), AX.X, ALU.max, apply_absolute_value=True)\
                       .then_inc(S["xb_ready"], 1)

                dve.wait_ge(S["rstd_ready"], 1)
                lo(0, 0)
                rows_loop(body)(dve)
    whole_scale(nc, sem, xb, g, "x")


def whole_scale(nc, sem, bm, g, tag):
    part, reduced = sem(tag + "_max_part"), sem(tag + "_max_whole")
    with nc.Block() as block:
        @block.vector
        def _(dve):
            dve.tensor_reduce(g[:, 4:5], bm[:], AX.XY, ALU.max).then_inc(part, 1)
            link = Chain(dve, sem(tag + "_scale_link"))
            dve.wait_ge(reduced, 1)
            link(dve.tensor_scalar(g[:, 0:1], g[:, 5:6], 1.0 / (FP8_MAX * 6.0), LEAST, ALU.mult, ALU.max))
            link(dve.reciprocal(g[:, 1:2], g[:, 0:1]))
            link(dve.tensor_scalar(g[:, 2:3], g[:, 0:1], 0.5, None, ALU.mult))
            link(dve.tensor_scalar(g[:, 3:4], g[:, 2:3], g[:, 0:1], None, ALU.mult))

        @block.gpsimd
        def _(pool):
            pool.wait_ge(part, 1)
            pool.partition_all_reduce(g[:, 5:6], g[:, 4:5], P, bass.bass_isa.ReduceOp.max).then_inc(reduced, 1)


def ffn0_load_up(nc, t, sem, ps, ident, scratch, W):
    with ExitStack() as here:
        sb = sb_in_stack(nc, here)
        idx = sb("idx_mid2", [P, len(IT)], I32)
        NR = 3
        R = sb("wrows", [P, NR, D])
        idx_loaded, wt_psum, wt_hi, wt_lo = sem("idx2_loaded"), sem("wt_psum"), sem("wt_hi"), sem("wt_lo")
        fetched = [sem(f"wrows_fetched{q}") for q in range(NR)]
        units = [(m, r, rows) for m in range(2) for r, rows in IT]
        bank = lambda n: ps[:, n % 4, :].rearrange("p (k n) -> p k n", k=KC)
        with nc.Block() as block:
            @block.sync
            def _(sp):
                full = I0 // P
                sp.dma_start(idx[:, 0:full], t["ri_mid_columns"]).then_inc(idx_loaded, 16)
                sp.dma_start(idx[0:I0 - full * P, full:full + 1], t["ri_mid_rest"]).then_inc(idx_loaded, 16)

            @block.gpsimd
            def _(pool):
                pool.wait_ge(idx_loaded, 32)
                for n, (m, r, rows) in enumerate(units):
                    if n >= NR:
                        pool.wait_ge(wt_psum, n - NR + 1)
                    pool.indirect_dma_start(R[0:rows, n % NR], None, scratch[("gate", "up")[m]],
                                            bass.IndirectOffsetOnAxis(ap=idx[0:rows, r // P:r // P + 1], axis=0))\
                        .then_inc(fetched[n % NR], 16)

            @block.tensor
            def _(pe):
                for n, (m, r, rows) in enumerate(units):
                    pe.wait_ge(fetched[n % NR], 16 * (n // NR + 1))
                    if n >= 4:
                        pe.wait_ge(wt_lo, n - 3)
                    for k in range(KC):
                        last = pe.transpose(bank(n)[:, k, 0:rows], R[0:rows, n % NR, k * P:(k + 1) * P], ident[0:rows, 0:rows])
                    last.then_inc(wt_psum, 1)

            @block.scalar
            def _(act):
                for n, (m, r, rows) in enumerate(units):
                    act.wait_ge(wt_psum, n + 1)
                    act.activation(W[m][0][:, :, r:r + rows], bank(n)[:, :, 0:rows], ACT.Copy).then_inc(wt_hi, 1)

            @block.vector
            def _(dve):
                for n, (m, r, rows) in enumerate(units):
                    dve.wait_ge(wt_hi, n + 1)
                    dve.tensor_tensor(W[m][1][:, :, r:r + rows], bank(n)[:, :, 0:rows],
                                      W[m][0][:, :, r:r + rows].bitcast(F32), ALU.subtract).then_inc(wt_lo, 1)


def block_scales(dve, link, bm, g, s, inv):
    link(dve.tensor_scalar(s, bm, g[:, 1:2], None, ALU.mult))
    link(dve.tensor_scalar(s, s, 1.0 / FP8_MAX, LEAST, ALU.mult, ALU.max))
    link(dve.reciprocal(inv, s))
    link(dve.tensor_scalar(inv, inv, g[:, 1:2], None, ALU.mult))


def ffn0_up(nc, sem, ps, ident, W, H, hb, xb, g):
    with ExitStack() as here:
        sb = sb_in_stack(nc, here)
        V, E, R, A = sb("u_V", [P, D]), sb("u_E", [P, D]), sb("u_R", [P, SELECT]), sb("u_A", [P, 2, D])
        sc, inv, bm = sb("u_sc", [P, D // BLK]), sb("u_inv", [P, D // BLK]), sb("u_bm", [P, 3, SELECT // BLK])
        ATh, ATl = sb("u_ATh", [P, 2, KC, P], F32R), sb("u_ATl", [P, 2, KC, P], F32R)
        T = sb("u_T", [P, I0])
        names = "a_ready at_psum at_hi at_lo gate_psum up_psum tanh_ready u_ready h_ready hb_ready"
        S = {n: sem("u_" + n) for n in names.split()}
        psA = lambda u: ps[:, u, :]
        gate = ps[:, 2:5, :].rearrange("p c n -> p (c n)")
        up = ps[:, 5:8, :].rearrange("p c n -> p (c n)")
        with nc.Block() as block:
            @block.tensor
            def _(pe):
                def turn(b, u):
                    pe.wait_ge(S["a_ready"], b + 1)
                    pe.wait_ge(S["at_lo"], b)
                    for k in range(KC):
                        last = pe.transpose(psA(u)[:, k * P:(k + 1) * P], A[:, u, k * P:(k + 1) * P], ident[:])
                    last.then_inc(S["at_psum"], 1)

                def product(out, u, w):
                    for c, n in IC:
                        for k in range(KC):
                            last = mm3(pe, out[:, c:c + n], ATh[:, u, k], ATl[:, u, k], w[0][:, k, c:c + n],
                                       w[1][:, k, c:c + n], k == 0, k == KC - 1)
                    return last

                def body(pe, b, u, more):
                    pe.wait_ge(S["at_hi"], b + 1)
                    pe.wait_ge(S["at_lo"], b + 2)
                    need(pe, S["u_ready"], b)
                    product(gate, u, W[0]).then_inc(S["gate_psum"], 1)
                    if more:
                        turn(b + 1, 1 - u)
                    need(pe, S["h_ready"], b)
                    product(up, u, W[1]).then_inc(S["up_psum"], 1)

                pe.sem_inc(S["at_lo"], 1)
                turn(0, 0)
                rows_loop(body)(pe)

            @block.scalar
            def _(act):
                def hi(b, u):
                    act.wait_ge(S["at_psum"], b + 1)
                    act.wait_ge(S["up_psum"], b)
                    act.activation(ATh[:, u], psA(u).rearrange("p (k n) -> p k n", k=KC), ACT.Copy).then_inc(S["at_hi"], 1)

                def body(act, b, u, more):
                    act.wait_ge(S["gate_psum"], b + 1)
                    need(act, S["h_ready"], b)
                    act.activation(T[:], gate[:, 0:I0], ACT.Tanh, scale=g[:, 2:3]).then_inc(S["tanh_ready"], 1)
                    if more:
                        hi(b + 1, 1 - u)

                act.sem_inc(S["up_psum"], 1)
                hi(0, 0)
                rows_loop(body)(act)

            @block.vector
            def _(dve):
                link = Chain(dve, sem("u_link"))

                def quantize(b, u):
                    link.row(b)
                    block_scales(dve, link, xb[:, b], g, sc[:], inv[:])
                    quantize_rows(dve, link, H[:, b, 0:D], inv[:], sc[:], V, E, R[:], A[:, u], bm, g[:, 1:2], D)\
                        .then_inc(S["a_ready"], 1)

                def lo(b, u):
                    dve.wait_ge(S["at_hi"], b + 1)
                    dve.tensor_tensor(ATl[:, u], psA(u).rearrange("p (k n) -> p k n", k=KC), ATh[:, u].bitcast(F32),
                                      ALU.subtract).then_inc(S["at_lo"], 1)

                def body(dve, b, u, more):
                    if more:
                        quantize(b + 1, 1 - u)
                    dve.wait_ge(S["tanh_ready"], b + 1)
                    dve.scalar_tensor_tensor(T[:], T[:], 1.0, gate[:, 0:I0], ALU.add, ALU.mult).then_inc(S["u_ready"], 1)
                    if more:
                        lo(b + 1, 1 - u)
                    dve.wait_ge(S["up_psum"], b + 2)
                    dve.wait_ge(S["u_ready"], b + 1)
                    dve.scalar_tensor_tensor(H[:, b], T[:], g[:, 3:4], up[:, 0:I0], ALU.mult, ALU.mult)\
                       .then_inc(S["h_ready"], 1)
                    dve.wait_ge(S["h_ready"], b + 1)
                    dve.tensor_reduce(hb[:, b], blocks(H[:, b]), AX.X, ALU.max, apply_absolute_value=True)\
                       .then_inc(S["hb_ready"], 1)

                quantize(0, 0)
                lo(0, 0)
                rows_loop(body)(dve)
    whole_scale(nc, sem, hb, g, "h")


def ffn0_down(nc, sem, ps, ident, scratch, X, stats, mv, H, hb, g):
    MT = len(IT)
    with ExitStack() as here:
        sb = sb_in_stack(nc, here)
        W = [sb(f"Wd{s}", [P, MT, D], F32R) for s in "hl"]
        with ExitStack() as loading:
            R = sb_in_stack(nc, loading)("wdrows", [P, D // P, I0])
            fetched, wt_psum, wt_hi, wt_lo = sem("wd_fetched"), sem("wd_psum"), sem("wd_hi"), sem("wd_lo")
            with nc.Block() as block:
                @block.sync
                def _(sp):
                    sp.dma_start(R[:], scratch["down"].rearrange("(o p) m -> p o m", p=P)).then_inc(fetched, 16)

                @block.tensor
                def _(pe):
                    pe.wait_ge(fetched, 16)
                    for n, (m, w) in enumerate(IT):
                        if n >= 4:
                            pe.wait_ge(wt_lo, n - 3)
                        for o in range(D // P):
                            last = pe.transpose(ps[0:w, n % 4, o * P:(o + 1) * P], R[:, o, m:m + w], ident[:])
                        last.then_inc(wt_psum, 1)

                @block.scalar
                def _(act):
                    for n, (m, w) in enumerate(IT):
                        act.wait_ge(wt_psum, n + 1)
                        act.activation(W[0][0:w, n], ps[0:w, n % 4, :], ACT.Copy).then_inc(wt_hi, 1)

                @block.vector
                def _(dve):
                    for n, (m, w) in enumerate(IT):
                        dve.wait_ge(wt_hi, n + 1)
                        dve.tensor_tensor(W[1][0:w, n], ps[0:w, n % 4, :], W[0][0:w, n].bitcast(F32), ALU.subtract)\
                           .then_inc(wt_lo, 1)

        V, E, R, A = sb("d_V", [P, I0]), sb("d_E", [P, I0]), sb("d_R", [P, SELECT]), sb("d_A", [P, 2, I0])
        sc, inv, bm = sb("d_sc", [P, I0 // BLK]), sb("d_inv", [P, I0 // BLK]), sb("d_bm", [P, 3, SELECT // BLK])
        ATh, ATl = sb("d_ATh", [P, MT, P], F32R), sb("d_ATl", [P, MT, P], F32R)
        names = "a_ready at_psum at_hi at_lo y_psum x_added stat_done"
        S = {n: sem("d_" + n) for n in names.split()}
        turned = lambda u: ps[:, 3 * u:3 * u + 3, :].rearrange("p c (m n) -> p (c m) n", n=P)
        y = lambda u: ps[:, 6 + u, :]
        parts = [(P, slice(0, I0 // P)), (IT[-1][1], slice(I0 // P, MT))]
        with nc.Block() as block:
            @block.tensor
            def _(pe):
                def turn(b, u):
                    pe.wait_ge(S["a_ready"], b + 1)
                    pe.wait_ge(S["at_lo"], 2 * b)
                    for n, (m, w) in enumerate(IT):
                        last = pe.transpose(turned(u)[0:w, n], A[:, u, m:m + w], ident[:])
                    last.then_inc(S["at_psum"], 1)

                def body(pe, b, u, more):
                    if more:
                        turn(b + 1, 1 - u)
                    pe.wait_ge(S["at_hi"], 2 * b + 2)
                    pe.wait_ge(S["at_lo"], 2 * b + 4)
                    pe.wait_ge(S["x_added"], b + 1)
                    for n, (m, w) in enumerate(IT):
                        last = mm3(pe, y(u), ATh[0:w, n], ATl[0:w, n], W[0][0:w, n], W[1][0:w, n], n == 0, n == MT - 1)
                    last.then_inc(S["y_psum"], 1)

                pe.sem_inc(S["at_lo"], 2)
                pe.sem_inc(S["x_added"], 2)
                turn(0, 0)
                rows_loop(body)(pe)

            @block.scalar
            def _(act):
                def body(act, b, u, more):
                    act.wait_ge(S["at_psum"], b + 1)
                    need(act, S["y_psum"], b)
                    for w, m in parts:
                        act.activation(ATh[0:w, m], turned(u)[0:w, m], ACT.Copy).then_inc(S["at_hi"], 1)

                rows_loop(body)(act)

            @block.vector
            def _(dve):
                link = Chain(dve, sem("d_link"))

                def quantize(b, u):
                    link.row(b)
                    block_scales(dve, link, hb[:, b], g, sc[:], inv[:])
                    quantize_rows(dve, link, H[:, b], inv[:], sc[:], V, E, R[:], A[:, u], bm, g[:, 1:2], I0)\
                        .then_inc(S["a_ready"], 1)

                def body(dve, b, u, more):
                    dve.wait_ge(S["at_hi"], 2 * b + 2)
                    for w, m in parts:
                        dve.tensor_tensor(ATl[0:w, m], turned(u)[0:w, m], ATh[0:w, m].bitcast(F32), ALU.subtract)\
                           .then_inc(S["at_lo"], 1)
                    if more:
                        quantize(b + 1, 1 - u)
                    dve.wait_ge(S["y_psum"], b + 1)
                    dve.scalar_tensor_tensor(X[:, b], y(u), g[:, 0:1], X[:, b], ALU.mult, ALU.add).then_inc(S["x_added"], 1)
                    dve.wait_ge(S["x_added"], b + 3)
                    dve.bn_stats(stats[:, b], X[:, b]).then_inc(S["stat_done"], 1)

                quantize(0, 0)
                rows_loop(body)(dve)
                for b in range(B):
                    dve.wait_ge(S["stat_done"], b + 1)
                    dve.bn_aggr(mv[:, b], stats[:, b]).then_inc(S["stat_done"], 1)


def layer0_ffn(nc, t, sem, ps, ident, X, stats, mv, rstd, minus_half, scratch):
    layer0_quantize_weights(nc, t, sem, ps, ident, scratch)
    with ExitStack() as here:
        sb = sb_in_stack(nc, here)
        H = sb("H", [P, B, I0])
        xb, hb, g = sb("xb", [P, B, D // BLK]), sb("hb", [P, B, I0 // BLK]), sb("g", [P, 6])
        ffn0_gather_x(nc, t, sem, ps, ident, X, mv, rstd, minus_half, H, xb, g)
        with ExitStack() as weights:
            sbw = sb_in_stack(nc, weights)
            W = [[sbw(f"W{n}{s}", [P, KC, I0], F32R) for s in "hl"] for n in ("gate", "up")]
            ffn0_load_up(nc, t, sem, ps, ident, scratch, W)
            ffn0_up(nc, sem, ps, ident, W, H, hb, xb, g)
        ffn0_down(nc, sem, ps, ident, scratch, X, stats, mv, H, hb, g)

G1, J1, E1 = 8, 4, 128
W1 = J1 * E1
QK = W1 + E1
VE = E1 + 2
MULT = 0.08838834764831845
CAP = 30.0
MASKED = -1e30


def rope_tables():
    freq = (np.float32(1.0) / np.float32(10000.0) ** (np.arange(0, E1, 2, dtype=np.float32) / np.float32(E1))).astype(np.float32)
    phase = np.arange(P, dtype=np.float32)[:, None] * freq[None, :]
    c, s = np.cos(phase), np.sin(phase)
    return np.stack([np.concatenate([c, c], 1), np.concatenate([-s, s], 1)], 1).astype(np.float32)


def normalize_rows(nc, sem, ps, ident, X, mv, rstd, minus_half, XTh, XTl):
    with ExitStack() as here:
        sb = sb_in_stack(nc, here)
        xh = sb("n_xh", [P, 2, D])
        S = {n: sem("n_" + n) for n in "eps_added rstd_ready xh_ready xt_psum xt_hi xt_lo".split()}
        psA = lambda u: ps[:, u, :]
        with nc.Block() as block:
            @block.gpsimd
            def _(pool):
                pool.wait_ge(S["eps_added"], 1)
                pool.tensor_tensor(rstd[:], rstd[:], minus_half[:], ALU.pow).then_inc(S["rstd_ready"], 1)

            @block.tensor
            def _(pe):
                def body(pe, b, u, more):
                    pe.wait_ge(S["xh_ready"], b + 1)
                    for k in range(KC):
                        last = pe.transpose(psA(u)[:, k * P:(k + 1) * P], xh[:, u, k * P:(k + 1) * P], ident[:])
                    last.then_inc(S["xt_psum"], 1)

                rows_loop(body)(pe)

            @block.scalar
            def _(act):
                def body(act, b, u, more):
                    act.wait_ge(S["xt_psum"], b + 1)
                    act.activation(XTh[:, b], psA(u).rearrange("p (k n) -> p k n", k=KC), ACT.Copy).then_inc(S["xt_hi"], 1)

                rows_loop(body)(act)

            @block.vector
            def _(dve):
                dve.tensor_scalar(rstd[:], mv[:, :, 1:2], EPS, None, ALU.add).then_inc(S["eps_added"], 1)

                def unit(b, u):
                    dve.tensor_scalar(xh[:, u], X[:, b], mv[:, b, 0:1], rstd[:, b], ALU.subtract, ALU.mult)\
                       .then_inc(S["xh_ready"], 1)

                def body(dve, b, u, more):
                    if more:
                        unit(b + 1, 1 - u)
                    dve.wait_ge(S["xt_hi"], b + 1)
                    dve.tensor_tensor(XTl[:, b], psA(u).rearrange("p (k n) -> p k n", k=KC), XTh[:, b].bitcast(F32),
                                      ALU.subtract).then_inc(S["xt_lo"], 1)

                dve.wait_ge(S["rstd_ready"], 1)
                unit(0, 0)
                rows_loop(body)(dve)


def layer1_tables(nc, t, sem, ps, ident, tables, bias):
    with ExitStack() as here:
        sb = sb_in_stack(nc, here)
        rope = sb("rope", [P, 2, E1])
        m8, m, live, q_bias = sb("m8", [P, P], mybir.dt.uint8), sb("m", [P, P]), sb("live", [P, 1]), sb("q_bias", [P, P])
        loaded, turned, ready = sem("t_loaded"), sem("t_turned"), sem("t_ready")
        q_bias_steps = sem("t_q_bias_steps")
        with nc.Block() as block:
            @block.sync
            def _(sp):
                sp.dma_start(rope[:], t["rope"]).then_inc(loaded, 16)
                sp.dma_start(m8[:], t["mask"]).then_inc(loaded, 16)

            @block.vector
            def _(dve):
                link = Chain(dve, q_bias_steps)
                dve.wait_ge(loaded, 32)
                link(dve.tensor_copy(m[:], m8[:]))
                link(dve.tensor_reduce(live[:], m[:], AX.X, ALU.max))
                link(dve.tensor_scalar(q_bias[:], m[:], 1.0, live[:], ALU.subtract, ALU.mult))
                link(dve.tensor_scalar(q_bias[:], q_bias[:], -MASKED / CAP, None, ALU.mult))
                for n in range(2):
                    for h in range(J1):
                        dve.tensor_scalar(tables[:, n, h], rope[:, n], live[:], None, ALU.mult)
                    dve.tensor_copy(tables[:, n, J1], rope[:, n])
                dve.wait_ge(turned, 1)
                dve.tensor_copy(bias[:], ps[:, 0, 0:P]).then_inc(ready, 1)

            @block.tensor
            def _(pe):
                pe.wait_ge(q_bias_steps, 4)
                pe.transpose(ps[:, 0, 0:P], q_bias[:], ident[:]).then_inc(turned, 1)


def layer1_attention(nc, t, sem, ps, X, stats, mv, ident, CTh, CTl, XTh, XTl, tables, bias):
    with ExitStack() as here:
        sb = sb_in_stack(nc, here)
        qkv_in = sb("qkv_in", [P, KC, QK + E1])
        o_in = qkv_in[:].rearrange("p k n -> p (k n)")[:, 0:J1 * D].rearrange("p (j n) -> p j n", n=D)
        Wi = [[sb(f"Wi{n}{s}", [P, KC, QK + E1], F32R) for s in "hl"] for n in range(2)]
        Wo = [[sb(f"Wo1{n}{s}", [P, J1, D], F32R) for s in "hl"] for n in range(2)]
        T1, T2 = sb("T1", [P, QK]), sb("T2", [P, QK])
        QTh, QTl = sb("QTh", [P, QK], F32R), sb("QTl", [P, QK], F32R)
        V = [sb(f"V1{s}", [P, 2, VE], F32R) for s in "hl"]
        E = sb("E", [P, W1])
        Ph, Pl = sb("Ph", [P, W1], F32R), sb("Pl", [P, W1], F32R)
        rden, A = sb("rden1", [P, J1]), sb("A1", [P, J1, E1])
        AT = [sb(f"AT{s}", [P, 2, J1, P], F32R) for s in "hl"]
        names = ("w_loaded wo_loaded w_hi w_lo qkv_psum t_one t_two v_hi v_lo roped qk_psum qk_hi qk_lo s_psum tanh_ready masked "
                 "exp_ready p_hi p_lo pv_psum rden_ready a_ready at_psum at_hi at_lo y_psum x_added preset stat_done")
        S = {n: sem("s_" + n) for n in names.split()}
        qkv = ps[:, 0:2, :].rearrange("p c n -> p (c n)")
        turned = ps[:, 2:4, :].rearrange("p c n -> p (c n)")
        psS = ps[:, 4, :]
        psV = ps[:, 5:7, 0:2 * VE].rearrange("p c (j e) -> p c j e", e=VE)
        psY = ps[:, 7, :]
        slices = [(True, k) for k in range(KC)] + [(False, j) for j in range(J1)]
        plan = {1: [0], 2: [1], 3: [2], 4: [3], 5: [4, 5], 6: [6, 7]}

        def steps(eng, body):
            with eng.Fori(0, G1 // 2) as i:
                for n in range(2):
                    for b in range(B):
                        body(i * 2 + n, n, b, i * (2 * B) + (n * B + b))

        def split_slice(n, w):
            inputs, k = slices[w]
            return (qkv_in[:, k], [x[:, k] for x in Wi[n]]) if inputs else (o_in[:, k], [x[:, k] for x in Wo[n]])

        with nc.Block() as block:
            @block.sync
            def _(sp):
                def load(g, n):
                    for dst, src in ((qkv_in[:, :, 0:W1], t["Wq1"][g]), (qkv_in[:, :, W1:QK], t["Wk1"][g]),
                                     (qkv_in[:, :, QK:QK + E1], t["Wv1"][g])):
                        sp.dma_start(dst, src).then_inc(S["w_loaded"], 16)
                    sp.wait_ge(S["w_lo"], n * len(slices) + KC)
                    sp.dma_start(o_in, t["Wo1"][g]).then_inc(S["wo_loaded"], 16)
                    sp.wait_ge(S["w_lo"], (n + 1) * len(slices))

                for g in range(G1):
                    load(g, g)
                load(0, G1)

            @block.gpsimd
            def _(pool):
                def split(n, w, count):
                    src, (hi, lo) = split_slice(n, w)
                    pool.wait_ge(S["w_hi"], count)
                    pool.tensor_tensor(lo, src, hi.bitcast(F32), ALU.subtract).then_inc(S["w_lo"], 1)

                for x in Wo[1]:
                    pool.memset(x[:].bitcast(F32), 0.0).then_inc(S["preset"], 1)
                pool.wait_ge(S["w_loaded"], 48)
                for w in range(len(slices)):
                    split(0, w, w + 1)

                def body(g, n, b, s):
                    for w in plan.get(b, []):
                        split(1 - n, w, (g + 1) * len(slices) + w + 1)

                steps(pool, body)

            @block.tensor
            def _(pe):
                def project(n, b):
                    for k in range(KC):
                        mm3(pe, qkv[:, 0:W1], XTh[:, b, k], XTl[:, b, k], Wi[n][0][:, k, 0:W1], Wi[n][1][:, k, 0:W1],
                            k == 0, k == KC - 1)
                    for k in range(KC):
                        c = slice(b * P, (b + 1) * P)
                        last = mm3(pe, qkv[:, W1:QK + E1], CTh[:, k, c], CTl[:, k, c], Wi[n][0][:, k, W1:QK + E1],
                                   Wi[n][1][:, k, W1:QK + E1], k == 0, k == KC - 1)
                    last.then_inc(S["qkv_psum"], 1)

                def turn(s):
                    pe.wait_ge(S["roped"], s + 1)
                    for j in range(J1 + 1):
                        last = pe.transpose(turned[:, j * P:(j + 1) * P], T1[:, j * E1:(j + 1) * E1], ident[:])
                    last.then_inc(S["qk_psum"], 1)

                def output(n, u, heads):
                    for j in heads:
                        last = mm3(pe, psY, AT[0][:, u, j], AT[1][:, u, j], Wo[n][0][:, j], Wo[n][1][:, j],
                                   j == 0, j == J1 - 1)
                    return last

                def body(g, n, b, s):
                    u = b % 2
                    pe.wait_ge(S["qk_lo"], s + 1)
                    pe.wait_ge(S["at_lo"], s + 1)
                    mm3(pe, psS, QTh[:, W1:QK], QTl[:, W1:QK], QTh[:, 0:W1], QTl[:, 0:W1], True, True)\
                        .then_inc(S["s_psum"], 1)
                    n2, b2 = (n, b + 1) if b + 1 < B else (1 - n, 0)
                    if b2 == 0:
                        pe.wait_ge(S["w_lo"], (g + 2) * len(slices))
                    pe.wait_ge(S["v_lo"], s + 1)
                    project(n2, b2)
                    pe.wait_ge(S["p_lo"], s + 1)
                    pe.wait_ge(S["a_ready"], s + 1)
                    for j in range(J1):
                        p = slice(j * P, (j + 1) * P)
                        last = mm3(pe, psV[:, j // 2, j % 2], Ph[:, p], Pl[:, p], V[0][:, u], V[1][:, u], True, True)
                    last.then_inc(S["pv_psum"], 1)
                    n0 = n if b else 1 - n
                    pe.wait_ge(S["x_added"], s + 1)
                    output(n0, 1 - u, (0, 1))
                    turn(s + 1)
                    pe.wait_ge(S["a_ready"], s + 2)
                    for j in range(J1):
                        last = pe.transpose(psS[:, j * P:(j + 1) * P], A[:, j], ident[:])
                    last.then_inc(S["at_psum"], 1)
                    output(n0, 1 - u, (2, 3)).then_inc(S["y_psum"], 1)

                pe.wait_ge(S["preset"], 8)
                pe.wait_ge(S["w_lo"], len(slices))
                project(0, 0)
                turn(0)
                steps(pe, body)
                pe.wait_ge(S["at_lo"], G1 * B + 1)
                pe.wait_ge(S["x_added"], G1 * B + 1)
                output(1, 1, range(J1)).then_inc(S["y_psum"], 1)

            @block.scalar
            def _(act):
                def split(n, w):
                    src, (hi, lo) = split_slice(n, w)
                    act.activation(hi, src, ACT.Copy).then_inc(S["w_hi"], 1)

                def inputs(s, u):
                    act.wait_ge(S["qkv_psum"], s + 1)
                    act.activation(V[0][:, u, 0:E1], qkv[:, QK:QK + E1], ACT.Copy).then_inc(S["v_hi"], 1)
                    act.wait_ge(S["qk_psum"], s + 1)
                    act.activation(QTh[:], turned[:, 0:QK], ACT.Copy).then_inc(S["qk_hi"], 1)

                act.wait_ge(S["w_loaded"], 48)
                for w in range(len(slices)):
                    if w == KC:
                        act.wait_ge(S["wo_loaded"], 16)
                    split(0, w)
                act.wait_ge(S["preset"], 6)
                inputs(0, 0)

                def body(g, n, b, s):
                    u = b % 2
                    act.wait_ge(S["s_psum"], s + 1)
                    act.activation(E[:], psS, ACT.Tanh, scale=MULT / CAP).then_inc(S["tanh_ready"], 1)
                    if b in plan:
                        if b == 1:
                            act.wait_ge(S["w_loaded"], (g + 2) * 48)
                        if b == 5:
                            act.wait_ge(S["wo_loaded"], (g + 2) * 16)
                        for w in plan[b]:
                            split(1 - n, w)
                    act.wait_ge(S["masked"], s + 1)
                    act.activation(E[:], E[:], ACT.Exp, scale=CAP).then_inc(S["exp_ready"], 1)
                    act.wait_ge(S["exp_ready"], s + 1)
                    act.activation(Ph[:], E[:], ACT.Copy).then_inc(S["p_hi"], 1)
                    inputs(s + 1, 1 - u)
                    act.wait_ge(S["at_psum"], s + 1)
                    act.activation(AT[0][:, u], psS.rearrange("p (j n) -> p j n", j=J1), ACT.Copy).then_inc(S["at_hi"], 1)

                steps(act, body)

            @block.vector
            def _(dve):
                def rope(s, u):
                    src = qkv[:, 0:QK].rearrange("p (h a e) -> p h a e", h=J1 + 1, a=2)
                    half = lambda x: x.rearrange("p h (a e) -> p h a e", a=2)
                    dve.wait_ge(S["v_hi"], s + 1)
                    dve.tensor_tensor(T1[:].rearrange("p (h a e) -> p h a e", h=J1 + 1, a=2), src, half(tables[:, 0]),
                                      ALU.mult).then_inc(S["t_one"], 1)
                    dve.tensor_tensor(T2[:].rearrange("p (h a e) -> p h a e", h=J1 + 1, a=2), src[:, :, ::-1],
                                      half(tables[:, 1]), ALU.mult).then_inc(S["t_two"], 1)
                    dve.tensor_tensor(V[1][:, u, 0:E1], qkv[:, QK:QK + E1], V[0][:, u, 0:E1].bitcast(F32), ALU.subtract)\
                       .then_inc(S["v_lo"], 1)
                    dve.wait_ge(S["t_one"], s + 1)
                    dve.wait_ge(S["t_two"], s + 1)
                    dve.tensor_tensor(T1[:], T1[:], T2[:], ALU.add).then_inc(S["roped"], 1)

                def low(s):
                    dve.wait_ge(S["qk_hi"], s + 1)
                    dve.tensor_tensor(QTl[:], turned[:, 0:QK], QTh[:].bitcast(F32), ALU.subtract).then_inc(S["qk_lo"], 1)

                def add(s, b):
                    dve.wait_ge(S["y_psum"], s)
                    dve.tensor_tensor(X[:, b], psY, X[:, b], ALU.add).then_inc(S["x_added"], 1)

                for u in range(2):
                    dve.memset(V[0][:, u, E1:VE].bitcast(F32), 1.0).then_inc(S["preset"], 1)
                    dve.memset(V[1][:, u, E1:VE].bitcast(F32), 0.0).then_inc(S["preset"], 1)
                for x in AT:
                    dve.memset(x[:, 1].bitcast(F32), 0.0).then_inc(S["preset"], 1)
                for name in ("at_lo", "a_ready", "x_added"):
                    dve.sem_inc(S[name], 1)
                rope(0, 0)
                low(0)

                def body(g, n, b, s):
                    u = b % 2
                    dve.wait_ge(S["tanh_ready"], s + 1)
                    dve.tensor_tensor(E[:].rearrange("p (j q) -> p j q", j=J1), E[:].rearrange("p (j q) -> p j q", j=J1),
                                      bias[:].unsqueeze(1).broadcast_to([P, J1, P]), ALU.add).then_inc(S["masked"], 1)
                    dve.wait_ge(S["p_hi"], s + 1)
                    dve.tensor_tensor(Pl[:], E[:], Ph[:].bitcast(F32), ALU.subtract).then_inc(S["p_lo"], 1)
                    rope(s + 1, 1 - u)
                    dve.wait_ge(S["pv_psum"], s + 1)
                    r = rden[:].rearrange("p (c j) -> p c j", c=2)
                    dve.reciprocal(r, psV[:, :, :, E1]).then_inc(S["rden_ready"], 1)
                    dve.wait_ge(S["rden_ready"], s + 1)
                    dve.tensor_tensor(A[:].rearrange("p (c j) e -> p c j e", c=2), psV[:, :, :, 0:E1], bcast(r, E1),
                                      ALU.mult).then_inc(S["a_ready"], 1)
                    low(s + 1)
                    dve.wait_ge(S["at_hi"], s + 1)
                    dve.tensor_tensor(AT[1][:, u], psS.rearrange("p (j n) -> p j n", j=J1), AT[0][:, u].bitcast(F32),
                                      ALU.subtract).then_inc(S["at_lo"], 1)
                    add(s + 1, (b - 1) % B)

                steps(dve, body)
                add(G1 * B + 1, B - 1)
                dve.wait_ge(S["x_added"], G1 * B + 2)
                for b in range(B):
                    dve.bn_stats(stats[:, b], X[:, b]).then_inc(S["stat_done"], 1)
                for b in range(B):
                    dve.wait_ge(S["stat_done"], b + 1)
                    dve.bn_aggr(mv[:, b], stats[:, b]).then_inc(S["stat_done"], 1)


def layer1_ffn(nc, t, sem, ps, ident, X, mv, rstd, minus_half):
    IB = 32
    OC = D // P
    with ExitStack() as here:
        sb = sb_in_stack(nc, here)
        WT = [sb(f"WT{s}", [P, KC, D], F32R) for s in "hl"]
        add_bias = sb("add_bias", [P, D])
        bias_loaded = sem("f_bias_loaded")
        with ExitStack() as loading:
            own = sb_in_stack(nc, loading)
            packed = own("packed", [P, OC, D // 2], I32)
            q = own("q", [P, OC, D // 2, 2], I32)
            W = own("W1f", [P, OC, D])
            s16, v8 = own("s16", [P, OC, D // IB], mybir.dt.float16), own("v8", [P, OC, D // IB], mybir.dt.uint8)
            sc, half = own("sc1", [P, OC, D // IB]), own("half1", [P, OC, D // IB])
            loaded, turned, w_hi, w_lo, w_done = sem("f_loaded"), sem("f_turned"), sem("f_w_hi"), sem("f_w_lo"), sem("f_w_done")
            with nc.Block() as block:
                @block.sync
                def _(sp):
                    sp.dma_start(packed[:], t["packed"]).then_inc(loaded, 16)
                    sp.dma_start(s16[:], t["scale"]).then_inc(loaded, 16)
                    sp.dma_start(v8[:], t["var_mask"]).then_inc(loaded, 16)
                    sp.dma_start(add_bias[:], t["L1_ffn_bias"].partition_broadcast(P)).then_inc(bias_loaded, 16)

                @block.vector
                def _(dve):
                    link = Chain(dve, w_done)
                    dve.wait_ge(loaded, 48)
                    link(dve.tensor_scalar(q[:, :, :, 0], packed[:], 15, None, ALU.bitwise_and))
                    link(dve.tensor_scalar(q[:, :, :, 1], packed[:], 4, 15, ALU.logical_shift_right, ALU.bitwise_and))
                    link(dve.tensor_scalar(half[:], v8[:], 0.5, 0.5, ALU.mult, ALU.add))
                    link(dve.tensor_tensor(sc[:], half[:], s16[:], ALU.mult))
                    for o in range(OC):
                        link(dve.scalar_tensor_tensor(W[:, o].rearrange("p (b e) -> p b e", e=IB),
                                                      q[:, o].rearrange("p (b e) c -> p b (e c)", b=D // IB), -8.0,
                                                      bcast(sc[:, o], IB), ALU.add, ALU.mult))
                    for k in range(KC):
                        dve.wait_ge(w_hi, k + 1)
                        dve.tensor_tensor(WT[1][:, k], ps[:, k, :], WT[0][:, k].bitcast(F32), ALU.subtract).then_inc(w_lo, 1)

                @block.tensor
                def _(pe):
                    pe.wait_ge(w_done, 4 + OC)
                    for k in range(KC):
                        for o in range(OC):
                            last = pe.transpose(ps[:, k, o * P:(o + 1) * P], W[:, o, k * P:(k + 1) * P], ident[:])
                        last.then_inc(turned, 1)

                @block.scalar
                def _(act):
                    for k in range(KC):
                        act.wait_ge(turned, k + 1)
                        act.activation(WT[0][:, k], ps[:, k, :], ACT.Copy).then_inc(w_hi, 1)

        xh = sb("f_xh", [P, 2, D])
        XTh, XTl = sb("f_XTh", [P, 2, KC, P], F32R), sb("f_XTl", [P, 2, KC, P], F32R)
        names = "eps_added rstd_ready xh_ready xt_psum xt_hi xt_lo y_psum biased out_ready stored"
        S = {n: sem("f_" + n) for n in names.split()}
        psA = lambda u: ps[:, u, :]
        psY = lambda u: ps[:, 2 + u, :]
        out = t["out"].rearrange("b p d -> p b d")
        with nc.Block() as block:
            @block.gpsimd
            def _(pool):
                pool.wait_ge(S["eps_added"], 1)
                pool.tensor_tensor(rstd[:], rstd[:], minus_half[:], ALU.pow).then_inc(S["rstd_ready"], 1)
                pool.wait_ge(bias_loaded, 16)

                def body(pool, b, u, more):
                    pool.wait_ge(S["xh_ready"], b + 1)
                    pool.tensor_tensor(X[:, b], X[:, b], add_bias[:], ALU.add).then_inc(S["biased"], 1)

                rows_loop(body)(pool)

            @block.tensor
            def _(pe):
                def turn(b, u):
                    pe.wait_ge(S["xh_ready"], b + 1)
                    pe.wait_ge(S["xt_lo"], b)
                    for k in range(KC):
                        last = pe.transpose(psA(u)[:, k * P:(k + 1) * P], xh[:, u, k * P:(k + 1) * P], ident[:])
                    last.then_inc(S["xt_psum"], 1)

                def body(pe, b, u, more):
                    if more:
                        turn(b + 1, 1 - u)
                    pe.wait_ge(S["xt_hi"], b + 1)
                    pe.wait_ge(S["xt_lo"], b + 2)
                    pe.wait_ge(S["out_ready"], b + 1)
                    for k in range(KC):
                        last = mm3(pe, psY(u), XTh[:, u, k], XTl[:, u, k], WT[0][:, k], WT[1][:, k], k == 0, k == KC - 1)
                    last.then_inc(S["y_psum"], 1)

                pe.sem_inc(S["xt_lo"], 1)
                pe.sem_inc(S["out_ready"], 2)
                turn(0, 0)
                rows_loop(body)(pe)

            @block.scalar
            def _(act):
                def body(act, b, u, more):
                    act.wait_ge(S["xt_psum"], b + 1)
                    act.wait_ge(S["out_ready"], b + 1)
                    act.activation(XTh[:, u], psA(u).rearrange("p (k n) -> p k n", k=KC), ACT.Copy).then_inc(S["xt_hi"], 1)

                rows_loop(body)(act)

            @block.vector
            def _(dve):
                dve.tensor_scalar(rstd[:], mv[:, :, 1:2], EPS, None, ALU.add).then_inc(S["eps_added"], 1)

                def split(b, u):
                    dve.tensor_scalar(xh[:, u], X[:, b], mv[:, b, 0:1], rstd[:, b], ALU.subtract, ALU.mult)\
                       .then_inc(S["xh_ready"], 1)
                    dve.wait_ge(S["xt_hi"], b + 1)
                    dve.tensor_tensor(XTl[:, u], psA(u).rearrange("p (k n) -> p k n", k=KC), XTh[:, u].bitcast(F32),
                                      ALU.subtract).then_inc(S["xt_lo"], 1)

                def body(dve, b, u, more):
                    if more:
                        split(b + 1, 1 - u)
                    dve.wait_ge(S["y_psum"], b + 1)
                    dve.wait_ge(S["biased"], b + 1)
                    dve.tensor_tensor(X[:, b], psY(u), X[:, b], ALU.add).then_inc(S["out_ready"], 1)

                dve.wait_ge(S["rstd_ready"], 1)
                split(0, 0)
                rows_loop(body)(dve)

            @block.sync
            def _(sp):
                def body(sp, b, u, more):
                    sp.wait_ge(S["out_ready"], b + 3)
                    sp.dma_start(out[:, b], X[:, b]).then_inc(S["stored"], 16)

                rows_loop(body)(sp)
                sp.wait_ge(S["stored"], 16 * B)


_INS = ["x", "ctx_4096", "L0_xattn_Wq", "L0_xattn_Wk", "L0_xattn_Wv", "L0_xattn_Wo",
        "L0_ffn_w_gate", "L0_ffn_w_up", "L0_ffn_w_down", "L0_ffn_ri_in", "L1_ffn_bias"]
STOP = 4


def kernel(**inputs):
    import concourse.bacc as bacc
    from concourse.bass_utils import run_bass_kernel_spmd as run

    nc = bacc.Bacc("TRN2", target_bir_lowering=False, num_devices=1)
    arrays, t = {}, {}
    ri_in, ri_mid = np.asarray(inputs["L0_ffn_ri_in"]), np.asarray(inputs["L0_ffn_ri_mid"])
    full = I0 // P * P
    inputs = {**inputs, "ri_in_columns": ri_in.reshape(KC, P).T, "ri_mid_columns": ri_mid[:full].reshape(-1, P).T,
              "ri_mid_rest": ri_mid[full:].reshape(-1, 1)}
    get = lambda name: np.asarray(inputs[name])
    inputs["Wq1"] = get("L1_xattn_Wq").reshape(KC, P, G1, W1).transpose(2, 1, 0, 3)
    inputs["Wk1"] = get("L1_xattn_Wk").reshape(KC, P, G1, E1).transpose(2, 1, 0, 3)
    inputs["Wv1"] = get("L1_xattn_Wv").reshape(KC, P, G1, E1).transpose(2, 1, 0, 3)
    inputs["Wo1"] = get("L1_xattn_Wo").reshape(G1, J1, P, D).transpose(0, 2, 1, 3)
    inputs["rope"] = rope_tables()
    inputs["mask"] = get("mask_1x1xSxS2_bk0").reshape(P, P)
    inputs["packed"] = get("L1_ffn_weight_packed").reshape(D // P, P, D // 2).transpose(1, 0, 2)
    inputs["scale"] = get("L1_ffn_weight_scale").reshape(D // P, P, -1).transpose(1, 0, 2)
    inputs["var_mask"] = get("L1_ffn_weight_var_mask").reshape(D // P, P, -1).transpose(1, 0, 2)
    made = ["ri_in_columns", "ri_mid_columns", "ri_mid_rest", "Wq1", "Wk1", "Wv1", "Wo1", "rope", "mask", "packed",
            "scale", "var_mask"]
    for name in _INS + made:
        a = np.asarray(inputs[name])
        if name == "L0_xattn_Wq":
            a = a.reshape(D, PAIRS, 2, J0, E0).transpose(0, 1, 3, 2, 4).reshape(D, D)
        if name.startswith("L0_ffn_w"):
            a = a.T
        a = np.ascontiguousarray(a)
        arrays["in_" + name] = a
        t[name] = nc.dram_tensor("in_" + name, a.shape, mybir.dt.from_np(a.dtype), kind="ExternalInput").ap()
    t["out"] = nc.dram_tensor("out_x", (B, P, D), F32, kind="ExternalOutput").ap()
    program(nc, t, STOP)
    return run(nc, [arrays], core_ids=[0]).results[0]["out_x"]
```

```python
from contextlib import ExitStack

import numpy as np

import concourse.bass as bass
from concourse import mybir

F32 = mybir.dt.float32
F32R = mybir.dt.float32r
I32 = mybir.dt.int32
ALU = mybir.AluOpType
ACT = mybir.ActivationFunctionType
AX = mybir.AxisListType

P = 128
B = 8
D = 512
KC = D // P
EPS = 1e-5
H0, G0, E0 = 32, 8, 16
J0 = H0 // G0
PAIRS = G0 // 2
STACK = 4 * E0
VC = E0 + 1


def mm3(pe, out, ah, al, bh, bl, start, stop):
    pe.matmul(out, ah, bh, start=start, stop=False)
    pe.matmul(out, ah, bl, start=False, stop=False)
    return pe.matmul(out, al, bh, start=False, stop=stop)


def program(nc, t, stop_after):
    with ExitStack() as whole:
        held = []

        def sem(name):
            held.append(nc.alloc_semaphore(name))
            return held[-1]

        def release():
            nc.clear_and_free_semaphores(held)
            held.clear()
            nc.all_engine_barrier()

        def sb_in(stack):
            return lambda name, shape, dt=F32: stack.enter_context(nc.sbuf_tensor(name, shape, dt))

        keep = sb_in(whole)
        scratch = {n: nc.dram_tensor("w_" + n, s, F32, kind="Internal").ap()
                   for n, s in (("down", (I0, D)),)}
        ps = whole.enter_context(nc.psum_tensor("ps", [P, 8, 512], F32))
        ident = keep("ident", [P, P])
        X = keep("X", [P, B, D])
        stats = keep("stats", [P, B, 6])
        mv = keep("mv", [P, B, 2])
        rstd = keep("rstd", [P, B, 1])
        minus_half = keep("minus_half", [P, B, 1])
        CTh = keep("CTh", [P, KC, B * P], F32R)
        CTl = keep("CTl", [P, KC, B * P], F32R)

        with ExitStack() as layer0:
            kw = layer0_setup(nc, t, sem, sb_in(layer0), ps, ident, X, stats, mv, rstd, minus_half, CTh, CTl)
            layer0_attention(nc, sem, ps, ident, X, stats, mv, rstd, **kw)
        release()
        if stop_after >= 2:
            layer0_ffn(nc, t, sem, ps, ident, X, stats, mv, rstd, minus_half, scratch)
            release()
        if stop_after >= 3:
            with ExitStack() as attention:
                sb = sb_in(attention)
                tables, bias = sb("tables", [P, 2, J1 + 1, E1]), sb("bias", [P, P])
                XTh, XTl = sb("XTh", [P, B, KC, P], F32R), sb("XTl", [P, B, KC, P], F32R)
                layer1_tables(nc, t, sem, ps, ident, tables, bias)
                normalize_rows(nc, sem, ps, ident, X, mv, rstd, minus_half, XTh, XTl)
                layer1_attention(nc, t, sem, ps, X, stats, mv, ident, CTh, CTl, XTh, XTl, tables, bias)
        if stop_after >= 4:
            return layer1_ffn(nc, t, sem, ps, ident, X, mv, rstd, minus_half)
        if stop_after:
            return finish(nc, t, sem, X)


def finish(nc, t, sem, X):
    stored = sem("stored")
    with nc.Block() as block:
        @block.sync
        def _(sp):
            sp.dma_start(t["out"].rearrange("b p d -> p b d"), X[:]).then_inc(stored, 16)
            sp.wait_ge(stored, 16)


def layer0_setup(nc, t, sem, sb, ps, ident, X, stats, mv, rstd, minus_half, CTh, CTl):
    KT = sb("KT", [P, B, PAIRS, P], F32R)
    V = sb("V", [P, B, G0, VC])
    Wq = [sb(f"Wq{s}", [P, KC, D], F32R) for s in "hl"]
    Wo = [sb(f"Wo{s}", [P, KC, D], F32R) for s in "hl"]
    with ExitStack() as here:
        own = sb_in_stack(nc, here)
        ctx_in = own("ctx_in", [P, B, D])
        w_in = own("w_in", [P, 2, KC, D])
        wkv_in = own("wkv_in", [P, KC, 2 * P])
        Wkv = [own(f"Wkv{s}", [P, KC, 2 * P], F32R) for s in "hl"]
        KS = own("KS", [P, 2, G0, STACK], F32R)
        ctx_loaded = [sem(f"ctx_loaded{b}") for b in range(B)]
        x_loaded, wkv_loaded, w_loaded = sem("x_loaded"), sem("wkv_loaded"), sem("w_loaded")
        ident_zero, ident_ready, half_ready = sem("ident_zero"), sem("ident_ready"), sem("half_ready")
        wkv_hi, wkv_lo, w_hi, w_lo = sem("wkv_hi"), sem("wkv_lo"), sem("w_hi"), sem("w_lo")
        ct_psum, ct_hi, ct_lo = sem("ct_psum"), sem("ct_hi"), sem("ct_lo")
        kv_psum, kv_hi, kv_lo, ks_full = sem("kv_psum"), sem("kv_hi"), sem("kv_lo"), sem("ks_full")
        v_ready, v_ones = sem("v_ready"), sem("v_ones")
        kt_psum, kt_ready = sem("kt_psum"), sem("kt_ready")
        stat_ready, mv_ready, rstd_ready = sem("stat_ready"), sem("mv_ready"), sem("rstd_ready")

        tr = lambda b: ps[:, b % 2, :]
        kv = lambda b: ps[:, 2 + b % 2, 0:2 * P]
        kt = lambda b: ps[:, 4 + b % 2, :]

        with nc.Block() as block:
            @block.sync
            def _(sp):
                sp.dma_start(ctx_in[:, 0], t["ctx_4096"][0]).then_inc(ctx_loaded[0], 16)
                sp.dma_start(wkv_in[:, :, 0:P], t["L0_xattn_Wk"].rearrange("(k p) n -> p k n", p=P)).then_inc(wkv_loaded, 16)
                sp.dma_start(wkv_in[:, :, P:2 * P], t["L0_xattn_Wv"].rearrange("(k p) n -> p k n", p=P)).then_inc(wkv_loaded, 16)
                for b in range(1, B):
                    sp.dma_start(ctx_in[:, b], t["ctx_4096"][b]).then_inc(ctx_loaded[b], 16)
                sp.dma_start(X[:], t["x"].rearrange("b p d -> p b d")).then_inc(x_loaded, 16)
                sp.dma_start(w_in[:, 0], t["L0_xattn_Wq"].rearrange("(k p) n -> p k n", p=P)).then_inc(w_loaded, 16)
                sp.dma_start(w_in[:, 1], t["L0_xattn_Wo"].rearrange("(k p) n -> p k n", p=P)).then_inc(w_loaded, 16)

            @block.gpsimd
            def _(pool):
                pool.memset(ident[:], 0.0).then_inc(ident_zero, 1)
                pool.wait_ge(ident_zero, 1)
                pool.affine_select(out=ident[:], in_=ident[:], compare_op=ALU.not_equal, fill=1.0, base=0,
                                   pattern=[[-1, P]], channel_multiplier=1).then_inc(ident_ready, 1)
                pool.memset(minus_half[:], -0.5).then_inc(half_ready, 1)
                pool.memset(V[:, :, :, E0:VC], 1.0).then_inc(v_ones, 1)
                pool.wait_ge(wkv_hi, 1)
                pool.tensor_tensor(Wkv[1][:], wkv_in[:], Wkv[0][:].bitcast(F32), ALU.subtract).then_inc(wkv_lo, 1)
                for b in range(B):
                    pool.wait_ge(kv_hi, b + 1)
                    pool.wait_ge(kv_lo, b + 1)
                    v = KS[:, b % 2].bitcast(F32).rearrange("p g (a c e) -> p g a c e", a=2, c=2)
                    o = KS[:, b % 2].rearrange("p g (a c e) -> p g a c e", a=2, c=2)
                    pool.tensor_copy(o[:, :, :, 1], v[:, :, :, 0]).then_inc(ks_full, 1)
                pool.wait_ge(w_hi, 2)
                pool.tensor_tensor(Wq[1][:], w_in[:, 0], Wq[0][:].bitcast(F32), ALU.subtract).then_inc(w_lo, 1)
                pool.tensor_tensor(Wo[1][:], w_in[:, 1], Wo[0][:].bitcast(F32), ALU.subtract).then_inc(w_lo, 1)
                pool.wait_ge(mv_ready, B)
                pool.wait_ge(half_ready, 1)
                pool.tensor_tensor(rstd[:], rstd[:], minus_half[:], ALU.pow).then_inc(rstd_ready, 1)

            @block.scalar
            def _(act):
                act.wait_ge(wkv_loaded, 32)
                act.activation(Wkv[0][:], wkv_in[:], ACT.Copy).then_inc(wkv_hi, 1)

                def keys(b):
                    act.wait_ge(kv_psum, b + 1)
                    if b >= 2:
                        act.wait_ge(kt_psum, b - 1)
                    act.activation(KS[:, b % 2, :, 0:E0], kv(b)[:, 0:P].rearrange("p (g e) -> p g e", g=G0),
                                   ACT.Copy).then_inc(kv_hi, 1)
                    act.activation(V[:, b, :, 0:E0], kv(b)[:, P:2 * P].rearrange("p (g e) -> p g e", g=G0),
                                   ACT.Copy).then_inc(v_ready, 1)

                def keys_out(b):
                    act.wait_ge(kt_psum, b + 1)
                    act.activation(KT[:, b], kt(b), ACT.Copy).then_inc(kt_ready, 1)

                for b in range(B + 2):
                    if b < B:
                        act.wait_ge(ct_psum, b + 1)
                        act.activation(CTh[:, :, b * P:(b + 1) * P], tr(b).rearrange("p (k n) -> p k n", k=KC),
                                       ACT.Copy).then_inc(ct_hi, 1)
                    if 1 <= b <= B:
                        keys(b - 1)
                    if b >= 2:
                        keys_out(b - 2)
                act.wait_ge(w_loaded, 32)
                act.activation(Wq[0][:], w_in[:, 0], ACT.Copy).then_inc(w_hi, 1)
                act.activation(Wo[0][:], w_in[:, 1], ACT.Copy).then_inc(w_hi, 1)

            @block.vector
            def _(dve):
                def keys_lo(b):
                    dve.wait_ge(v_ready, b + 1)
                    if b >= 2:
                        dve.wait_ge(kt_psum, b - 1)
                    dve.tensor_tensor(KS[:, b % 2, :, 2 * E0:3 * E0], kv(b)[:, 0:P].rearrange("p (g e) -> p g e", g=G0),
                                      KS[:, b % 2, :, 0:E0].bitcast(F32), ALU.subtract).then_inc(kv_lo, 1)

                for b in range(B + 1):
                    if b < B:
                        dve.wait_ge(ct_hi, b + 1)
                        dve.tensor_tensor(CTl[:, :, b * P:(b + 1) * P], tr(b).rearrange("p (k n) -> p k n", k=KC),
                                          CTh[:, :, b * P:(b + 1) * P].bitcast(F32), ALU.subtract).then_inc(ct_lo, 1)
                    if b >= 1:
                        keys_lo(b - 1)
                dve.wait_ge(x_loaded, 16)
                for b in range(B):
                    dve.bn_stats(stats[:, b], X[:, b]).then_inc(stat_ready, 1)
                for b in range(B):
                    dve.wait_ge(stat_ready, b + 1)
                    dve.bn_aggr(mv[:, b], stats[:, b]).then_inc(stat_ready, 1)
                dve.wait_ge(stat_ready, 2 * B)
                dve.tensor_scalar(rstd[:], mv[:, :, 1:2], EPS, None, ALU.add).then_inc(mv_ready, B)

            @block.tensor
            def _(pe):
                def project(b):
                    pe.wait_ge(ct_hi, b + 1)
                    pe.wait_ge(ct_lo, b + 1)
                    if b >= 2:
                        pe.wait_ge(kv_lo, b - 1)
                        pe.wait_ge(v_ready, b - 1)
                    for k in range(KC):
                        last = mm3(pe, kv(b), CTh[:, k, b * P:(b + 1) * P], CTl[:, k, b * P:(b + 1) * P],
                                   Wkv[0][:, k], Wkv[1][:, k], k == 0, k == KC - 1)
                    last.then_inc(kv_psum, 1)

                def turn_keys(b):
                    pe.wait_ge(ks_full, b + 1)
                    if b >= 2:
                        pe.wait_ge(kt_ready, b - 1)
                    for pr in range(PAIRS):
                        last = pe.transpose(kt(b)[:, pr * P:(pr + 1) * P],
                                            KS[:, b % 2, 2 * pr:2 * pr + 2].bitcast(F32).rearrange("p g c -> p (g c)"),
                                            ident[:])
                    last.then_inc(kt_psum, 1)

                pe.wait_ge(ident_ready, 1)
                for b in range(B + 2):
                    if b < B:
                        pe.wait_ge(ctx_loaded[b], 16)
                        if b >= 2:
                            pe.wait_ge(ct_lo, b - 1)
                        for k in range(KC):
                            last = pe.transpose(tr(b)[:, k * P:(k + 1) * P], ctx_in[:, b, k * P:(k + 1) * P], ident[:])
                        last.then_inc(ct_psum, 1)
                    if b == 0:
                        pe.wait_ge(wkv_lo, 1)
                    if 1 <= b <= B:
                        project(b - 1)
                    if b >= 2:
                        turn_keys(b - 2)
    return dict(KT=KT, V=V, Wq=Wq, Wo=Wo, sb=sb)


def sb_in_stack(nc, stack):
    return lambda name, shape, dt=F32: stack.enter_context(nc.sbuf_tensor(name, shape, dt))


def layer0_attention(nc, sem, ps, ident, X, stats, mv, rstd, KT, V, Wq, Wo, sb):
    xh = sb("xh", [P, D])
    XTh, XTl = sb("XTh0", [P, KC, P], F32R), sb("XTl0", [P, KC, P], F32R)
    QS = sb("QS", [P, H0, STACK], F32R)
    QT = sb("QT", [P, 2, PAIRS, J0 * P], F32R)
    KTb = sb("KTb", [P, 2, PAIRS, P], F32R)
    Vb = sb("Vb", [P, 2, G0, VC])
    mx = sb("mx", [P, 2, J0])
    PR = sb("PR", [P, 4, J0 * P])
    PT = sb("PT", [P, 2, J0 * P])
    rden = sb("rden", [P, H0 // 2])
    O = sb("O", [P, 2, D])
    OTh, OTl = sb("OTh", [P, KC, P], F32R), sb("OTl", [P, KC, P], F32R)
    zero, zero_ready = sb("zero", [P, 1]), sem("a_zero_ready")

    xh_ready, xt_psum, xt_hi, xt_lo = sem("a_xh_ready"), sem("a_xt_psum"), sem("a_xt_hi"), sem("a_xt_lo")
    q_psum, qs_hi, qs_lo, qs_full = sem("a_q_psum"), sem("a_qs_hi"), sem("a_qs_lo"), sem("a_qs_full")
    qt_psum, qt_ready, kv_staged = sem("a_qt_psum"), sem("a_qt_ready"), sem("a_kv_staged")
    s_psum, mx_ready, s_shifted = sem("a_s_psum"), sem("a_mx_ready"), sem("a_s_shifted")
    pt_psum, pt_ready, pv_done = sem("a_pt_psum"), sem("a_pt_ready"), sem("a_pv_done")
    rden_ready, o_ready = sem("a_rden_ready"), sem("a_o_ready")
    ot_psum, ot_hi, ot_lo = sem("a_ot_psum"), sem("a_ot_hi"), sem("a_ot_lo")
    y_psum, x_added, stat_done = sem("a_y_psum"), sem("a_x_added"), sem("a_stat_done")

    psA = ps[:, 0, :]
    psA3 = psA.rearrange("p (k n) -> p k n", k=KC)
    psB = ps[:, 1, :]
    psB3 = psB.rearrange("p (h e) -> p h e", h=H0)
    psS = lambda n: ps[:, 2 + n % 2, :]
    psT = lambda n: ps[:, 4 + n % 2, :]
    psO = lambda half: ps[:, 6 + half, 0:H0 // 2 * VC].rearrange("p (h e) -> p h e", e=VC)

    def behind(b, u, g, by):
        return (b, u, g - by, b * G0 + g - by) if g >= by else (b - 1, 1 - u, g - by + G0, b * G0 + g - by)

    def rows(body):
        def run(eng):
            body(eng, 0, 0, False, True, True)
            with eng.Fori(0, B // 2 - 1) as i:
                for u in (1, 0):
                    body(eng, i * 2 + (2 - u), u, True, True, True)
            body(eng, B - 1, 1, True, True, False)
            body(eng, B, 0, True, False, False)
        return run

    with nc.Block() as block:
        @block.tensor
        def _(pe):
            def turn_x(b):
                pe.wait_ge(xh_ready, b + 1)
                need(pe, qt_ready, b * PAIRS)
                for k in range(KC):
                    last = pe.transpose(psA[:, k * P:(k + 1) * P], xh[:, k * P:(k + 1) * P], ident[:])
                last.then_inc(xt_psum, 1)

            def project_q(b, ks):
                if ks[0] == 0:
                    pe.wait_ge(xt_hi, b + 1)
                    pe.wait_ge(xt_lo, b + 1)
                    if not isinstance(b, int) or b >= 3:
                        pe.wait_ge(x_added, b - 2)
                for k in ks:
                    last = mm3(pe, psB, XTh[:, k], XTl[:, k], Wq[0][:, k], Wq[1][:, k], k == 0, k == KC - 1)
                if k == KC - 1:
                    last.then_inc(q_psum, 1)

            def turn_q(b, pr):
                pe.wait_ge(qs_full, b + 1)
                need(pe, qt_ready, b * PAIRS + pr)
                for j in range(J0):
                    src = QS[:, 2 * (pr * J0 + j):2 * (pr * J0 + j + 1)].bitcast(F32).rearrange("p h c -> p (h c)")
                    last = pe.transpose(psA[:, j * P:(j + 1) * P], src, ident[:])
                last.then_inc(qt_psum, 1)

            def scores(b, u, g):
                n = b * G0 + g
                pe.wait_ge(qt_ready, b * PAIRS + g // 2 + 1)
                if g == 0:
                    pe.wait_ge(kv_staged, 2 * (b + 1))
                need(pe, s_shifted, n - 1)
                r = slice((g % 2) * STACK, (g % 2 + 1) * STACK)
                for j in range(J0):
                    last = pe.matmul(psS(g)[:, j * P:(j + 1) * P], QT[r, u, g // 2, j * P:(j + 1) * P],
                                     KTb[r, u, g // 2], start=True, stop=True)
                last.then_inc(s_psum, 1)

            def turn(b, u, g, n):
                pe.wait_ge(s_shifted, n + 1)
                need(pe, pt_ready, n - 1)
                for j in range(J0):
                    last = pe.transpose(psT(g)[:, j * P:(j + 1) * P], PR[:, g % 4, j * P:(j + 1) * P], ident[:])
                last.then_inc(pt_psum, 1)

            def weigh(b, u, g, n):
                pe.wait_ge(pt_ready, n + 1)
                if g % 4 == 0:
                    need(pe, o_ready, 2 * b + g // 4 - 1)
                for j in range(J0):
                    last = pe.matmul(psO(g // 4)[:, g % 4 * J0 + j], PT[:, g % 2, j * P:(j + 1) * P],
                                     Vb[:, u, g], start=True, stop=True)
                last.then_inc(pv_done, 1)

            def turn_o(b, u, more):
                pe.wait_ge(o_ready, 2 * b + 2)
                if not more:
                    pe.wait_ge(qt_ready, B * PAIRS)
                for k in range(KC):
                    last = pe.transpose(psA[:, k * P:(k + 1) * P], O[:, u, k * P:(k + 1) * P], ident[:])
                last.then_inc(ot_psum, 1)

            def project_o(b, ks):
                pe.wait_ge(ot_hi, b + 1)
                pe.wait_ge(ot_lo, b + 1)
                for k in ks:
                    last = mm3(pe, psB, OTh[:, k], OTl[:, k], Wo[0][:, k], Wo[1][:, k], k == 0, k == KC - 1)
                if k == KC - 1:
                    last.then_inc(y_psum, 1)

            def body(pe, b, u, before, here, more):
                for g in range(G0):
                    if here:
                        scores(b, u, g)
                    if (before or g >= 2) and (here or g < 2):
                        turn(*behind(b, u, g, 2))
                    if (before or g >= 3) and (here or g < 3):
                        weigh(*behind(b, u, g, 3))
                    if here and g in (0, 1):
                        turn_q(b, 2 + g)
                    if g == 2 and more:
                        turn_x(b + 1)
                    if g == 3 and more:
                        project_q(b + 1, [0, 1])
                    if g == 4 and before:
                        turn_o(b - 1, 1 - u, more)
                    if g == 4 and more:
                        project_q(b + 1, [2, 3])
                    if g in (6, 7):
                        if more:
                            if g == 6 and before:
                                pe.wait_ge(ot_lo, b)
                            turn_q(b + 1, g - 6)
                        if before:
                            if g == 6 and more:
                                pe.wait_ge(qs_lo, b + 2)
                            project_o(b - 1, [2 * (g - 6), 2 * (g - 6) + 1])

            turn_x(0)
            project_q(0, list(range(KC)))
            turn_q(0, 0)
            turn_q(0, 1)
            rows(body)(pe)

        @block.scalar
        def _(act):
            def x_hi(b):
                act.wait_ge(xt_psum, b + 1)
                act.activation(XTh[:], psA3, ACT.Copy).then_inc(xt_hi, 1)

            def q_hi(b):
                act.wait_ge(q_psum, b + 1)
                act.activation(QS[:, :, 0:E0], psB3, ACT.Copy).then_inc(qs_hi, 1)

            def q_turned(b, u, pr):
                act.wait_ge(qt_psum, b * PAIRS + pr + 1)
                act.activation(QT[:, u, pr], psA, ACT.Copy).then_inc(qt_ready, 1)

            def exps(b, u, g, n):
                act.wait_ge(pt_psum, n + 1)
                need(act, pv_done, n - 1)
                act.activation(PT[:, g % 2], psT(g), ACT.Exp, scale=float(E0) ** -0.5).then_inc(pt_ready, 1)

            def body(act, b, u, before, here, more):
                for g in range(G0):
                    if (before or g >= 2) and (here or g < 2):
                        exps(*behind(b, u, g, 2))
                    if here and g in (0, 1):
                        q_turned(b, u, 2 + g)
                    if g == 2 and more:
                        x_hi(b + 1)
                    if g == 4 and before:
                        act.wait_ge(ot_psum, b)
                        act.activation(OTh[:], psA3, ACT.Copy).then_inc(ot_hi, 1)
                    if g == 4 and more:
                        q_hi(b + 1)
                    if g in (6, 7) and more:
                        q_turned(b + 1, 1 - u, g - 6)

            x_hi(0)
            q_hi(0)
            q_turned(0, 0, 0)
            q_turned(0, 0, 1)
            rows(body)(act)

        @block.gpsimd
        def _(pool):
            def stage(b, u):
                pool.tensor_copy(KTb[:, u], KT[:, b].bitcast(F32)).then_inc(kv_staged, 1)
                pool.tensor_copy(Vb[:, u], V[:, b]).then_inc(kv_staged, 1)

            def dup(b):
                pool.wait_ge(qs_hi, b + 1)
                pool.wait_ge(qs_lo, b + 1)
                pool.tensor_tensor(QS[:, :, 2 * E0:4 * E0], QS[:, :, 0:2 * E0].bitcast(F32),
                                   bcast(bcast(zero[:, 0], H0), 2 * E0), ALU.add).then_inc(qs_full, 1)

            def body(pool, b, u, before, here, more):
                if more:
                    need(pool, pv_done, b * G0)
                    stage(b + 1, 1 - u)
                    dup(b + 1)

            pool.memset(zero[:], 0.0).then_inc(zero_ready, 1)
            pool.wait_ge(zero_ready, 1)
            stage(0, 0)
            dup(0)
            rows(body)(pool)

        @block.vector
        def _(dve):
            def normalize(b):
                need(dve, xt_psum, b)
                dve.tensor_scalar(xh[:], X[:, b], mv[:, b, 0:1], rstd[:, b],
                                  ALU.subtract, ALU.mult).then_inc(xh_ready, 1)

            def x_lo(b):
                dve.wait_ge(xt_hi, b + 1)
                dve.tensor_tensor(XTl[:], psA3, XTh[:].bitcast(F32), ALU.subtract).then_inc(xt_lo, 1)

            def q_lo(b):
                dve.wait_ge(qs_hi, b + 1)
                dve.tensor_tensor(QS[:, :, E0:2 * E0], psB3, QS[:, :, 0:E0].bitcast(F32), ALU.subtract)\
                   .then_inc(qs_lo, 1)

            def shift(b, g):
                n = b * G0 + g
                dve.wait_ge(s_psum, n + 1)
                s = psS(g).rearrange("p (j k) -> p j k", j=J0)
                dve.tensor_reduce(mx[:, g % 2], s, AX.X, ALU.max).then_inc(mx_ready, 1)
                dve.wait_ge(mx_ready, n + 1)
                need(dve, pt_psum, n - 3)
                dve.tensor_tensor(PR[:, g % 4].rearrange("p (j k) -> p j k", j=J0), s, bcast(mx[:, g % 2], P),
                                  ALU.subtract).then_inc(s_shifted, 1)

            def norm(b, u, half):
                n = 2 * b + half
                dve.wait_ge(pv_done, 4 * n + 4)
                dve.reciprocal(rden[:], psO(half)[:, :, E0]).then_inc(rden_ready, 1)
                dve.wait_ge(rden_ready, n + 1)
                dve.tensor_tensor(O[:, u, half * (D // 2):(half + 1) * (D // 2)].rearrange("p (h e) -> p h e", e=E0),
                                  psO(half)[:, :, 0:E0], bcast(rden[:], E0), ALU.mult).then_inc(o_ready, 1)

            def body(dve, b, u, before, here, more):
                for g in range(G0):
                    if here:
                        shift(b, g)
                    if g == 1 and more:
                        normalize(b + 1)
                    if g == 2 and more:
                        x_lo(b + 1)
                    if g == 2 and before:
                        norm(b - 1, 1 - u, 1)
                    if g == 5 and before:
                        dve.wait_ge(ot_hi, b)
                        dve.tensor_tensor(OTl[:], psA3, OTh[:].bitcast(F32), ALU.subtract).then_inc(ot_lo, 1)
                    if g == 5 and more:
                        q_lo(b + 1)
                    if g == 6 and here:
                        norm(b, u, 0)
                    if g == 7 and before:
                        dve.wait_ge(y_psum, b)
                        dve.tensor_tensor(X[:, b - 1], psB, X[:, b - 1], ALU.add).then_inc(x_added, 1)
                        dve.wait_ge(x_added, b)
                        dve.bn_stats(stats[:, b - 1], X[:, b - 1]).then_inc(stat_done, 1)

            normalize(0)
            x_lo(0)
            q_lo(0)
            rows(body)(dve)
            for b in range(B):
                dve.wait_ge(stat_done, b + 1)
                dve.bn_aggr(mv[:, b], stats[:, b]).then_inc(stat_done, 1)


def bcast(ap, n):
    return ap.unsqueeze(len(ap.shape)).broadcast_to([*ap.shape, n])

I0 = 1376
IT = [(r, min(P, I0 - r)) for r in range(0, I0, P)]
IC = [(c, min(512, I0 - c)) for c in range(0, I0, 512)]
BLK = 16
SELECT = 128
FP8_MAX = 448.0
INT4_MAX = 7.0
LEAST = 1e-8
ROUND_INT = 1.5 * 2.0 ** 23
EXPONENT = 0x7F800000
FP8_LEAST_NORMAL = 2.0 ** -6
FP8_STEP = 1.5 * 2.0 ** (23 - 3)


def quantize_fp8(dve, link, V, E, bits):
    e = E.bitcast(I32)
    link(dve.tensor_scalar(e, V.bitcast(I32), bits, None, ALU.bitwise_and))
    link(dve.tensor_scalar(E, E, FP8_LEAST_NORMAL, FP8_STEP, ALU.max, ALU.mult))
    link(dve.tensor_tensor(V, V, E, ALU.add))
    link(dve.tensor_tensor(V, V, E, ALU.subtract))


class Chain:
    def __init__(self, eng, sem):
        self.eng, self.sem, self.base, self.n, self.per = eng, sem, 0, 0, None

    def row(self, b):
        if self.n and self.per is None:
            self.per = self.n
        if self.per is not None:
            assert self.n == self.per
            self.base = b * self.per
        self.n = 0

    def __call__(self, ins):
        self.n += 1
        ins.then_inc(self.sem, 1)
        self.eng.wait_ge(self.sem, self.base + self.n)


def blocks(ap):
    return ap.rearrange("p (b e) -> p b e", e=BLK)


def quantize_rest(dve, link, src, sc, V, E, R, A, bm, g_inv):
    link(dve.tensor_tensor(blocks(A), blocks(V), bcast(sc, BLK), ALU.mult))
    link(dve.scalar_tensor_tensor(R, src, g_inv, A, ALU.mult, ALU.subtract))
    link(dve.tensor_reduce(bm[:, 0], blocks(R), AX.X, ALU.max, apply_absolute_value=True))
    link(dve.tensor_scalar(bm[:, 1], bm[:, 0], 1.0 / FP8_MAX, LEAST, ALU.mult, ALU.max))
    link(dve.reciprocal(bm[:, 2], bm[:, 1]))
    link(dve.tensor_tensor(blocks(V), blocks(R), bcast(bm[:, 2], BLK), ALU.mult))
    quantize_fp8(dve, link, V, E, EXPONENT)
    link(dve.tensor_tensor(blocks(V), blocks(V), bcast(bm[:, 1], BLK), ALU.mult))
    return dve.tensor_tensor(A, A, V, ALU.add)


def quantize_rows(dve, link, src, inv, sc, V, E, R, A, bm, g_inv, width):
    n = width - SELECT
    link(dve.tensor_tensor(blocks(V), blocks(src), bcast(inv, BLK), ALU.mult))
    quantize_fp8(dve, link, V, E, EXPONENT)
    link(dve.tensor_tensor(blocks(A[:, 0:n]), blocks(V[:, 0:n]), bcast(sc[:, 0:n // BLK], BLK), ALU.mult))
    return quantize_rest(dve, link, src[:, n:width], sc[:, n // BLK:], V[:, n:width], E[:, n:width], R, A[:, n:width],
                         bm, g_inv)


def rows_loop(body, last=1):
    def run(eng):
        body(eng, 0, 0, last)
        with eng.Fori(0, (B - 1 - last) // 2) as i:
            for u in (1, 0):
                body(eng, i * 2 + (2 - u), u, last)
        for b in range(B - last, B):
            body(eng, b, b % 2, B - 1 - b)
    return run


def need(eng, sem, value):
    if not isinstance(value, int) or value > 0:
        eng.wait_ge(sem, value)


def ffn0_prepare_weights(nc, t, sem, ps, ident, scratch, work, pick, W):
    with ExitStack() as here:
        sb = sb_in_stack(nc, here)
        NR, NV, NQ, NS = 3, 3, 2, 2
        cut = lambda at, n: work[:, at * 512:(at + n) * 512].rearrange("p (i n) -> p i n", n=512)
        R, V, Q = cut(0, NR), cut(NR, NV), cut(NR + NV, NQ)
        out = cut(NR + NV + NQ, NS)
        Gd = cut(NR + NV + NQ + NS, len(IT))
        idx = sb("idx_mid", [P, len(IT)], I32)
        ri, rif, pid, pidf = sb("ri", [P, D], I32), sb("rif", [P, D]), sb("pid", [P, KC], I32), sb("pidf", [P, KC])
        wh, wl = sb("p_wh", [P, 2, KC, P], F32R), sb("p_wl", [P, 2, KC, P], F32R)
        NB = 512 // BLK
        bm, sc, rs = (sb("p_" + n, [P, NV, NB]) for n in ("bm", "sc", "rs"))
        names = ("idx_loaded ri_loaded pid_ready pick_ready down_gathered in_psum in_hi in_lo w_psum bm_ready "
                 "sc_ready rs_ready scaled shifted rounded clipped w_ready out_psum out_hi out_lo out_rest as_float")
        S = {n: sem("p_" + n) for n in names.split()}
        gathered, stored = [sem(f"p_gathered{q}") for q in range(NR)], [sem(f"p_stored{q}") for q in range(NS)]

        ups = [("up", m, r, rows) for m in range(2) for r, rows in IT]
        units = ups + [("down", r, c, n) for r in range(0, D, P) for c, n in IC]
        UP = len(ups)
        rows_of = lambda n: units[n][3] if n < UP else P
        width_of = lambda n: D if n < UP else units[n][3]
        slices = lambda n: [(m - units[n][2], m // P, w) for m, w in IT if units[n][2] <= m < units[n][2] + units[n][3]]
        bank_in = lambda n: ps[:, n % 2, :].rearrange("p (k n) -> p k n", k=KC)
        bank_w = lambda n: ps[:, 2 + n % 3, :]
        bank_out = lambda n: ps[:, 5 + n % 3, :].rearrange("p (k n) -> p k n", k=KC)
        LAST = len(units) + 3

        with nc.Block() as block:
            @block.sync
            def _(sp):
                full = I0 // P
                sp.dma_start(idx[:, 0:full], t["ri_mid_columns"]).then_inc(S["idx_loaded"], 16)
                sp.dma_start(idx[0:I0 - full * P, full:full + 1], t["ri_mid_rest"]).then_inc(S["idx_loaded"], 16)
                sp.dma_start(ri[:], t["L0_ffn_ri_in"].partition_broadcast(P)).then_inc(S["ri_loaded"], 16)
                count = [0] * NS
                for n in range(UP, len(units)):
                    _, r, c, width = units[n]
                    whole = width // P
                    sp.wait_ge(S["out_hi"], n + 1)
                    sp.dma_start(scratch["down"][c:c + whole * P, r:r + P].rearrange("(i p) d -> p i d", p=P),
                                 out[:, n % NS, 0:whole * P].rearrange("p (i d) -> p i d", d=P))\
                        .then_inc(stored[n % NS], 16)
                    rest = width - whole * P
                    if rest:
                        sp.dma_start(scratch["down"][c + whole * P:c + width, r:r + P],
                                     out[0:rest, n % NS, whole * P:(whole + 1) * P]).then_inc(stored[n % NS], 16)
                    count[n % NS] += 2 if rest else 1
                for q in range(NS):
                    sp.wait_ge(stored[q], 16 * count[q])

            @block.gpsimd
            def _(pool):
                pool.iota(pid[:], [[P, KC]], base=0, channel_multiplier=1).then_inc(S["pid_ready"], 1)
                pool.wait_ge(S["idx_loaded"], 32)

                def gather_rows(n):
                    _, m, r, rows = units[n]
                    if n >= NR:
                        pool.wait_ge(S["in_psum"], n - NR + 1)
                    pool.indirect_dma_start(R[0:rows, n % NR], None, t[("L0_ffn_w_gate", "L0_ffn_w_up")[m]],
                                            bass.IndirectOffsetOnAxis(ap=idx[0:rows, r // P:r // P + 1], axis=0))\
                        .then_inc(gathered[n % NR], 16)

                def gather_down(m):
                    w = IT[m][1]
                    pool.indirect_dma_start(Gd[0:w, m], None, t["L0_ffn_w_down"],
                                            bass.IndirectOffsetOnAxis(ap=idx[0:w, m:m + 1], axis=0))\
                        .then_inc(S["down_gathered"], 16)

                def scale(n):
                    rows, w = rows_of(n), width_of(n)
                    pool.wait_ge(S["clipped"], n + 1)
                    if n >= NQ:
                        pool.wait_ge(S["out_psum"], n - NQ + 1)
                    pool.tensor_tensor(blocks(Q[0:rows, n % NQ, 0:w]), blocks(V[0:rows, n % NV, 0:w]),
                                       bcast(sc[0:rows, n % NV, 0:w // BLK], BLK), ALU.mult).then_inc(S["w_ready"], 1)

                for n in range(2):
                    gather_rows(n)
                for s in range(LAST):
                    if s + 2 < UP:
                        gather_rows(s + 2)
                    if 2 <= s < 2 + len(IT):
                        gather_down(s - 2)
                    if 2 <= s < len(units) + 2:
                        scale(s - 2)

            @block.tensor
            def _(pe):
                def turn_in(n):
                    rows = rows_of(n)
                    pe.wait_ge(gathered[n % NR], 16 * (n // NR + 1))
                    if n >= 2:
                        pe.wait_ge(S["in_lo"], n - 1)
                    for k in range(KC):
                        last = pe.transpose(bank_in(n)[:, k, 0:rows], R[0:rows, n % NR, k * P:(k + 1) * P],
                                            ident[0:rows, 0:rows])
                    last.then_inc(S["in_psum"], 1)

                def reorder(n):
                    rows = rows_of(n)
                    if n >= 3:
                        pe.wait_ge(S["scaled"], n - 2)
                    if n < UP:
                        pe.wait_ge(S["in_hi"], n + 1)
                        pe.wait_ge(S["in_lo"], n + 1)
                        for k in range(KC):
                            pe.matmul(bank_w(n)[0:rows], wh[:, n % 2, k, 0:rows], pick[:, k], start=k == 0, stop=False)
                            last = pe.matmul(bank_w(n)[0:rows], wl[:, n % 2, k, 0:rows], pick[:, k], start=False,
                                             stop=k == KC - 1)
                    else:
                        if n == UP:
                            pe.wait_ge(S["down_gathered"], 16 * len(IT))
                        for at, m, w in slices(n):
                            last = pe.transpose(bank_w(n)[:, at:at + w], Gd[0:w, m, units[n][1]:units[n][1] + P],
                                                ident[0:w, 0:w])
                    last.then_inc(S["w_psum"], 1)

                def turn_out(n):
                    rows = rows_of(n)
                    pe.wait_ge(S["w_ready"], n + 1)
                    if n >= 3:
                        pe.wait_ge(S["out_hi"], n - 2)
                        if n - 3 < UP:
                            pe.wait_ge(S["out_lo"], n - 2)
                    if n < UP:
                        for k in range(KC):
                            last = pe.transpose(bank_out(n)[:, k, 0:rows], Q[0:rows, n % NQ, k * P:(k + 1) * P],
                                                ident[0:rows, 0:rows])
                    else:
                        for i, (at, _, w) in enumerate(slices(n)):
                            last = pe.transpose(bank_out(n)[0:w, i], Q[:, n % NQ, at:at + w], ident[:])
                    last.then_inc(S["out_psum"], 1)

                for s in range(LAST):
                    if s < UP:
                        turn_in(s)
                    if s == 1:
                        pe.wait_ge(S["pick_ready"], KC)
                    if 1 <= s <= len(units):
                        reorder(s - 1)
                    if s >= 3:
                        turn_out(s - 3)

            @block.scalar
            def _(act):
                def split_hi(n):
                    rows = rows_of(n)
                    act.wait_ge(S["in_psum"], n + 1)
                    if n >= 2:
                        act.wait_ge(S["w_psum"], n - 1)
                    act.activation(wh[:, n % 2, :, 0:rows], bank_in(n)[:, :, 0:rows], ACT.Copy).then_inc(S["in_hi"], 1)

                def round_(n):
                    v = V[0:rows_of(n), n % NV, 0:width_of(n)]
                    act.wait_ge(S["scaled"], n + 1)
                    act.activation(v, v, ACT.Copy, bias=ROUND_INT).then_inc(S["shifted"], 1)
                    act.wait_ge(S["shifted"], n + 1)
                    act.activation(v, v, ACT.Copy, bias=-ROUND_INT).then_inc(S["rounded"], 1)

                def take(n):
                    act.wait_ge(S["out_psum"], n + 1)
                    if n < UP:
                        _, m, r, rows = units[n]
                        act.activation(W[m][0][:, :, r:r + rows], bank_out(n)[:, :, 0:rows], ACT.Copy)\
                            .then_inc(S["out_hi"], 1)
                        return
                    whole, rest = width_of(n) // P, width_of(n) % P
                    if n - NS >= UP:
                        act.wait_ge(stored[n % NS], 16 * sum(2 if width_of(i) % P else 1
                                                             for i in range(UP, n) if i % NS == n % NS))
                    if rest:
                        act.activation(out[0:rest, n % NS, whole * P:(whole + 1) * P], bank_out(n)[0:rest, whole],
                                       ACT.Copy).then_inc(S["out_rest"], 1)
                    act.activation(out[:, n % NS, 0:whole * P], bank_out(n)[:, 0:whole].rearrange("p k n -> p (k n)"),
                                   ACT.Copy).then_inc(S["out_hi"], 1)

                for s in range(LAST):
                    if s < UP:
                        split_hi(s)
                    if 1 <= s <= len(units):
                        round_(s - 1)
                    if s >= 3:
                        take(s - 3)

            @block.vector
            def _(dve):
                dve.wait_ge(S["ri_loaded"], 16)
                dve.wait_ge(S["pid_ready"], 1)
                dve.tensor_copy(rif[:], ri[:]).then_inc(S["as_float"], 1)
                dve.tensor_copy(pidf[:], pid[:]).then_inc(S["as_float"], 1)
                dve.wait_ge(S["as_float"], 2)
                for k in range(KC):
                    dve.tensor_scalar(pick[:, k], rif[:], pidf[:, k:k + 1], None, ALU.is_equal).then_inc(S["pick_ready"], 1)

                def split_lo(n):
                    rows = rows_of(n)
                    dve.wait_ge(S["in_hi"], n + 1)
                    dve.tensor_tensor(wl[:, n % 2, :, 0:rows], bank_in(n)[:, :, 0:rows],
                                      wh[:, n % 2, :, 0:rows].bitcast(F32), ALU.subtract).then_inc(S["in_lo"], 1)

                def to_scale(n):
                    rows, w = rows_of(n), width_of(n)
                    at = slice(0, w // BLK)
                    m, s, r = (x[0:rows, n % NV, at] for x in (bm, sc, rs))
                    dve.wait_ge(S["w_psum"], n + 1)
                    dve.tensor_reduce(m, blocks(bank_w(n)[0:rows, 0:w]), AX.X, ALU.max, apply_absolute_value=True)\
                       .then_inc(S["bm_ready"], 1)
                    dve.wait_ge(S["bm_ready"], n + 1)
                    if n >= NV:
                        dve.wait_ge(S["w_ready"], n - NV + 1)
                    dve.tensor_scalar(s, m, 1.0 / INT4_MAX, LEAST, ALU.mult, ALU.max).then_inc(S["sc_ready"], 1)
                    dve.wait_ge(S["sc_ready"], n + 1)
                    dve.reciprocal(r, s).then_inc(S["rs_ready"], 1)
                    dve.wait_ge(S["rs_ready"], n + 1)
                    dve.tensor_tensor(blocks(V[0:rows, n % NV, 0:w]), blocks(bank_w(n)[0:rows, 0:w]), bcast(r, BLK),
                                      ALU.mult).then_inc(S["scaled"], 1)

                def clip(n):
                    v = V[0:rows_of(n), n % NV, 0:width_of(n)]
                    dve.wait_ge(S["rounded"], n + 1)
                    dve.tensor_scalar(v, v, INT4_MAX, -INT4_MAX - 1, ALU.min, ALU.max).then_inc(S["clipped"], 1)

                def take_lo(n):
                    _, m, r, rows = units[n]
                    dve.wait_ge(S["out_hi"], n + 1)
                    dve.tensor_tensor(W[m][1][:, :, r:r + rows], bank_out(n)[:, :, 0:rows],
                                      W[m][0][:, :, r:r + rows].bitcast(F32), ALU.subtract).then_inc(S["out_lo"], 1)

                for s in range(LAST):
                    if 2 <= s < len(units) + 2:
                        clip(s - 2)
                    if s < UP:
                        split_lo(s)
                    if 1 <= s <= len(units):
                        to_scale(s - 1)
                    if 3 <= s < UP + 3:
                        take_lo(s - 3)


def ffn0_gather_x(nc, sem, ps, ident, X, mv, rstd, minus_half, pick, H, xb, g):
    with ExitStack() as here:
        sb = sb_in_stack(nc, here)
        xh = sb("g_xh", [P, 2, D])
        XTh, XTl = sb("g_XTh", [P, 2, KC, P], F32R), sb("g_XTl", [P, 2, KC, P], F32R)
        names = "eps_added rstd_ready xh_ready xt_psum xt_hi xt_lo xg_psum xg_copied xb_ready"
        S = {n: sem("g_" + n) for n in names.split()}
        psA = lambda u: ps[:, u, :]
        psG = lambda u: ps[:, 2 + u, :]
        with nc.Block() as block:
            @block.gpsimd
            def _(pool):
                pool.wait_ge(S["eps_added"], 1)
                pool.tensor_tensor(rstd[:], rstd[:], minus_half[:], ALU.pow).then_inc(S["rstd_ready"], 1)

            @block.tensor
            def _(pe):
                def turn(b, u):
                    pe.wait_ge(S["xh_ready"], b + 1)
                    pe.wait_ge(S["xt_lo"], b)
                    for k in range(KC):
                        last = pe.transpose(psA(u)[:, k * P:(k + 1) * P], xh[:, u, k * P:(k + 1) * P], ident[:])
                    last.then_inc(S["xt_psum"], 1)

                def body(pe, b, u, more):
                    if more:
                        turn(b + 1, 1 - u)
                    pe.wait_ge(S["xt_hi"], b + 1)
                    pe.wait_ge(S["xt_lo"], b + 2)
                    pe.wait_ge(S["xb_ready"], b + 1)
                    for k in range(KC):
                        pe.matmul(psG(u), XTh[:, u, k], pick[:, k], start=k == 0, stop=False)
                        last = pe.matmul(psG(u), XTl[:, u, k], pick[:, k], start=False, stop=k == KC - 1)
                    last.then_inc(S["xg_psum"], 1)

                pe.sem_inc(S["xt_lo"], 1)
                pe.sem_inc(S["xb_ready"], 2)
                turn(0, 0)
                rows_loop(body)(pe)

            @block.scalar
            def _(act):
                def hi(b, u):
                    act.wait_ge(S["xt_psum"], b + 1)
                    act.activation(XTh[:, u], psA(u).rearrange("p (k n) -> p k n", k=KC), ACT.Copy).then_inc(S["xt_hi"], 1)

                def body(act, b, u, more):
                    if more:
                        hi(b + 1, 1 - u)
                    act.wait_ge(S["xg_psum"], b + 1)
                    act.activation(H[:, b, 0:D], psG(u), ACT.Copy).then_inc(S["xg_copied"], 1)

                hi(0, 0)
                rows_loop(body)(act)

            @block.vector
            def _(dve):
                dve.tensor_scalar(rstd[:], mv[:, :, 1:2], EPS, None, ALU.add).then_inc(S["eps_added"], 1)

                def lo(b, u):
                    dve.tensor_scalar(xh[:, u], X[:, b], mv[:, b, 0:1], rstd[:, b], ALU.subtract, ALU.mult)\
                       .then_inc(S["xh_ready"], 1)
                    dve.wait_ge(S["xt_hi"], b + 1)
                    dve.tensor_tensor(XTl[:, u], psA(u).rearrange("p (k n) -> p k n", k=KC), XTh[:, u].bitcast(F32),
                                      ALU.subtract).then_inc(S["xt_lo"], 1)

                def body(dve, b, u, more):
                    if more:
                        lo(b + 1, 1 - u)
                    dve.wait_ge(S["xg_copied"], b + 1)
                    dve.tensor_reduce(xb[:, b], blocks(psG(u)), AX.X, ALU.max, apply_absolute_value=True)\
                       .then_inc(S["xb_ready"], 1)

                dve.wait_ge(S["rstd_ready"], 1)
                lo(0, 0)
                rows_loop(body)(dve)
    whole_scale(nc, sem, xb, g, "x")


def whole_scale(nc, sem, bm, g, tag):
    part, reduced = sem(tag + "_max_part"), sem(tag + "_max_whole")
    with nc.Block() as block:
        @block.vector
        def _(dve):
            dve.tensor_reduce(g[:, 4:5], bm[:], AX.XY, ALU.max).then_inc(part, 1)
            link = Chain(dve, sem(tag + "_scale_link"))
            dve.wait_ge(reduced, 1)
            link(dve.tensor_scalar(g[:, 0:1], g[:, 5:6], 1.0 / (FP8_MAX * 6.0), LEAST, ALU.mult, ALU.max))
            link(dve.reciprocal(g[:, 1:2], g[:, 0:1]))
            link(dve.tensor_scalar(g[:, 2:3], g[:, 0:1], 0.5, None, ALU.mult))
            link(dve.tensor_scalar(g[:, 3:4], g[:, 2:3], g[:, 0:1], None, ALU.mult))

        @block.gpsimd
        def _(pool):
            pool.wait_ge(part, 1)
            pool.partition_all_reduce(g[:, 5:6], g[:, 4:5], P, bass.bass_isa.ReduceOp.max).then_inc(reduced, 1)


def block_scales(dve, link, bm, g, s, inv):
    link(dve.tensor_scalar(s, bm, g[:, 1:2], None, ALU.mult))
    link(dve.tensor_scalar(s, s, 1.0 / FP8_MAX, LEAST, ALU.mult, ALU.max))
    link(dve.reciprocal(inv, s))
    link(dve.tensor_scalar(inv, inv, g[:, 1:2], None, ALU.mult))


def ffn0_up(nc, sem, ps, ident, W, H, hb, xb, g):
    with ExitStack() as here:
        sb = sb_in_stack(nc, here)
        V, E, R, A = sb("u_V", [P, D]), sb("u_E", [P, D]), sb("u_R", [P, SELECT]), sb("u_A", [P, 2, D])
        sc, inv, bm = sb("u_sc", [P, D // BLK]), sb("u_inv", [P, D // BLK]), sb("u_bm", [P, 3, SELECT // BLK])
        ATh, ATl = sb("u_ATh", [P, 2, KC, P], F32R), sb("u_ATl", [P, 2, KC, P], F32R)
        T = sb("u_T", [P, I0])
        names = "a_ready at_psum at_hi at_lo gate_psum up_psum tanh_ready u_ready h_ready hb_ready"
        S = {n: sem("u_" + n) for n in names.split()}
        psA = lambda u: ps[:, u, :]
        gate = ps[:, 2:5, :].rearrange("p c n -> p (c n)")
        up = ps[:, 5:8, :].rearrange("p c n -> p (c n)")
        with nc.Block() as block:
            @block.tensor
            def _(pe):
                def turn(b, u):
                    pe.wait_ge(S["a_ready"], b + 1)
                    pe.wait_ge(S["at_lo"], b)
                    for k in range(KC):
                        last = pe.transpose(psA(u)[:, k * P:(k + 1) * P], A[:, u, k * P:(k + 1) * P], ident[:])
                    last.then_inc(S["at_psum"], 1)

                def product(out, u, w, pieces):
                    for c, n in pieces:
                        for k in range(KC):
                            last = mm3(pe, out[:, c:c + n], ATh[:, u, k], ATl[:, u, k], w[0][:, k, c:c + n],
                                       w[1][:, k, c:c + n], k == 0, k == KC - 1)
                    return last

                def body(pe, b, u, more):
                    pe.wait_ge(S["at_hi"], b + 1)
                    pe.wait_ge(S["at_lo"], b + 2)
                    need(pe, S["u_ready"], b)
                    product(gate, u, W[0], IC).then_inc(S["gate_psum"], 1)
                    need(pe, S["h_ready"], b)
                    product(up, u, W[1], IC[:-1])
                    if more:
                        turn(b + 1, 1 - u)
                    product(up, u, W[1], IC[-1:]).then_inc(S["up_psum"], 1)

                pe.sem_inc(S["at_lo"], 1)
                turn(0, 0)
                rows_loop(body)(pe)

            @block.scalar
            def _(act):
                def hi(b, u):
                    act.wait_ge(S["at_psum"], b + 1)
                    act.wait_ge(S["up_psum"], b)
                    act.activation(ATh[:, u], psA(u).rearrange("p (k n) -> p k n", k=KC), ACT.Copy).then_inc(S["at_hi"], 1)

                def body(act, b, u, more):
                    act.wait_ge(S["gate_psum"], b + 1)
                    need(act, S["h_ready"], b)
                    act.activation(T[:], gate[:, 0:I0], ACT.Tanh, scale=g[:, 2:3]).then_inc(S["tanh_ready"], 1)
                    if more:
                        hi(b + 1, 1 - u)

                act.sem_inc(S["up_psum"], 1)
                hi(0, 0)
                rows_loop(body)(act)

            @block.vector
            def _(dve):
                link = Chain(dve, sem("u_link"))

                def quantize(b, u):
                    link.row(b)
                    block_scales(dve, link, xb[:, b], g, sc[:], inv[:])
                    quantize_rows(dve, link, H[:, b, 0:D], inv[:], sc[:], V[:], E[:], R[:], A[:, u], bm, g[:, 1:2], D)\
                        .then_inc(S["a_ready"], 1)

                def lo(b, u):
                    dve.wait_ge(S["at_hi"], b + 1)
                    dve.tensor_tensor(ATl[:, u], psA(u).rearrange("p (k n) -> p k n", k=KC), ATh[:, u].bitcast(F32),
                                      ALU.subtract).then_inc(S["at_lo"], 1)

                def body(dve, b, u, more):
                    if more:
                        quantize(b + 1, 1 - u)
                    dve.wait_ge(S["tanh_ready"], b + 1)
                    dve.scalar_tensor_tensor(T[:], T[:], 1.0, gate[:, 0:I0], ALU.add, ALU.mult).then_inc(S["u_ready"], 1)
                    if more:
                        lo(b + 1, 1 - u)
                    dve.wait_ge(S["up_psum"], b + 2)
                    dve.wait_ge(S["u_ready"], b + 1)
                    dve.scalar_tensor_tensor(H[:, b], T[:], g[:, 3:4], up[:, 0:I0], ALU.mult, ALU.mult)\
                       .then_inc(S["h_ready"], 1)
                    dve.wait_ge(S["h_ready"], b + 1)
                    dve.tensor_reduce(hb[:, b], blocks(H[:, b]), AX.X, ALU.max, apply_absolute_value=True)\
                       .then_inc(S["hb_ready"], 1)

                quantize(0, 0)
                lo(0, 0)
                rows_loop(body)(dve)
    whole_scale(nc, sem, hb, g, "h")


def ffn0_down(nc, sem, ps, ident, scratch, X, stats, mv, H, hb, g):
    MT = len(IT)
    with ExitStack() as here:
        sb = sb_in_stack(nc, here)
        W = [sb(f"Wd{s}", [P, MT, D], F32R) for s in "hl"]
        sc, inv = sb("d_sc", [P, B, I0 // BLK]), sb("d_inv", [P, B, I0 // BLK])
        with ExitStack() as loading:
            R = sb_in_stack(nc, loading)("wdrows", [P, MT, D])
            fetched, wt_hi, wt_lo = sem("wd_fetched"), sem("wd_hi"), sem("wd_lo")
            full, rest = I0 // P, I0 % P
            with nc.Block() as block:
                @block.sync
                def _(sp):
                    sp.dma_start(R[:, 0:full], scratch["down"][0:full * P].rearrange("(m p) d -> p m d", p=P))\
                      .then_inc(fetched, 16)
                    sp.dma_start(R[0:rest, full], scratch["down"][full * P:I0]).then_inc(fetched, 16)

                @block.scalar
                def _(act):
                    act.wait_ge(fetched, 32)
                    for n, (m, w) in enumerate(IT):
                        act.activation(W[0][0:w, n], R[0:w, n], ACT.Copy).then_inc(wt_hi, 1)

                @block.vector
                def _(dve):
                    block_scales(dve, Chain(dve, sem("wd_link")), hb[:], g, sc[:], inv[:])
                    for n, (m, w) in enumerate(IT):
                        dve.wait_ge(wt_hi, n + 1)
                        dve.tensor_tensor(W[1][0:w, n], R[0:w, n], W[0][0:w, n].bitcast(F32), ALU.subtract)\
                           .then_inc(wt_lo, 1)

        V, E, R, A = sb("d_V", [P, 2, I0]), sb("d_E", [P, I0]), sb("d_R", [P, SELECT]), sb("d_A", [P, 2, I0])
        bm = sb("d_bm", [P, 3, SELECT // BLK])
        ATh, ATl = sb("d_ATh", [P, MT, P], F32R), sb("d_ATl", [P, MT, P], F32R)
        names = "v_scaled v_rounded normal_ready a_ready at_psum at_hi at_lo y_psum x_added stat_done"
        S = {n: sem("d_" + n) for n in names.split()}
        turned = lambda u: ps[:, 3 * u:3 * u + 3, :].rearrange("p c (m n) -> p (c m) n", n=P)
        y = lambda u: ps[:, 6 + u, :]
        full = I0 // P
        parts = [(P, slice(m, min(m + 4, full))) for m in range(0, full, 4)] + [(IT[-1][1], slice(full, MT))]
        NP = len(parts)
        N = I0 - SELECT
        with nc.Block() as block:
            @block.tensor
            def _(pe):
                def body(pe, b, u, more):
                    pe.wait_ge(S["a_ready"], b + 1)
                    pe.wait_ge(S["normal_ready"], b + 1)
                    pe.wait_ge(S["at_lo"], NP * b)
                    for n, (m, w) in enumerate(IT):
                        last = pe.transpose(turned(u)[0:w, n], A[:, u, m:m + w], ident[:])
                    last.then_inc(S["at_psum"], 1)
                    pe.wait_ge(S["x_added"], b + 1)
                    for part, (w, m) in enumerate(parts):
                        pe.wait_ge(S["at_hi"], NP * b + part + 1)
                        pe.wait_ge(S["at_lo"], NP * (b + 1) + part + 1)
                        for n in range(m.start, m.stop):
                            last = mm3(pe, y(u), ATh[0:w, n], ATl[0:w, n], W[0][0:w, n], W[1][0:w, n], n == 0, n == MT - 1)
                    last.then_inc(S["y_psum"], 1)

                pe.sem_inc(S["at_lo"], NP)
                pe.sem_inc(S["x_added"], 2)
                rows_loop(body)(pe)

            @block.scalar
            def _(act):
                def body(act, b, u, more):
                    act.wait_ge(S["at_psum"], b + 1)
                    need(act, S["y_psum"], b)
                    for w, m in parts:
                        act.activation(ATh[0:w, m], turned(u)[0:w, m], ACT.Copy).then_inc(S["at_hi"], 1)

                rows_loop(body)(act)

            @block.gpsimd
            def _(pool):
                def scale_in(b, u):
                    if not isinstance(b, int) or b >= 2:
                        pool.wait_ge(S["a_ready"], b - 1)
                        pool.wait_ge(S["normal_ready"], b - 1)
                    pool.tensor_tensor(blocks(V[:, u]), blocks(H[:, b]), bcast(inv[:, b], BLK), ALU.mult)\
                        .then_inc(S["v_scaled"], 1)

                def scale_out(b, u):
                    pool.wait_ge(S["v_rounded"], b + 1)
                    if not isinstance(b, int) or b >= 2:
                        pool.wait_ge(S["at_psum"], b - 1)
                    pool.tensor_tensor(blocks(A[:, u, 0:N]), blocks(V[:, u, 0:N]), bcast(sc[:, b, 0:N // BLK], BLK),
                                       ALU.mult).then_inc(S["normal_ready"], 1)

                def body(pool, b, u, more):
                    if more:
                        scale_out(b + 1, 1 - u)
                    if more >= 3:
                        scale_in(b + 3, 1 - u)

                scale_in(0, 0)
                scale_in(1, 1)
                scale_out(0, 0)
                scale_in(2, 0)
                rows_loop(body, last=3)(pool)

            @block.vector
            def _(dve):
                link = Chain(dve, sem("d_link"))

                def normal(b, u):
                    link.row(b)
                    dve.wait_ge(S["v_scaled"], b + 1)
                    quantize_fp8(dve, link, V[:, u], E[:], EXPONENT)
                    dve.sem_inc(S["v_rounded"], 1)

                def outlier(b, u):
                    quantize_rest(dve, link, H[:, b, N:I0], sc[:, b, N // BLK:], V[:, u, N:I0], E[:, 0:SELECT], R[:],
                                  A[:, u, N:I0], bm, g[:, 1:2]).then_inc(S["a_ready"], 1)

                def body(dve, b, u, more):
                    if more:
                        normal(b + 1, 1 - u)
                    for part, (w, m) in enumerate(parts):
                        dve.wait_ge(S["at_hi"], NP * b + (part + 1 if part < NP - 2 else NP))
                        dve.tensor_tensor(ATl[0:w, m], turned(u)[0:w, m], ATh[0:w, m].bitcast(F32), ALU.subtract)\
                           .then_inc(S["at_lo"], 1)
                    if more:
                        outlier(b + 1, 1 - u)
                    dve.wait_ge(S["y_psum"], b + 1)
                    dve.scalar_tensor_tensor(X[:, b], y(u), g[:, 0:1], X[:, b], ALU.mult, ALU.add).then_inc(S["x_added"], 1)
                    dve.wait_ge(S["x_added"], b + 3)
                    dve.bn_stats(stats[:, b], X[:, b]).then_inc(S["stat_done"], 1)

                normal(0, 0)
                outlier(0, 0)
                rows_loop(body)(dve)
                for b in range(B):
                    dve.wait_ge(S["stat_done"], b + 1)
                    dve.bn_aggr(mv[:, b], stats[:, b]).then_inc(S["stat_done"], 1)


def layer0_ffn(nc, t, sem, ps, ident, X, stats, mv, rstd, minus_half, scratch):
    with ExitStack() as here:
        sb = sb_in_stack(nc, here)
        H = sb("H", [P, B, I0])
        xb, hb, g = sb("xb", [P, B, D // BLK]), sb("hb", [P, B, I0 // BLK]), sb("g", [P, 6])
        with ExitStack() as weights:
            sbw = sb_in_stack(nc, weights)
            W = [[sbw(f"W{n}{s}", [P, KC, I0], F32R) for s in "hl"] for n in ("gate", "up")]
            with ExitStack() as reordering:
                pick = sb_in_stack(nc, reordering)("pick", [P, KC, D], F32R)
                work = H[:].rearrange("p b i -> p (b i)")
                ffn0_prepare_weights(nc, t, sem, ps, ident, scratch, work, pick, W)
                ffn0_gather_x(nc, sem, ps, ident, X, mv, rstd, minus_half, pick, H, xb, g)
            ffn0_up(nc, sem, ps, ident, W, H, hb, xb, g)
        ffn0_down(nc, sem, ps, ident, scratch, X, stats, mv, H, hb, g)

G1, J1, E1 = 8, 4, 128
W1 = J1 * E1
QK = W1 + E1
VE = E1 + 2
MULT = 0.08838834764831845
CAP = 30.0
MASKED = -1e30


def rope_tables():
    freq = (np.float32(1.0) / np.float32(10000.0) ** (np.arange(0, E1, 2, dtype=np.float32) / np.float32(E1))).astype(np.float32)
    phase = np.arange(P, dtype=np.float32)[:, None] * freq[None, :]
    c, s = np.cos(phase), np.sin(phase)
    return np.stack([np.concatenate([c, c], 1), np.concatenate([-s, s], 1)], 1).astype(np.float32)


def normalize_rows(nc, sem, ps, ident, X, mv, rstd, minus_half, XTh, XTl):
    with ExitStack() as here:
        sb = sb_in_stack(nc, here)
        xh = sb("n_xh", [P, 2, D])
        S = {n: sem("n_" + n) for n in "eps_added rstd_ready xh_ready xt_psum xt_hi xt_lo".split()}
        psA = lambda u: ps[:, u, :]
        with nc.Block() as block:
            @block.gpsimd
            def _(pool):
                pool.wait_ge(S["eps_added"], 1)
                pool.tensor_tensor(rstd[:], rstd[:], minus_half[:], ALU.pow).then_inc(S["rstd_ready"], 1)

            @block.tensor
            def _(pe):
                def body(pe, b, u, more):
                    pe.wait_ge(S["xh_ready"], b + 1)
                    for k in range(KC):
                        last = pe.transpose(psA(u)[:, k * P:(k + 1) * P], xh[:, u, k * P:(k + 1) * P], ident[:])
                    last.then_inc(S["xt_psum"], 1)

                rows_loop(body)(pe)

            @block.scalar
            def _(act):
                def body(act, b, u, more):
                    act.wait_ge(S["xt_psum"], b + 1)
                    act.activation(XTh[:, b], psA(u).rearrange("p (k n) -> p k n", k=KC), ACT.Copy).then_inc(S["xt_hi"], 1)

                rows_loop(body)(act)

            @block.vector
            def _(dve):
                dve.tensor_scalar(rstd[:], mv[:, :, 1:2], EPS, None, ALU.add).then_inc(S["eps_added"], 1)

                def unit(b, u):
                    dve.tensor_scalar(xh[:, u], X[:, b], mv[:, b, 0:1], rstd[:, b], ALU.subtract, ALU.mult)\
                       .then_inc(S["xh_ready"], 1)

                def body(dve, b, u, more):
                    if more:
                        unit(b + 1, 1 - u)
                    dve.wait_ge(S["xt_hi"], b + 1)
                    dve.tensor_tensor(XTl[:, b], psA(u).rearrange("p (k n) -> p k n", k=KC), XTh[:, b].bitcast(F32),
                                      ALU.subtract).then_inc(S["xt_lo"], 1)

                dve.wait_ge(S["rstd_ready"], 1)
                unit(0, 0)
                rows_loop(body)(dve)


def layer1_tables(nc, t, sem, ps, ident, tables, bias):
    with ExitStack() as here:
        sb = sb_in_stack(nc, here)
        rope = sb("rope", [P, 2, E1])
        m8, m, live, q_bias = sb("m8", [P, P], mybir.dt.uint8), sb("m", [P, P]), sb("live", [P, 1]), sb("q_bias", [P, P])
        loaded, turned, ready = sem("t_loaded"), sem("t_turned"), sem("t_ready")
        q_bias_steps = sem("t_q_bias_steps")
        with nc.Block() as block:
            @block.sync
            def _(sp):
                sp.dma_start(rope[:], t["rope"]).then_inc(loaded, 16)
                sp.dma_start(m8[:], t["mask"]).then_inc(loaded, 16)

            @block.vector
            def _(dve):
                link = Chain(dve, q_bias_steps)
                dve.wait_ge(loaded, 32)
                link(dve.tensor_copy(m[:], m8[:]))
                link(dve.tensor_reduce(live[:], m[:], AX.X, ALU.max))
                link(dve.tensor_scalar(q_bias[:], m[:], 1.0, live[:], ALU.subtract, ALU.mult))
                link(dve.tensor_scalar(q_bias[:], q_bias[:], -MASKED / CAP, None, ALU.mult))
                for n in range(2):
                    for h in range(J1):
                        dve.tensor_scalar(tables[:, n, h], rope[:, n], live[:], None, ALU.mult)
                    dve.tensor_copy(tables[:, n, J1], rope[:, n])
                dve.wait_ge(turned, 1)
                dve.tensor_copy(bias[:], ps[:, 0, 0:P]).then_inc(ready, 1)

            @block.tensor
            def _(pe):
                pe.wait_ge(q_bias_steps, 4)
                pe.transpose(ps[:, 0, 0:P], q_bias[:], ident[:]).then_inc(turned, 1)


def layer1_attention(nc, t, sem, ps, X, stats, mv, ident, CTh, CTl, XTh, XTl, tables, bias):
    with ExitStack() as here:
        sb = sb_in_stack(nc, here)
        qkv_in = sb("qkv_in", [P, KC, QK + E1])
        o_in = qkv_in[:].rearrange("p k n -> p (k n)")[:, 0:J1 * D].rearrange("p (j n) -> p j n", n=D)
        Wi = [[sb(f"Wi{n}{s}", [P, KC, QK + E1], F32R) for s in "hl"] for n in range(2)]
        Wo = [[sb(f"Wo1{n}{s}", [P, J1, D], F32R) for s in "hl"] for n in range(2)]
        T1, T2 = sb("T1", [P, QK]), sb("T2", [P, QK])
        QTh, QTl = sb("QTh", [P, QK], F32R), sb("QTl", [P, QK], F32R)
        V = [sb(f"V1{s}", [P, 2, VE], F32R) for s in "hl"]
        E = sb("E", [P, W1])
        Ph, Pl = sb("Ph", [P, W1], F32R), sb("Pl", [P, W1], F32R)
        rden, A = sb("rden1", [P, J1]), sb("A1", [P, J1, E1])
        AT = [sb(f"AT{s}", [P, 2, J1, P], F32R) for s in "hl"]
        names = ("w_loaded wo_loaded w_hi w_lo qkv_psum t_one t_two v_hi v_lo roped qk_psum qk_hi qk_lo s_psum tanh_ready masked "
                 "exp_ready p_hi p_lo pv_psum rden_ready a_ready at_psum at_hi at_lo y_psum x_added preset stat_done")
        S = {n: sem("s_" + n) for n in names.split()}
        qkv = ps[:, 0:2, :].rearrange("p c n -> p (c n)")
        turned = ps[:, 2:4, :].rearrange("p c n -> p (c n)")
        psS = ps[:, 4, :]
        psV = ps[:, 5:7, 0:2 * VE].rearrange("p c (j e) -> p c j e", e=VE)
        psY = ps[:, 7, :]
        slices = [(True, k) for k in range(KC)] + [(False, j) for j in range(J1)]
        plan = {1: [0], 2: [1], 3: [2], 4: [3], 5: [4, 5], 6: [6, 7]}

        def steps(eng, body):
            with eng.Fori(0, G1 // 2) as i:
                for n in range(2):
                    for b in range(B):
                        body(i * 2 + n, n, b, i * (2 * B) + (n * B + b))

        def split_slice(n, w):
            inputs, k = slices[w]
            return (qkv_in[:, k], [x[:, k] for x in Wi[n]]) if inputs else (o_in[:, k], [x[:, k] for x in Wo[n]])

        with nc.Block() as block:
            @block.sync
            def _(sp):
                def load(g, n):
                    for dst, src in ((qkv_in[:, :, 0:W1], t["Wq1"][g]), (qkv_in[:, :, W1:QK], t["Wk1"][g]),
                                     (qkv_in[:, :, QK:QK + E1], t["Wv1"][g])):
                        sp.dma_start(dst, src).then_inc(S["w_loaded"], 16)
                    sp.wait_ge(S["w_lo"], n * len(slices) + KC)
                    sp.dma_start(o_in, t["Wo1"][g]).then_inc(S["wo_loaded"], 16)
                    sp.wait_ge(S["w_lo"], (n + 1) * len(slices))

                for g in range(G1):
                    load(g, g)
                load(0, G1)

            @block.gpsimd
            def _(pool):
                def split(n, w, count):
                    src, (hi, lo) = split_slice(n, w)
                    pool.wait_ge(S["w_hi"], count)
                    pool.tensor_tensor(lo, src, hi.bitcast(F32), ALU.subtract).then_inc(S["w_lo"], 1)

                for x in Wo[1]:
                    pool.memset(x[:].bitcast(F32), 0.0).then_inc(S["preset"], 1)
                pool.wait_ge(S["w_loaded"], 48)
                for w in range(len(slices)):
                    split(0, w, w + 1)

                def body(g, n, b, s):
                    for w in plan.get(b, []):
                        split(1 - n, w, (g + 1) * len(slices) + w + 1)

                steps(pool, body)

            @block.tensor
            def _(pe):
                def project(n, b):
                    for k in range(KC):
                        mm3(pe, qkv[:, 0:W1], XTh[:, b, k], XTl[:, b, k], Wi[n][0][:, k, 0:W1], Wi[n][1][:, k, 0:W1],
                            k == 0, k == KC - 1)
                    for k in range(KC):
                        c = slice(b * P, (b + 1) * P)
                        last = mm3(pe, qkv[:, W1:QK + E1], CTh[:, k, c], CTl[:, k, c], Wi[n][0][:, k, W1:QK + E1],
                                   Wi[n][1][:, k, W1:QK + E1], k == 0, k == KC - 1)
                    last.then_inc(S["qkv_psum"], 1)

                def turn(s):
                    pe.wait_ge(S["roped"], s + 1)
                    for j in range(J1 + 1):
                        last = pe.transpose(turned[:, j * P:(j + 1) * P], T1[:, j * E1:(j + 1) * E1], ident[:])
                    last.then_inc(S["qk_psum"], 1)

                def output(n, u, heads):
                    for j in heads:
                        last = mm3(pe, psY, AT[0][:, u, j], AT[1][:, u, j], Wo[n][0][:, j], Wo[n][1][:, j],
                                   j == 0, j == J1 - 1)
                    return last

                def body(g, n, b, s):
                    u = b % 2
                    pe.wait_ge(S["qk_lo"], s + 1)
                    pe.wait_ge(S["at_lo"], s + 1)
                    mm3(pe, psS, QTh[:, W1:QK], QTl[:, W1:QK], QTh[:, 0:W1], QTl[:, 0:W1], True, True)\
                        .then_inc(S["s_psum"], 1)
                    n2, b2 = (n, b + 1) if b + 1 < B else (1 - n, 0)
                    if b2 == 0:
                        pe.wait_ge(S["w_lo"], (g + 2) * len(slices))
                    pe.wait_ge(S["v_lo"], s + 1)
                    project(n2, b2)
                    pe.wait_ge(S["p_lo"], s + 1)
                    pe.wait_ge(S["a_ready"], s + 1)
                    for j in range(J1):
                        p = slice(j * P, (j + 1) * P)
                        last = mm3(pe, psV[:, j // 2, j % 2], Ph[:, p], Pl[:, p], V[0][:, u], V[1][:, u], True, True)
                    last.then_inc(S["pv_psum"], 1)
                    n0 = n if b else 1 - n
                    pe.wait_ge(S["x_added"], s + 1)
                    output(n0, 1 - u, (0, 1))
                    turn(s + 1)
                    pe.wait_ge(S["a_ready"], s + 2)
                    for j in range(J1):
                        last = pe.transpose(psS[:, j * P:(j + 1) * P], A[:, j], ident[:])
                    last.then_inc(S["at_psum"], 1)
                    output(n0, 1 - u, (2, 3)).then_inc(S["y_psum"], 1)

                pe.wait_ge(S["preset"], 8)
                pe.wait_ge(S["w_lo"], len(slices))
                project(0, 0)
                turn(0)
                steps(pe, body)
                pe.wait_ge(S["at_lo"], G1 * B + 1)
                pe.wait_ge(S["x_added"], G1 * B + 1)
                output(1, 1, range(J1)).then_inc(S["y_psum"], 1)

            @block.scalar
            def _(act):
                def split(n, w):
                    src, (hi, lo) = split_slice(n, w)
                    act.activation(hi, src, ACT.Copy).then_inc(S["w_hi"], 1)

                def inputs(s, u):
                    act.wait_ge(S["qkv_psum"], s + 1)
                    act.activation(V[0][:, u, 0:E1], qkv[:, QK:QK + E1], ACT.Copy).then_inc(S["v_hi"], 1)
                    act.wait_ge(S["qk_psum"], s + 1)
                    act.activation(QTh[:], turned[:, 0:QK], ACT.Copy).then_inc(S["qk_hi"], 1)

                act.wait_ge(S["w_loaded"], 48)
                for w in range(len(slices)):
                    if w == KC:
                        act.wait_ge(S["wo_loaded"], 16)
                    split(0, w)
                act.wait_ge(S["preset"], 6)
                inputs(0, 0)

                def body(g, n, b, s):
                    u = b % 2
                    act.wait_ge(S["s_psum"], s + 1)
                    act.activation(E[:], psS, ACT.Tanh, scale=MULT / CAP).then_inc(S["tanh_ready"], 1)
                    if b in plan:
                        if b == 1:
                            act.wait_ge(S["w_loaded"], (g + 2) * 48)
                        if b == 5:
                            act.wait_ge(S["wo_loaded"], (g + 2) * 16)
                        for w in plan[b]:
                            split(1 - n, w)
                    act.wait_ge(S["masked"], s + 1)
                    act.activation(E[:], E[:], ACT.Exp, scale=CAP).then_inc(S["exp_ready"], 1)
                    act.wait_ge(S["exp_ready"], s + 1)
                    act.activation(Ph[:], E[:], ACT.Copy).then_inc(S["p_hi"], 1)
                    inputs(s + 1, 1 - u)
                    act.wait_ge(S["at_psum"], s + 1)
                    act.activation(AT[0][:, u], psS.rearrange("p (j n) -> p j n", j=J1), ACT.Copy).then_inc(S["at_hi"], 1)

                steps(act, body)

            @block.vector
            def _(dve):
                def rope(s, u):
                    src = qkv[:, 0:QK].rearrange("p (h a e) -> p h a e", h=J1 + 1, a=2)
                    half = lambda x: x.rearrange("p h (a e) -> p h a e", a=2)
                    dve.wait_ge(S["v_hi"], s + 1)
                    dve.tensor_tensor(T1[:].rearrange("p (h a e) -> p h a e", h=J1 + 1, a=2), src, half(tables[:, 0]),
                                      ALU.mult).then_inc(S["t_one"], 1)
                    dve.tensor_tensor(T2[:].rearrange("p (h a e) -> p h a e", h=J1 + 1, a=2), src[:, :, ::-1],
                                      half(tables[:, 1]), ALU.mult).then_inc(S["t_two"], 1)
                    dve.tensor_tensor(V[1][:, u, 0:E1], qkv[:, QK:QK + E1], V[0][:, u, 0:E1].bitcast(F32), ALU.subtract)\
                       .then_inc(S["v_lo"], 1)
                    dve.wait_ge(S["t_one"], s + 1)
                    dve.wait_ge(S["t_two"], s + 1)
                    dve.tensor_tensor(T1[:], T1[:], T2[:], ALU.add).then_inc(S["roped"], 1)

                def low(s):
                    dve.wait_ge(S["qk_hi"], s + 1)
                    dve.tensor_tensor(QTl[:], turned[:, 0:QK], QTh[:].bitcast(F32), ALU.subtract).then_inc(S["qk_lo"], 1)

                def add(s, b):
                    dve.wait_ge(S["y_psum"], s)
                    dve.tensor_tensor(X[:, b], psY, X[:, b], ALU.add).then_inc(S["x_added"], 1)

                for u in range(2):
                    dve.memset(V[0][:, u, E1:VE].bitcast(F32), 1.0).then_inc(S["preset"], 1)
                    dve.memset(V[1][:, u, E1:VE].bitcast(F32), 0.0).then_inc(S["preset"], 1)
                for x in AT:
                    dve.memset(x[:, 1].bitcast(F32), 0.0).then_inc(S["preset"], 1)
                for name in ("at_lo", "a_ready", "x_added"):
                    dve.sem_inc(S[name], 1)
                rope(0, 0)
                low(0)

                def body(g, n, b, s):
                    u = b % 2
                    dve.wait_ge(S["tanh_ready"], s + 1)
                    dve.tensor_tensor(E[:].rearrange("p (j q) -> p j q", j=J1), E[:].rearrange("p (j q) -> p j q", j=J1),
                                      bias[:].unsqueeze(1).broadcast_to([P, J1, P]), ALU.add).then_inc(S["masked"], 1)
                    dve.wait_ge(S["p_hi"], s + 1)
                    dve.tensor_tensor(Pl[:], E[:], Ph[:].bitcast(F32), ALU.subtract).then_inc(S["p_lo"], 1)
                    rope(s + 1, 1 - u)
                    dve.wait_ge(S["pv_psum"], s + 1)
                    r = rden[:].rearrange("p (c j) -> p c j", c=2)
                    dve.reciprocal(r, psV[:, :, :, E1]).then_inc(S["rden_ready"], 1)
                    dve.wait_ge(S["rden_ready"], s + 1)
                    dve.tensor_tensor(A[:].rearrange("p (c j) e -> p c j e", c=2), psV[:, :, :, 0:E1], bcast(r, E1),
                                      ALU.mult).then_inc(S["a_ready"], 1)
                    low(s + 1)
                    dve.wait_ge(S["at_hi"], s + 1)
                    dve.tensor_tensor(AT[1][:, u], psS.rearrange("p (j n) -> p j n", j=J1), AT[0][:, u].bitcast(F32),
                                      ALU.subtract).then_inc(S["at_lo"], 1)
                    add(s + 1, (b - 1) % B)

                steps(dve, body)
                add(G1 * B + 1, B - 1)
                dve.wait_ge(S["x_added"], G1 * B + 2)
                for b in range(B):
                    dve.bn_stats(stats[:, b], X[:, b]).then_inc(S["stat_done"], 1)
                for b in range(B):
                    dve.wait_ge(S["stat_done"], b + 1)
                    dve.bn_aggr(mv[:, b], stats[:, b]).then_inc(S["stat_done"], 1)


def layer1_ffn(nc, t, sem, ps, ident, X, mv, rstd, minus_half):
    IB = 32
    OC = D // P
    with ExitStack() as here:
        sb = sb_in_stack(nc, here)
        WT = [sb(f"WT{s}", [P, KC, D], F32R) for s in "hl"]
        add_bias = sb("add_bias", [P, D])
        bias_loaded = sem("f_bias_loaded")
        with ExitStack() as loading:
            own = sb_in_stack(nc, loading)
            packed = own("packed", [P, OC, D // 2], I32)
            q = own("q", [P, OC, D // 2, 2], I32)
            W = own("W1f", [P, OC, D])
            s16, v8 = own("s16", [P, OC, D // IB], mybir.dt.float16), own("v8", [P, OC, D // IB], mybir.dt.uint8)
            sc, half = own("sc1", [P, OC, D // IB]), own("half1", [P, OC, D // IB])
            loaded, turned, w_hi, w_lo, w_done = sem("f_loaded"), sem("f_turned"), sem("f_w_hi"), sem("f_w_lo"), sem("f_w_done")
            with nc.Block() as block:
                @block.sync
                def _(sp):
                    sp.dma_start(packed[:], t["packed"]).then_inc(loaded, 16)
                    sp.dma_start(s16[:], t["scale"]).then_inc(loaded, 16)
                    sp.dma_start(v8[:], t["var_mask"]).then_inc(loaded, 16)
                    sp.dma_start(add_bias[:], t["L1_ffn_bias"].partition_broadcast(P)).then_inc(bias_loaded, 16)

                @block.vector
                def _(dve):
                    link = Chain(dve, w_done)
                    dve.wait_ge(loaded, 48)
                    link(dve.tensor_scalar(q[:, :, :, 0], packed[:], 15, None, ALU.bitwise_and))
                    link(dve.tensor_scalar(q[:, :, :, 1], packed[:], 4, 15, ALU.logical_shift_right, ALU.bitwise_and))
                    link(dve.tensor_scalar(half[:], v8[:], 0.5, 0.5, ALU.mult, ALU.add))
                    link(dve.tensor_tensor(sc[:], half[:], s16[:], ALU.mult))
                    for o in range(OC):
                        link(dve.scalar_tensor_tensor(W[:, o].rearrange("p (b e) -> p b e", e=IB),
                                                      q[:, o].rearrange("p (b e) c -> p b (e c)", b=D // IB), -8.0,
                                                      bcast(sc[:, o], IB), ALU.add, ALU.mult))
                    for k in range(KC):
                        dve.wait_ge(w_hi, k + 1)
                        dve.tensor_tensor(WT[1][:, k], ps[:, k, :], WT[0][:, k].bitcast(F32), ALU.subtract).then_inc(w_lo, 1)

                @block.tensor
                def _(pe):
                    pe.wait_ge(w_done, 4 + OC)
                    for k in range(KC):
                        for o in range(OC):
                            last = pe.transpose(ps[:, k, o * P:(o + 1) * P], W[:, o, k * P:(k + 1) * P], ident[:])
                        last.then_inc(turned, 1)

                @block.scalar
                def _(act):
                    for k in range(KC):
                        act.wait_ge(turned, k + 1)
                        act.activation(WT[0][:, k], ps[:, k, :], ACT.Copy).then_inc(w_hi, 1)

        xh = sb("f_xh", [P, 2, D])
        XTh, XTl = sb("f_XTh", [P, 2, KC, P], F32R), sb("f_XTl", [P, 2, KC, P], F32R)
        names = "eps_added rstd_ready xh_ready xt_psum xt_hi xt_lo y_psum biased out_ready stored"
        S = {n: sem("f_" + n) for n in names.split()}
        psA = lambda u: ps[:, u, :]
        psY = lambda u: ps[:, 2 + u, :]
        out = t["out"].rearrange("b p d -> p b d")
        with nc.Block() as block:
            @block.gpsimd
            def _(pool):
                pool.wait_ge(S["eps_added"], 1)
                pool.tensor_tensor(rstd[:], rstd[:], minus_half[:], ALU.pow).then_inc(S["rstd_ready"], 1)
                pool.wait_ge(bias_loaded, 16)

                def body(pool, b, u, more):
                    pool.wait_ge(S["xh_ready"], b + 1)
                    pool.tensor_tensor(X[:, b], X[:, b], add_bias[:], ALU.add).then_inc(S["biased"], 1)

                rows_loop(body)(pool)

            @block.tensor
            def _(pe):
                def turn(b, u):
                    pe.wait_ge(S["xh_ready"], b + 1)
                    pe.wait_ge(S["xt_lo"], b)
                    for k in range(KC):
                        last = pe.transpose(psA(u)[:, k * P:(k + 1) * P], xh[:, u, k * P:(k + 1) * P], ident[:])
                    last.then_inc(S["xt_psum"], 1)

                def body(pe, b, u, more):
                    if more:
                        turn(b + 1, 1 - u)
                    pe.wait_ge(S["xt_hi"], b + 1)
                    pe.wait_ge(S["xt_lo"], b + 2)
                    pe.wait_ge(S["out_ready"], b + 1)
                    for k in range(KC):
                        last = mm3(pe, psY(u), XTh[:, u, k], XTl[:, u, k], WT[0][:, k], WT[1][:, k], k == 0, k == KC - 1)
                    last.then_inc(S["y_psum"], 1)

                pe.sem_inc(S["xt_lo"], 1)
                pe.sem_inc(S["out_ready"], 2)
                turn(0, 0)
                rows_loop(body)(pe)

            @block.scalar
            def _(act):
                def body(act, b, u, more):
                    act.wait_ge(S["xt_psum"], b + 1)
                    act.wait_ge(S["out_ready"], b + 1)
                    act.activation(XTh[:, u], psA(u).rearrange("p (k n) -> p k n", k=KC), ACT.Copy).then_inc(S["xt_hi"], 1)

                rows_loop(body)(act)

            @block.vector
            def _(dve):
                dve.tensor_scalar(rstd[:], mv[:, :, 1:2], EPS, None, ALU.add).then_inc(S["eps_added"], 1)

                def split(b, u):
                    dve.tensor_scalar(xh[:, u], X[:, b], mv[:, b, 0:1], rstd[:, b], ALU.subtract, ALU.mult)\
                       .then_inc(S["xh_ready"], 1)
                    dve.wait_ge(S["xt_hi"], b + 1)
                    dve.tensor_tensor(XTl[:, u], psA(u).rearrange("p (k n) -> p k n", k=KC), XTh[:, u].bitcast(F32),
                                      ALU.subtract).then_inc(S["xt_lo"], 1)

                def body(dve, b, u, more):
                    if more:
                        split(b + 1, 1 - u)
                    dve.wait_ge(S["y_psum"], b + 1)
                    dve.wait_ge(S["biased"], b + 1)
                    dve.tensor_tensor(X[:, b], psY(u), X[:, b], ALU.add).then_inc(S["out_ready"], 1)

                dve.wait_ge(S["rstd_ready"], 1)
                split(0, 0)
                rows_loop(body)(dve)

            @block.sync
            def _(sp):
                def body(sp, b, u, more):
                    sp.wait_ge(S["out_ready"], b + 3)
                    sp.dma_start(out[:, b], X[:, b]).then_inc(S["stored"], 16)

                rows_loop(body)(sp)
                sp.wait_ge(S["stored"], 16 * B)


_INS = ["x", "ctx_4096", "L0_xattn_Wq", "L0_xattn_Wk", "L0_xattn_Wv", "L0_xattn_Wo",
        "L0_ffn_w_gate", "L0_ffn_w_up", "L0_ffn_w_down", "L0_ffn_ri_in", "L1_ffn_bias"]
STOP = 4


def kernel(**inputs):
    import concourse.bacc as bacc
    from concourse.bass_utils import run_bass_kernel_spmd as run

    nc = bacc.Bacc("TRN2", target_bir_lowering=False, num_devices=1)
    arrays, t = {}, {}
    ri_in, ri_mid = np.asarray(inputs["L0_ffn_ri_in"]), np.asarray(inputs["L0_ffn_ri_mid"])
    full = I0 // P * P
    inputs = {**inputs, "ri_in_columns": ri_in.reshape(KC, P).T, "ri_mid_columns": ri_mid[:full].reshape(-1, P).T,
              "ri_mid_rest": ri_mid[full:].reshape(-1, 1)}
    get = lambda name: np.asarray(inputs[name])
    inputs["Wq1"] = get("L1_xattn_Wq").reshape(KC, P, G1, W1).transpose(2, 1, 0, 3)
    inputs["Wk1"] = get("L1_xattn_Wk").reshape(KC, P, G1, E1).transpose(2, 1, 0, 3)
    inputs["Wv1"] = get("L1_xattn_Wv").reshape(KC, P, G1, E1).transpose(2, 1, 0, 3)
    inputs["Wo1"] = get("L1_xattn_Wo").reshape(G1, J1, P, D).transpose(0, 2, 1, 3)
    inputs["rope"] = rope_tables()
    inputs["mask"] = get("mask_1x1xSxS2_bk0").reshape(P, P)
    inputs["packed"] = get("L1_ffn_weight_packed").reshape(D // P, P, D // 2).transpose(1, 0, 2)
    inputs["scale"] = get("L1_ffn_weight_scale").reshape(D // P, P, -1).transpose(1, 0, 2)
    inputs["var_mask"] = get("L1_ffn_weight_var_mask").reshape(D // P, P, -1).transpose(1, 0, 2)
    made = ["ri_in_columns", "ri_mid_columns", "ri_mid_rest", "Wq1", "Wk1", "Wv1", "Wo1", "rope", "mask", "packed",
            "scale", "var_mask"]
    for name in _INS + made:
        a = np.asarray(inputs[name])
        if name == "L0_xattn_Wq":
            a = a.reshape(D, PAIRS, 2, J0, E0).transpose(0, 1, 3, 2, 4).reshape(D, D)
        if name == "L0_ffn_w_down":
            a = a.T
        a = np.ascontiguousarray(a)
        arrays["in_" + name] = a
        t[name] = nc.dram_tensor("in_" + name, a.shape, mybir.dt.from_np(a.dtype), kind="ExternalInput").ap()
    t["out"] = nc.dram_tensor("out_x", (B, P, D), F32, kind="ExternalOutput").ap()
    program(nc, t, STOP)
    return run(nc, [arrays], core_ids=[0]).results[0]["out_x"]
```

```python
from contextlib import ExitStack

import numpy as np

import concourse.bass as bass
from concourse import mybir

F32 = mybir.dt.float32
F32R = mybir.dt.float32r
I32 = mybir.dt.int32
ALU = mybir.AluOpType
ACT = mybir.ActivationFunctionType
AX = mybir.AxisListType

P = 128
B = 8
D = 512
KC = D // P
EPS = 1e-5
H0, G0, E0 = 32, 8, 16
J0 = H0 // G0
PAIRS = G0 // 2
STACK = 4 * E0
VC = E0 + 1
SLOT = 32


def mm3(pe, out, ah, al, bh, bl, start, stop):
    pe.matmul(out, ah, bh, start=start, stop=False)
    pe.matmul(out, ah, bl, start=False, stop=False)
    return pe.matmul(out, al, bh, start=False, stop=stop)


def program(nc, t, stop_after):
    with ExitStack() as whole:
        held = []

        def sem(name):
            held.append(nc.alloc_semaphore(name))
            return held[-1]

        def release():
            nc.clear_and_free_semaphores(held)
            held.clear()
            nc.all_engine_barrier()

        def sb_in(stack):
            return lambda name, shape, dt=F32: stack.enter_context(nc.sbuf_tensor(name, shape, dt))

        keep = sb_in(whole)
        scratch = {n: nc.dram_tensor("w_" + n, s, F32, kind="Internal").ap()
                   for n, s in (("down", (I0, D)),)}
        ps = whole.enter_context(nc.psum_tensor("ps", [P, 8, 512], F32))
        ident = keep("ident", [P, P])
        X = keep("X", [P, B, D])
        stats = keep("stats", [P, B, 6])
        mv = keep("mv", [P, B, 2])
        rstd = keep("rstd", [P, B, 1])
        minus_half = keep("minus_half", [P, B, 1])
        CTh = keep("CTh", [P, KC, B * P], F32R)
        CTl = keep("CTl", [P, KC, B * P], F32R)

        with ExitStack() as layer0:
            kw = layer0_setup(nc, t, sem, sb_in(layer0), ps, ident, X, stats, mv, rstd, minus_half, CTh, CTl)
            layer0_attention(nc, sem, ps, ident, X, stats, mv, rstd, **kw)
        release()
        if stop_after >= 2:
            layer0_ffn(nc, t, sem, ps, ident, X, stats, mv, rstd, minus_half, scratch)
            release()
        if stop_after >= 3:
            with ExitStack() as attention:
                sb = sb_in(attention)
                tables, bias = sb("tables", [P, 2, J1 + 1, E1]), sb("bias", [P, P])
                XTh, XTl = sb("XTh", [P, B, KC, P], F32R), sb("XTl", [P, B, KC, P], F32R)
                layer1_attention(nc, t, sem, ps, X, stats, mv, rstd, minus_half, ident, CTh, CTl, XTh, XTl, tables, bias)
        if stop_after >= 4:
            return layer1_ffn(nc, t, sem, ps, ident, X, mv, rstd, minus_half)
        if stop_after:
            return finish(nc, t, sem, X)


def finish(nc, t, sem, X):
    stored = sem("stored")
    with nc.Block() as block:
        @block.sync
        def _(sp):
            sp.dma_start(t["out"].rearrange("b p d -> p b d"), X[:]).then_inc(stored, 16)
            sp.wait_ge(stored, 16)


def layer0_setup(nc, t, sem, sb, ps, ident, X, stats, mv, rstd, minus_half, CTh, CTl):
    KT = sb("KT", [P, B, PAIRS, P], F32R)
    V = sb("V", [P, B, G0, VC])
    Wq = [sb(f"Wq{s}", [P, KC, D], F32R) for s in "hl"]
    wo_in = sb("wo_in", [P, KC, D])
    with ExitStack() as here:
        own = sb_in_stack(nc, here)
        ctx_in = own("ctx_in", [P, B, D])
        wq_in = own("wq_in", [P, KC, D])
        wkv_in = own("wkv_in", [P, KC, 2 * P])
        Wkv = [own(f"Wkv{s}", [P, KC, 2 * P], F32R) for s in "hl"]
        KS = own("KS", [P, 2, G0, STACK], F32R)
        ctx_loaded = [sem(f"ctx_loaded{b}") for b in range(B)]
        x_loaded, wkv_loaded, w_loaded = sem("x_loaded"), sem("wkv_loaded"), sem("w_loaded")
        wo_loaded = sem("wo_loaded")
        ident_zero, ident_ready, half_ready = sem("ident_zero"), sem("ident_ready"), sem("half_ready")
        wkv_hi, wkv_lo, w_hi, w_lo = sem("wkv_hi"), sem("wkv_lo"), sem("w_hi"), sem("w_lo")
        ct_psum, ct_hi, ct_lo = sem("ct_psum"), sem("ct_hi"), sem("ct_lo")
        kv_psum, kv_hi, kv_lo, ks_full = sem("kv_psum"), sem("kv_hi"), sem("kv_lo"), sem("ks_full")
        v_ready, v_ones = sem("v_ready"), sem("v_ones")
        kt_psum, kt_ready = sem("kt_psum"), sem("kt_ready")
        stat_ready, mv_ready, rstd_ready = sem("stat_ready"), sem("mv_ready"), sem("rstd_ready")

        tr = lambda b: ps[:, b % 2, :]
        kv = lambda b: ps[:, 2 + b % 2, 0:2 * P]
        kt = lambda b: ps[:, 4 + b % 2, :]

        with nc.Block() as block:
            @block.sync
            def _(sp):
                sp.dma_start(ctx_in[:, 0], t["ctx_4096"][0]).then_inc(ctx_loaded[0], 16)
                sp.dma_start(wkv_in[:, :, 0:P], t["L0_xattn_Wk"].rearrange("(k p) n -> p k n", p=P)).then_inc(wkv_loaded, 16)
                sp.dma_start(wkv_in[:, :, P:2 * P], t["L0_xattn_Wv"].rearrange("(k p) n -> p k n", p=P)).then_inc(wkv_loaded, 16)
                for b in range(1, B):
                    sp.dma_start(ctx_in[:, b], t["ctx_4096"][b]).then_inc(ctx_loaded[b], 16)
                sp.dma_start(X[:], t["x"].rearrange("b p d -> p b d")).then_inc(x_loaded, 16)
                sp.dma_start(wq_in[:], t["L0_xattn_Wq"].rearrange("(k p) n -> p k n", p=P)).then_inc(w_loaded, 16)
                sp.dma_start(wo_in[:], t["L0_xattn_Wo"].rearrange("(k p) n -> p k n", p=P)).then_inc(wo_loaded, 16)
                sp.wait_ge(wo_loaded, 16)

            @block.gpsimd
            def _(pool):
                pool.memset(ident[:], 0.0).then_inc(ident_zero, 1)
                pool.wait_ge(ident_zero, 1)
                pool.affine_select(out=ident[:], in_=ident[:], compare_op=ALU.not_equal, fill=1.0, base=0,
                                   pattern=[[-1, P]], channel_multiplier=1).then_inc(ident_ready, 1)
                pool.memset(minus_half[:], -0.5).then_inc(half_ready, 1)
                pool.memset(V[:, :, :, E0:VC], 1.0).then_inc(v_ones, 1)
                pool.wait_ge(wkv_hi, 1)
                pool.tensor_tensor(Wkv[1][:], wkv_in[:], Wkv[0][:].bitcast(F32), ALU.subtract).then_inc(wkv_lo, 1)
                for b in range(B):
                    pool.wait_ge(kv_hi, b + 1)
                    pool.wait_ge(kv_lo, b + 1)
                    v = KS[:, b % 2].bitcast(F32).rearrange("p g (a c e) -> p g a c e", a=2, c=2)
                    o = KS[:, b % 2].rearrange("p g (a c e) -> p g a c e", a=2, c=2)
                    pool.tensor_copy(o[:, :, :, 1], v[:, :, :, 0]).then_inc(ks_full, 1)
                pool.wait_ge(mv_ready, B)
                pool.wait_ge(half_ready, 1)
                pool.tensor_tensor(rstd[:], rstd[:], minus_half[:], ALU.pow).then_inc(rstd_ready, 1)

            @block.scalar
            def _(act):
                act.wait_ge(wkv_loaded, 32)
                act.activation(Wkv[0][:], wkv_in[:], ACT.Copy).then_inc(wkv_hi, 1)

                def keys(b):
                    act.wait_ge(kv_psum, b + 1)
                    if b >= 2:
                        act.wait_ge(kt_psum, b - 1)
                    act.activation(KS[:, b % 2, :, 0:E0], kv(b)[:, 0:P].rearrange("p (g e) -> p g e", g=G0),
                                   ACT.Copy).then_inc(kv_hi, 1)
                    act.activation(V[:, b, :, 0:E0], kv(b)[:, P:2 * P].rearrange("p (g e) -> p g e", g=G0),
                                   ACT.Copy).then_inc(v_ready, 1)

                def keys_out(b):
                    act.wait_ge(kt_psum, b + 1)
                    act.activation(KT[:, b], kt(b), ACT.Copy).then_inc(kt_ready, 1)

                for b in range(B + 2):
                    if b < B:
                        act.wait_ge(ct_psum, b + 1)
                        act.activation(CTh[:, :, b * P:(b + 1) * P], tr(b).rearrange("p (k n) -> p k n", k=KC),
                                       ACT.Copy).then_inc(ct_hi, 1)
                    if 1 <= b <= B:
                        keys(b - 1)
                    if b >= 2:
                        keys_out(b - 2)
                    k = b - (B + 2 - KC)
                    if k >= 0:
                        act.wait_ge(w_loaded, 16)
                        act.activation(Wq[0][:, k], wq_in[:, k], ACT.Copy).then_inc(w_hi, 1)

            @block.vector
            def _(dve):
                def keys_lo(b):
                    dve.wait_ge(v_ready, b + 1)
                    if b >= 2:
                        dve.wait_ge(kt_psum, b - 1)
                    dve.tensor_tensor(KS[:, b % 2, :, 2 * E0:3 * E0], kv(b)[:, 0:P].rearrange("p (g e) -> p g e", g=G0),
                                      KS[:, b % 2, :, 0:E0].bitcast(F32), ALU.subtract).then_inc(kv_lo, 1)

                for b in range(B + 1):
                    if b < B:
                        dve.wait_ge(ct_hi, b + 1)
                        dve.tensor_tensor(CTl[:, :, b * P:(b + 1) * P], tr(b).rearrange("p (k n) -> p k n", k=KC),
                                          CTh[:, :, b * P:(b + 1) * P].bitcast(F32), ALU.subtract).then_inc(ct_lo, 1)
                    if b >= 1:
                        keys_lo(b - 1)
                    if b >= B // 2:
                        dve.wait_ge(x_loaded, 16)
                        for r in range(2 * (b - B // 2), min(2 * (b - B // 2) + 2, B)):
                            dve.bn_stats(stats[:, r], X[:, r]).then_inc(stat_ready, 1)
                for b in range(B):
                    dve.wait_ge(stat_ready, b + 1)
                    dve.bn_aggr(mv[:, b], stats[:, b]).then_inc(stat_ready, 1)
                dve.wait_ge(stat_ready, 2 * B)
                dve.tensor_scalar(rstd[:], mv[:, :, 1:2], EPS, None, ALU.add).then_inc(mv_ready, B)
                for k in range(KC):
                    dve.wait_ge(w_hi, k + 1)
                    dve.tensor_tensor(Wq[1][:, k], wq_in[:, k], Wq[0][:, k].bitcast(F32), ALU.subtract).then_inc(w_lo, 1)

            @block.tensor
            def _(pe):
                def project(b):
                    pe.wait_ge(ct_hi, b + 1)
                    pe.wait_ge(ct_lo, b + 1)
                    if b >= 2:
                        pe.wait_ge(kv_lo, b - 1)
                        pe.wait_ge(v_ready, b - 1)
                    for k in range(KC):
                        last = mm3(pe, kv(b), CTh[:, k, b * P:(b + 1) * P], CTl[:, k, b * P:(b + 1) * P],
                                   Wkv[0][:, k], Wkv[1][:, k], k == 0, k == KC - 1)
                    last.then_inc(kv_psum, 1)

                def turn_keys(b):
                    pe.wait_ge(ks_full, b + 1)
                    if b >= 2:
                        pe.wait_ge(kt_ready, b - 1)
                    for pr in range(PAIRS):
                        last = pe.transpose(kt(b)[:, pr * P:(pr + 1) * P],
                                            KS[:, b % 2, 2 * pr:2 * pr + 2].bitcast(F32).rearrange("p g c -> p (g c)"),
                                            ident[:])
                    last.then_inc(kt_psum, 1)

                pe.wait_ge(ident_ready, 1)
                for b in range(B + 2):
                    if b < B:
                        pe.wait_ge(ctx_loaded[b], 16)
                        if b >= 2:
                            pe.wait_ge(ct_lo, b - 1)
                        for k in range(KC):
                            last = pe.transpose(tr(b)[:, k * P:(k + 1) * P], ctx_in[:, b, k * P:(k + 1) * P], ident[:])
                        last.then_inc(ct_psum, 1)
                    if b == 0:
                        pe.wait_ge(wkv_lo, 1)
                    if 1 <= b <= B:
                        project(b - 1)
                    if b >= 2:
                        turn_keys(b - 2)
    return dict(KT=KT, V=V, Wq=Wq, wo_in=wo_in, sb=sb)


def sb_in_stack(nc, stack):
    return lambda name, shape, dt=F32: stack.enter_context(nc.sbuf_tensor(name, shape, dt))


def layer0_attention(nc, sem, ps, ident, X, stats, mv, rstd, KT, V, Wq, wo_in, sb):
    Wo = [sb(f"Wo{s}", [P, KC, D], F32R) for s in "hl"]
    wo_hi, wo_lo = sem("a_wo_hi"), sem("a_wo_lo")
    xh = sb("xh", [P, D])
    XTh, XTl = sb("XTh0", [P, KC, P], F32R), sb("XTl0", [P, KC, P], F32R)
    QS = sb("QS", [P, H0, STACK], F32R)
    QT = sb("QT", [P, 2, PAIRS, J0 * P], F32R)
    KTb = sb("KTb", [P, 2, PAIRS, P], F32R)
    Vb = sb("Vb", [P, 2, 2, G0 // 2 * (P + SLOT)])
    OV = sb("OV", [P, J0 * P])
    mx = sb("mx", [P, 2, J0])
    PR = sb("PR", [P, 4, J0 * P])
    PT = sb("PT", [P, 2, J0 * P])
    rden = sb("rden", [P, J0, G0 // 2])
    O = sb("O", [P, 2, D])
    OTh, OTl = sb("OTh", [P, KC, P], F32R), sb("OTl", [P, KC, P], F32R)
    zero, zero_ready = sb("zero", [P, 1]), sem("a_zero_ready")

    xh_ready, xt_psum, xt_hi, xt_lo = sem("a_xh_ready"), sem("a_xt_psum"), sem("a_xt_hi"), sem("a_xt_lo")
    q_psum, qs_hi, qs_lo, qs_full = sem("a_q_psum"), sem("a_qs_hi"), sem("a_qs_lo"), sem("a_qs_full")
    qt_psum, qt_ready, kv_staged = sem("a_qt_psum"), sem("a_qt_ready"), sem("a_kv_staged")
    s_psum, mx_ready, s_shifted = sem("a_s_psum"), sem("a_mx_ready"), sem("a_s_shifted")
    pt_psum, pt_ready, pv_done = sem("a_pt_psum"), sem("a_pt_ready"), sem("a_pv_done")
    vb_zero, ov_taken, ov_turned = sem("a_vb_zero"), sem("a_ov_taken"), sem("a_ov_turned")
    rden_ready, o_ready = sem("a_rden_ready"), sem("a_o_ready")
    ot_psum, ot_hi, ot_lo = sem("a_ot_psum"), sem("a_ot_hi"), sem("a_ot_lo")
    y_psum, x_added, stat_done = sem("a_y_psum"), sem("a_x_added"), sem("a_stat_done")

    psA = ps[:, 0, :]
    psA3 = psA.rearrange("p (k n) -> p k n", k=KC)
    psB = ps[:, 1, :]
    psB3 = psB.rearrange("p (h e) -> p h e", h=H0)
    psS = lambda n: ps[:, 2 + n % 2, :]
    psT = lambda n: ps[:, 4 + n % 2, :]
    psV = ps[:, 6, :]
    psO = ps[:, 7, :]
    heads = psO.rearrange("p (j g e) -> p j g e", j=J0, e=SLOT)

    def behind(b, u, g, by):
        return (b, u, g - by, b * G0 + g - by) if g >= by else (b - 1, 1 - u, g - by + G0, b * G0 + g - by)

    def rows(body):
        def run(eng):
            body(eng, 0, 0, False, True, True)
            with eng.Fori(0, B // 2 - 1) as i:
                for u in (1, 0):
                    body(eng, i * 2 + (2 - u), u, True, True, True)
            body(eng, B - 1, 1, True, True, False)
            body(eng, B, 0, True, False, False)
        return run

    with nc.Block() as block:
        @block.tensor
        def _(pe):
            def turn_x(b):
                pe.wait_ge(xh_ready, b + 1)
                need(pe, qt_ready, b * PAIRS)
                for k in range(KC):
                    last = pe.transpose(psA[:, k * P:(k + 1) * P], xh[:, k * P:(k + 1) * P], ident[:])
                last.then_inc(xt_psum, 1)

            def project_q(b, ks):
                if ks[0] == 0:
                    pe.wait_ge(xt_hi, b + 1)
                    pe.wait_ge(xt_lo, b + 1)
                    if not isinstance(b, int) or b >= 3:
                        pe.wait_ge(x_added, b - 2)
                for k in ks:
                    last = mm3(pe, psB, XTh[:, k], XTl[:, k], Wq[0][:, k], Wq[1][:, k], k == 0, k == KC - 1)
                if k == KC - 1:
                    last.then_inc(q_psum, 1)

            def turn_q(b, pr):
                pe.wait_ge(qs_full, b + 1)
                need(pe, qt_ready, b * PAIRS + pr)
                for j in range(J0):
                    src = QS[:, 2 * (pr * J0 + j):2 * (pr * J0 + j + 1)].bitcast(F32).rearrange("p h c -> p (h c)")
                    last = pe.transpose(psA[:, j * P:(j + 1) * P], src, ident[:])
                last.then_inc(qt_psum, 1)

            def scores(b, u, g):
                n = b * G0 + g
                pe.wait_ge(qt_ready, b * PAIRS + g // 2 + 1)
                if g == 0:
                    pe.wait_ge(kv_staged, 2 * (b + 1))
                need(pe, s_shifted, n - 1)
                r = slice((g % 2) * STACK, (g % 2 + 1) * STACK)
                for j in range(J0):
                    last = pe.matmul(psS(g)[:, j * P:(j + 1) * P], QT[r, u, g // 2, j * P:(j + 1) * P],
                                     KTb[r, u, g // 2], start=True, stop=True)
                last.then_inc(s_psum, 1)

            def turn(b, u, g, n):
                pe.wait_ge(s_shifted, n + 1)
                need(pe, pt_ready, n - 1)
                for j in range(J0):
                    last = pe.transpose(psT(g)[:, j * P:(j + 1) * P], PR[:, g % 4, j * P:(j + 1) * P], ident[:])
                last.then_inc(pt_psum, 1)

            def weigh(b, u, g, n):
                pe.wait_ge(pt_ready, n + 1)
                if g % 4 == 0:
                    need(pe, ov_taken, 2 * b + g // 4)
                pe.matmul(psV, Vb[:, u, g // 4, g % 4 * P:(g % 4 + 1) * P], PT[:, g % 2], start=g % 4 == 0,
                          stop=g % 4 == 3).then_inc(pv_done, 1)

            def turn_back(b, half):
                m = 2 * b + half
                pe.wait_ge(ov_taken, m + 1)
                need(pe, o_ready, m)
                for j in range(J0):
                    last = pe.transpose(psO[:, j * P:(j + 1) * P], OV[:, j * P:(j + 1) * P], ident[:])
                last.then_inc(ov_turned, 1)

            def turn_o(b, u, more):
                pe.wait_ge(o_ready, 2 * b + 2)
                if not more:
                    pe.wait_ge(qt_ready, B * PAIRS)
                for k in range(KC):
                    last = pe.transpose(psA[:, k * P:(k + 1) * P], O[:, u, k * P:(k + 1) * P], ident[:])
                last.then_inc(ot_psum, 1)

            def project_o(b, ks):
                pe.wait_ge(ot_hi, b + 1)
                pe.wait_ge(ot_lo, b + 1)
                pe.wait_ge(wo_lo, KC)
                for k in ks:
                    last = mm3(pe, psB, OTh[:, k], OTl[:, k], Wo[0][:, k], Wo[1][:, k], k == 0, k == KC - 1)
                if k == KC - 1:
                    last.then_inc(y_psum, 1)

            def body(pe, b, u, before, here, more):
                for g in range(G0):
                    if here:
                        scores(b, u, g)
                    if (before or g >= 2) and (here or g < 2):
                        turn(*behind(b, u, g, 2))
                    if (before or g >= 3) and (here or g < 3):
                        weigh(*behind(b, u, g, 3))
                    if g == 3 and before:
                        turn_back(b - 1, 1)
                    if g == 7 and here:
                        turn_back(b, 0)
                    if here and g in (0, 1):
                        turn_q(b, 2 + g)
                    if g == 2 and more:
                        turn_x(b + 1)
                    if g == 3 and more:
                        project_q(b + 1, [0, 1])
                    if g == 4 and before:
                        turn_o(b - 1, 1 - u, more)
                    if g == 4 and more:
                        project_q(b + 1, [2, 3])
                    if g in (6, 7):
                        if before:
                            if g == 6 and more:
                                pe.wait_ge(qs_lo, b + 2)
                            project_o(b - 1, [2 * (g - 6), 2 * (g - 6) + 1])
                        if more:
                            turn_q(b + 1, g - 6)

            turn_x(0)
            project_q(0, list(range(KC)))
            turn_q(0, 0)
            turn_q(0, 1)
            rows(body)(pe)

        @block.scalar
        def _(act):
            def x_hi(b):
                act.wait_ge(xt_psum, b + 1)
                act.activation(XTh[:], psA3, ACT.Copy).then_inc(xt_hi, 1)

            def q_hi(b):
                act.wait_ge(q_psum, b + 1)
                act.activation(QS[:, :, 0:E0], psB3, ACT.Copy).then_inc(qs_hi, 1)

            def q_turned(b, u, pr):
                act.wait_ge(qt_psum, b * PAIRS + pr + 1)
                act.activation(QT[:, u, pr], psA, ACT.Copy).then_inc(qt_ready, 1)

            def exps(b, u, g, n):
                act.wait_ge(pt_psum, n + 1)
                need(act, pv_done, n - 1)
                act.activation(PT[:, g % 2], psT(g), ACT.Exp, scale=float(E0) ** -0.5).then_inc(pt_ready, 1)

            def take(b, half):
                m = 2 * b + half
                act.wait_ge(pv_done, 4 * m + 4)
                need(act, ov_turned, m)
                act.activation(OV[:], psV, ACT.Copy).then_inc(ov_taken, 1)

            def body(act, b, u, before, here, more):
                for g in range(G0):
                    if (before or g >= 2) and (here or g < 2):
                        exps(*behind(b, u, g, 2))
                    if g == 2 and before:
                        take(b - 1, 1)
                    if g == 6 and here:
                        take(b, 0)
                    if here and g in (0, 1):
                        q_turned(b, u, 2 + g)
                    if g == 2 and more:
                        x_hi(b + 1)
                    if g == 4 and before:
                        act.wait_ge(ot_psum, b)
                        act.activation(OTh[:], psA3, ACT.Copy).then_inc(ot_hi, 1)
                    if g == 4 and more:
                        q_hi(b + 1)
                    if g in (6, 7) and more:
                        q_turned(b + 1, 1 - u, g - 6)

            x_hi(0)
            for k in range(KC):
                act.activation(Wo[0][:, k], wo_in[:, k], ACT.Copy).then_inc(wo_hi, 1)
            q_hi(0)
            q_turned(0, 0, 0)
            q_turned(0, 0, 1)
            rows(body)(act)

        @block.gpsimd
        def _(pool):
            def stage(b, u):
                pool.tensor_copy(KTb[:, u], KT[:, b].bitcast(F32)).then_inc(kv_staged, 1)
                if isinstance(b, int) and b == 0:
                    pool.wait_ge(vb_zero, 2)
                pool.tensor_copy(Vb[:, u].rearrange("p a (g c) -> p a g c", c=P + SLOT)[:, :, :, 0:VC],
                                 V[:, b].rearrange("p (a g) c -> p a g c", a=2)).then_inc(kv_staged, 1)

            def dup(b):
                pool.wait_ge(qs_hi, b + 1)
                pool.wait_ge(qs_lo, b + 1)
                pool.tensor_tensor(QS[:, :, 2 * E0:4 * E0], QS[:, :, 0:2 * E0].bitcast(F32),
                                   bcast(bcast(zero[:, 0], H0), 2 * E0), ALU.add).then_inc(qs_full, 1)

            def body(pool, b, u, before, here, more):
                if more:
                    need(pool, pv_done, b * G0)
                    stage(b + 1, 1 - u)
                    dup(b + 1)

            pool.memset(zero[:], 0.0).then_inc(zero_ready, 1)
            pool.wait_ge(zero_ready, 1)
            stage(0, 0)
            dup(0)
            for k in range(KC):
                pool.wait_ge(wo_hi, k + 1)
                pool.tensor_tensor(Wo[1][:, k], wo_in[:, k], Wo[0][:, k].bitcast(F32), ALU.subtract).then_inc(wo_lo, 1)
            rows(body)(pool)

        @block.vector
        def _(dve):
            def normalize(b):
                need(dve, xt_psum, b)
                dve.tensor_scalar(xh[:], X[:, b], mv[:, b, 0:1], rstd[:, b],
                                  ALU.subtract, ALU.mult).then_inc(xh_ready, 1)

            def x_lo(b):
                dve.wait_ge(xt_hi, b + 1)
                dve.tensor_tensor(XTl[:], psA3, XTh[:].bitcast(F32), ALU.subtract).then_inc(xt_lo, 1)

            def q_lo(b):
                dve.wait_ge(qs_hi, b + 1)
                dve.tensor_tensor(QS[:, :, E0:2 * E0], psB3, QS[:, :, 0:E0].bitcast(F32), ALU.subtract)\
                   .then_inc(qs_lo, 1)

            def shift(b, g):
                n = b * G0 + g
                dve.wait_ge(s_psum, n + 1)
                s = psS(g).rearrange("p (j k) -> p j k", j=J0)
                dve.tensor_reduce(mx[:, g % 2], s, AX.X, ALU.max).then_inc(mx_ready, 1)
                dve.wait_ge(mx_ready, n + 1)
                need(dve, pt_psum, n - 3)
                dve.tensor_tensor(PR[:, g % 4].rearrange("p (j k) -> p j k", j=J0), s, bcast(mx[:, g % 2], P),
                                  ALU.subtract).then_inc(s_shifted, 1)

            def norm(b, u, half):
                n = 2 * b + half
                dve.wait_ge(ov_turned, n + 1)
                dve.reciprocal(rden[:], heads[:, :, :, E0]).then_inc(rden_ready, 1)
                dve.wait_ge(rden_ready, n + 1)
                dve.tensor_tensor(O[:, u, half * (D // 2):(half + 1) * (D // 2)]
                                  .rearrange("p (g j e) -> p j g e", j=J0, e=E0),
                                  heads[:, :, :, 0:E0], bcast(rden[:], E0), ALU.mult).then_inc(o_ready, 1)

            def body(dve, b, u, before, here, more):
                for g in range(G0):
                    if here:
                        shift(b, g)
                    if g == 1 and more:
                        normalize(b + 1)
                    if g == 2 and more:
                        x_lo(b + 1)
                    if g == 3 and before:
                        norm(b - 1, 1 - u, 1)
                    if g == 5 and more:
                        q_lo(b + 1)
                    if g == 5 and before:
                        dve.wait_ge(ot_hi, b)
                        dve.tensor_tensor(OTl[:], psA3, OTh[:].bitcast(F32), ALU.subtract).then_inc(ot_lo, 1)
                    if g == 7 and here:
                        norm(b, u, 0)
                    if g == 7 and before:
                        dve.wait_ge(y_psum, b)
                        dve.tensor_tensor(X[:, b - 1], psB, X[:, b - 1], ALU.add).then_inc(x_added, 1)
                        dve.wait_ge(x_added, b)
                        dve.bn_stats(stats[:, b - 1], X[:, b - 1]).then_inc(stat_done, 1)

            normalize(0)
            dve.memset(Vb[:, 0], 0.0).then_inc(vb_zero, 1)
            x_lo(0)
            dve.memset(Vb[:, 1], 0.0).then_inc(vb_zero, 1)
            q_lo(0)
            rows(body)(dve)
            for b in range(B):
                dve.wait_ge(stat_done, b + 1)
                dve.bn_aggr(mv[:, b], stats[:, b]).then_inc(stat_done, 1)


def bcast(ap, n):
    return ap.unsqueeze(len(ap.shape)).broadcast_to([*ap.shape, n])

I0 = 1376
IT = [(r, min(P, I0 - r)) for r in range(0, I0, P)]
IC = [(c, min(512, I0 - c)) for c in range(0, I0, 512)]
BLK = 16
SELECT = 128
FP8_MAX = 448.0
INT4_MAX = 7.0
LEAST = 1e-8
ROUND_INT = 1.5 * 2.0 ** 23
EXPONENT = 0x7F800000
FP8_LEAST_NORMAL = 2.0 ** -6
FP8_STEP = 1.5 * 2.0 ** (23 - 3)


def quantize_fp8(dve, link, V, E, bits):
    e = E.bitcast(I32)
    link(dve.tensor_scalar(e, V.bitcast(I32), bits, None, ALU.bitwise_and))
    link(dve.tensor_scalar(E, E, FP8_LEAST_NORMAL, FP8_STEP, ALU.max, ALU.mult))
    link(dve.tensor_tensor(V, V, E, ALU.add))
    link(dve.tensor_tensor(V, V, E, ALU.subtract))


class Chain:
    def __init__(self, eng, sem):
        self.eng, self.sem, self.base, self.n, self.per = eng, sem, 0, 0, None

    def row(self, b):
        if self.n and self.per is None:
            self.per = self.n
        if self.per is not None:
            assert self.n == self.per
            self.base = b * self.per
        self.n = 0

    def __call__(self, ins):
        self.n += 1
        ins.then_inc(self.sem, 1)
        self.eng.wait_ge(self.sem, self.base + self.n)


def blocks(ap):
    return ap.rearrange("p (b e) -> p b e", e=BLK)


def quantize_rest(dve, link, src, sc, V, E, R, A, bm, g_inv):
    link(dve.tensor_tensor(blocks(A), blocks(V), bcast(sc, BLK), ALU.mult))
    link(dve.scalar_tensor_tensor(R, src, g_inv, A, ALU.mult, ALU.subtract))
    link(dve.tensor_reduce(bm[:, 0], blocks(R), AX.X, ALU.max, apply_absolute_value=True))
    link(dve.tensor_scalar(bm[:, 1], bm[:, 0], 1.0 / FP8_MAX, LEAST, ALU.mult, ALU.max))
    link(dve.reciprocal(bm[:, 2], bm[:, 1]))
    link(dve.tensor_tensor(blocks(V), blocks(R), bcast(bm[:, 2], BLK), ALU.mult))
    quantize_fp8(dve, link, V, E, EXPONENT)
    link(dve.tensor_tensor(blocks(V), blocks(V), bcast(bm[:, 1], BLK), ALU.mult))
    return dve.tensor_tensor(A, A, V, ALU.add)


def quantize_rows(dve, link, src, inv, sc, V, E, R, A, bm, g_inv, width):
    n = width - SELECT
    link(dve.tensor_tensor(blocks(V), blocks(src), bcast(inv, BLK), ALU.mult))
    quantize_fp8(dve, link, V, E, EXPONENT)
    link(dve.tensor_tensor(blocks(A[:, 0:n]), blocks(V[:, 0:n]), bcast(sc[:, 0:n // BLK], BLK), ALU.mult))
    return quantize_rest(dve, link, src[:, n:width], sc[:, n // BLK:], V[:, n:width], E[:, n:width], R, A[:, n:width],
                         bm, g_inv)


def rows_loop(body, last=1):
    def run(eng):
        body(eng, 0, 0, last)
        with eng.Fori(0, (B - 1 - last) // 2) as i:
            for u in (1, 0):
                body(eng, i * 2 + (2 - u), u, last)
        for b in range(B - last, B):
            body(eng, b, b % 2, B - 1 - b)
    return run


def need(eng, sem, value):
    if not isinstance(value, int) or value > 0:
        eng.wait_ge(sem, value)


def ffn0_prepare_weights(nc, t, sem, ps, ident, scratch, work, pick, W):
    with ExitStack() as here:
        sb = sb_in_stack(nc, here)
        NR, NV, NQ, NS = 3, 3, 2, 2
        cut = lambda at, n: work[:, at * 512:(at + n) * 512].rearrange("p (i n) -> p i n", n=512)
        R, V, Q = cut(0, NR), cut(NR, NV), cut(NR + NV, NQ)
        out = cut(NR + NV + NQ, NS)
        Gd = cut(NR + NV + NQ + NS, len(IT))
        idx = sb("idx_mid", [P, len(IT)], I32)
        ri, rif, pid, pidf = sb("ri", [P, D], I32), sb("rif", [P, D]), sb("pid", [P, KC], I32), sb("pidf", [P, KC])
        wh, wl = sb("p_wh", [P, 2, KC, P], F32R), sb("p_wl", [P, 2, KC, P], F32R)
        NB = 512 // BLK
        bm, sc, rs = (sb("p_" + n, [P, NV, NB]) for n in ("bm", "sc", "rs"))
        names = ("idx_loaded ri_loaded pid_ready pick_ready down_gathered in_psum in_hi in_lo w_psum bm_ready "
                 "sc_ready rs_ready scaled shifted rounded clipped w_ready out_psum out_hi out_lo out_rest as_float")
        S = {n: sem("p_" + n) for n in names.split()}
        gathered, stored = [sem(f"p_gathered{q}") for q in range(NR)], [sem(f"p_stored{q}") for q in range(NS)]

        ups = [("up", m, r, rows) for m in range(2) for r, rows in IT]
        units = ups + [("down", r, c, n) for r in range(0, D, P) for c, n in IC]
        UP = len(ups)
        rows_of = lambda n: units[n][3] if n < UP else P
        width_of = lambda n: D if n < UP else units[n][3]
        slices = lambda n: [(m - units[n][2], m // P, w) for m, w in IT if units[n][2] <= m < units[n][2] + units[n][3]]
        bank_in = lambda n: ps[:, n % 2, :].rearrange("p (k n) -> p k n", k=KC)
        bank_w = lambda n: ps[:, 2 + n % 3, :]
        bank_out = lambda n: ps[:, 5 + n % 3, :].rearrange("p (k n) -> p k n", k=KC)
        BACK = 4
        LAST = len(units) + BACK

        with nc.Block() as block:
            @block.sync
            def _(sp):
                full = I0 // P
                sp.dma_start(idx[:, 0:full], t["ri_mid_columns"]).then_inc(S["idx_loaded"], 16)
                sp.dma_start(idx[0:I0 - full * P, full:full + 1], t["ri_mid_rest"]).then_inc(S["idx_loaded"], 16)
                sp.dma_start(ri[:], t["L0_ffn_ri_in"].partition_broadcast(P)).then_inc(S["ri_loaded"], 16)
                count = [0] * NS
                for n in range(UP, len(units)):
                    _, r, c, width = units[n]
                    whole = width // P
                    sp.wait_ge(S["out_hi"], n + 1)
                    sp.dma_start(scratch["down"][c:c + whole * P, r:r + P].rearrange("(i p) d -> p i d", p=P),
                                 out[:, n % NS, 0:whole * P].rearrange("p (i d) -> p i d", d=P))\
                        .then_inc(stored[n % NS], 16)
                    rest = width - whole * P
                    if rest:
                        sp.dma_start(scratch["down"][c + whole * P:c + width, r:r + P],
                                     out[0:rest, n % NS, whole * P:(whole + 1) * P]).then_inc(stored[n % NS], 16)
                    count[n % NS] += 2 if rest else 1
                for q in range(NS):
                    sp.wait_ge(stored[q], 16 * count[q])

            @block.gpsimd
            def _(pool):
                pool.iota(pid[:], [[P, KC]], base=0, channel_multiplier=1).then_inc(S["pid_ready"], 1)
                pool.wait_ge(S["idx_loaded"], 32)

                def gather_rows(n):
                    _, m, r, rows = units[n]
                    if n >= NR:
                        pool.wait_ge(S["in_psum"], n - NR + 1)
                    pool.indirect_dma_start(R[0:rows, n % NR], None, t[("L0_ffn_w_gate", "L0_ffn_w_up")[m]],
                                            bass.IndirectOffsetOnAxis(ap=idx[0:rows, r // P:r // P + 1], axis=0))\
                        .then_inc(gathered[n % NR], 16)

                def gather_down(m):
                    w = IT[m][1]
                    pool.indirect_dma_start(Gd[0:w, m], None, t["L0_ffn_w_down"],
                                            bass.IndirectOffsetOnAxis(ap=idx[0:w, m:m + 1], axis=0))\
                        .then_inc(S["down_gathered"], 16)

                def scale(n):
                    rows, w = rows_of(n), width_of(n)
                    pool.wait_ge(S["clipped"], n + 1)
                    if n >= NQ:
                        pool.wait_ge(S["out_psum"], n - NQ + 1)
                    pool.tensor_tensor(blocks(Q[0:rows, n % NQ, 0:w]), blocks(V[0:rows, n % NV, 0:w]),
                                       bcast(sc[0:rows, n % NV, 0:w // BLK], BLK), ALU.mult).then_inc(S["w_ready"], 1)

                for n in range(2):
                    gather_rows(n)
                for s in range(LAST):
                    if s + 2 < UP:
                        gather_rows(s + 2)
                    if 2 <= s < 2 + len(IT):
                        gather_down(s - 2)
                    if 3 <= s < len(units) + 3:
                        scale(s - 3)

            @block.tensor
            def _(pe):
                def turn_in(n):
                    rows = rows_of(n)
                    pe.wait_ge(gathered[n % NR], 16 * (n // NR + 1))
                    if n >= 2:
                        pe.wait_ge(S["in_lo"], n - 1)
                    for k in range(KC):
                        last = pe.transpose(bank_in(n)[:, k, 0:rows], R[0:rows, n % NR, k * P:(k + 1) * P],
                                            ident[0:rows, 0:rows])
                    last.then_inc(S["in_psum"], 1)

                def reorder(n):
                    rows = rows_of(n)
                    if n >= 3:
                        pe.wait_ge(S["scaled"], n - 2)
                    if n < UP:
                        pe.wait_ge(S["in_hi"], n + 1)
                        pe.wait_ge(S["in_lo"], n + 1)
                        for k in range(KC):
                            pe.matmul(bank_w(n)[0:rows], wh[:, n % 2, k, 0:rows], pick[:, k], start=k == 0, stop=False)
                            last = pe.matmul(bank_w(n)[0:rows], wl[:, n % 2, k, 0:rows], pick[:, k], start=False,
                                             stop=k == KC - 1)
                    else:
                        if n == UP:
                            pe.wait_ge(S["down_gathered"], 16 * len(IT))
                        for at, m, w in slices(n):
                            last = pe.transpose(bank_w(n)[:, at:at + w], Gd[0:w, m, units[n][1]:units[n][1] + P],
                                                ident[0:w, 0:w])
                    last.then_inc(S["w_psum"], 1)

                def turn_out(n):
                    rows = rows_of(n)
                    pe.wait_ge(S["w_ready"], n + 1)
                    if n >= 3:
                        pe.wait_ge(S["out_hi"], n - 2)
                        if n - 3 < UP:
                            pe.wait_ge(S["out_lo"], n - 2)
                    if n < UP:
                        for k in range(KC):
                            last = pe.transpose(bank_out(n)[:, k, 0:rows], Q[0:rows, n % NQ, k * P:(k + 1) * P],
                                                ident[0:rows, 0:rows])
                    else:
                        for i, (at, _, w) in enumerate(slices(n)):
                            last = pe.transpose(bank_out(n)[0:w, i], Q[:, n % NQ, at:at + w], ident[:])
                    last.then_inc(S["out_psum"], 1)

                for s in range(LAST):
                    if s < UP:
                        turn_in(s)
                    if s == 1:
                        pe.wait_ge(S["pick_ready"], KC)
                    if 1 <= s <= len(units):
                        reorder(s - 1)
                    if s >= BACK:
                        turn_out(s - BACK)

            @block.scalar
            def _(act):
                def split_hi(n):
                    rows = rows_of(n)
                    act.wait_ge(S["in_psum"], n + 1)
                    if n >= 2:
                        act.wait_ge(S["w_psum"], n - 1)
                    act.activation(wh[:, n % 2, :, 0:rows], bank_in(n)[:, :, 0:rows], ACT.Copy).then_inc(S["in_hi"], 1)

                def round_(n):
                    v = V[0:rows_of(n), n % NV, 0:width_of(n)]
                    act.wait_ge(S["scaled"], n + 1)
                    act.activation(v, v, ACT.Copy, bias=ROUND_INT).then_inc(S["shifted"], 1)
                    act.wait_ge(S["shifted"], n + 1)
                    act.activation(v, v, ACT.Copy, bias=-ROUND_INT).then_inc(S["rounded"], 1)

                def take(n):
                    act.wait_ge(S["out_psum"], n + 1)
                    if n < UP:
                        _, m, r, rows = units[n]
                        act.activation(W[m][0][:, :, r:r + rows], bank_out(n)[:, :, 0:rows], ACT.Copy)\
                            .then_inc(S["out_hi"], 1)
                        return
                    whole, rest = width_of(n) // P, width_of(n) % P
                    if n - NS >= UP:
                        act.wait_ge(stored[n % NS], 16 * sum(2 if width_of(i) % P else 1
                                                             for i in range(UP, n) if i % NS == n % NS))
                    if rest:
                        act.activation(out[0:rest, n % NS, whole * P:(whole + 1) * P], bank_out(n)[0:rest, whole],
                                       ACT.Copy).then_inc(S["out_rest"], 1)
                    act.activation(out[:, n % NS, 0:whole * P], bank_out(n)[:, 0:whole].rearrange("p k n -> p (k n)"),
                                   ACT.Copy).then_inc(S["out_hi"], 1)

                for s in range(LAST):
                    if s < UP:
                        split_hi(s)
                    if s >= BACK:
                        take(s - BACK)
                    if 2 <= s < len(units) + 2:
                        round_(s - 2)

            @block.vector
            def _(dve):
                dve.wait_ge(S["ri_loaded"], 16)
                dve.wait_ge(S["pid_ready"], 1)
                dve.tensor_copy(rif[:], ri[:]).then_inc(S["as_float"], 1)
                dve.tensor_copy(pidf[:], pid[:]).then_inc(S["as_float"], 1)
                dve.wait_ge(S["as_float"], 2)
                for k in range(KC):
                    dve.tensor_scalar(pick[:, k], rif[:], pidf[:, k:k + 1], None, ALU.is_equal).then_inc(S["pick_ready"], 1)

                def split_lo(n):
                    rows = rows_of(n)
                    dve.wait_ge(S["in_hi"], n + 1)
                    dve.tensor_tensor(wl[:, n % 2, :, 0:rows], bank_in(n)[:, :, 0:rows],
                                      wh[:, n % 2, :, 0:rows].bitcast(F32), ALU.subtract).then_inc(S["in_lo"], 1)

                def to_scale(n):
                    rows, w = rows_of(n), width_of(n)
                    at = slice(0, w // BLK)
                    m, s, r = (x[0:rows, n % NV, at] for x in (bm, sc, rs))
                    dve.wait_ge(S["w_psum"], n + 1)
                    dve.tensor_reduce(m, blocks(bank_w(n)[0:rows, 0:w]), AX.X, ALU.max, apply_absolute_value=True)\
                       .then_inc(S["bm_ready"], 1)
                    yield
                    dve.wait_ge(S["bm_ready"], n + 1)
                    if n >= NV:
                        dve.wait_ge(S["w_ready"], n - NV + 1)
                    dve.tensor_scalar(s, m, 1.0 / INT4_MAX, LEAST, ALU.mult, ALU.max).then_inc(S["sc_ready"], 1)
                    yield
                    dve.wait_ge(S["sc_ready"], n + 1)
                    dve.reciprocal(r, s).then_inc(S["rs_ready"], 1)
                    yield
                    dve.wait_ge(S["rs_ready"], n + 1)
                    dve.tensor_tensor(blocks(V[0:rows, n % NV, 0:w]), blocks(bank_w(n)[0:rows, 0:w]), bcast(r, BLK),
                                      ALU.mult).then_inc(S["scaled"], 1)
                    yield

                def clip(n):
                    v = V[0:rows_of(n), n % NV, 0:width_of(n)]
                    dve.wait_ge(S["rounded"], n + 1)
                    dve.tensor_scalar(v, v, INT4_MAX, -INT4_MAX - 1, ALU.min, ALU.max).then_inc(S["clipped"], 1)

                def take_lo(n):
                    _, m, r, rows = units[n]
                    dve.wait_ge(S["out_hi"], n + 1)
                    dve.tensor_tensor(W[m][1][:, :, r:r + rows], bank_out(n)[:, :, 0:rows],
                                      W[m][0][:, :, r:r + rows].bitcast(F32), ALU.subtract).then_inc(S["out_lo"], 1)

                for s in range(LAST):
                    scaling = to_scale(s - 1) if 1 <= s <= len(units) else iter([None] * 4)
                    if s < UP:
                        split_lo(s)
                    next(scaling)
                    if 3 <= s < len(units) + 3:
                        clip(s - 3)
                    next(scaling)
                    if BACK <= s < UP + BACK:
                        take_lo(s - BACK)
                    next(scaling)
                    next(scaling)


def ffn0_gather_x(nc, sem, ps, ident, X, mv, rstd, minus_half, pick, H, xb, g):
    with ExitStack() as here:
        sb = sb_in_stack(nc, here)
        xh = sb("g_xh", [P, 2, D])
        XTh, XTl = sb("g_XTh", [P, 2, KC, P], F32R), sb("g_XTl", [P, 2, KC, P], F32R)
        names = "eps_added rstd_ready xh_ready xt_psum xt_hi xt_lo xg_psum xg_copied xb_ready"
        S = {n: sem("g_" + n) for n in names.split()}
        psA = lambda u: ps[:, u, :]
        psG = lambda u: ps[:, 2 + u, :]
        with nc.Block() as block:
            @block.gpsimd
            def _(pool):
                pool.wait_ge(S["eps_added"], 1)
                pool.tensor_tensor(rstd[:], rstd[:], minus_half[:], ALU.pow).then_inc(S["rstd_ready"], 1)

            @block.tensor
            def _(pe):
                def turn(b, u):
                    pe.wait_ge(S["xh_ready"], b + 1)
                    pe.wait_ge(S["xt_lo"], b)
                    for k in range(KC):
                        last = pe.transpose(psA(u)[:, k * P:(k + 1) * P], xh[:, u, k * P:(k + 1) * P], ident[:])
                    last.then_inc(S["xt_psum"], 1)

                def body(pe, b, u, more):
                    if more:
                        turn(b + 1, 1 - u)
                    pe.wait_ge(S["xt_hi"], b + 1)
                    pe.wait_ge(S["xt_lo"], b + 2)
                    pe.wait_ge(S["xb_ready"], b + 1)
                    for k in range(KC):
                        pe.matmul(psG(u), XTh[:, u, k], pick[:, k], start=k == 0, stop=False)
                        last = pe.matmul(psG(u), XTl[:, u, k], pick[:, k], start=False, stop=k == KC - 1)
                    last.then_inc(S["xg_psum"], 1)

                pe.sem_inc(S["xt_lo"], 1)
                pe.sem_inc(S["xb_ready"], 2)
                turn(0, 0)
                rows_loop(body)(pe)

            @block.scalar
            def _(act):
                def hi(b, u):
                    act.wait_ge(S["xt_psum"], b + 1)
                    act.activation(XTh[:, u], psA(u).rearrange("p (k n) -> p k n", k=KC), ACT.Copy).then_inc(S["xt_hi"], 1)

                def body(act, b, u, more):
                    if more:
                        hi(b + 1, 1 - u)
                    act.wait_ge(S["xg_psum"], b + 1)
                    act.activation(H[:, b, 0:D], psG(u), ACT.Copy).then_inc(S["xg_copied"], 1)

                hi(0, 0)
                rows_loop(body)(act)

            @block.vector
            def _(dve):
                dve.tensor_scalar(rstd[:], mv[:, :, 1:2], EPS, None, ALU.add).then_inc(S["eps_added"], 1)

                def normalize(b, u):
                    dve.tensor_scalar(xh[:, u], X[:, b], mv[:, b, 0:1], rstd[:, b], ALU.subtract, ALU.mult)\
                       .then_inc(S["xh_ready"], 1)

                def lo(b, u):
                    dve.wait_ge(S["xt_hi"], b + 1)
                    dve.tensor_tensor(XTl[:, u], psA(u).rearrange("p (k n) -> p k n", k=KC), XTh[:, u].bitcast(F32),
                                      ALU.subtract).then_inc(S["xt_lo"], 1)

                def body(dve, b, u, more):
                    if more:
                        lo(b + 1, 1 - u)
                    if more >= 2:
                        normalize(b + 2, u)
                    dve.wait_ge(S["xg_copied"], b + 1)
                    dve.tensor_reduce(xb[:, b], blocks(psG(u)), AX.X, ALU.max, apply_absolute_value=True)\
                       .then_inc(S["xb_ready"], 1)

                dve.wait_ge(S["rstd_ready"], 1)
                normalize(0, 0)
                normalize(1, 1)
                lo(0, 0)
                rows_loop(body, last=3)(dve)
    whole_scale(nc, sem, xb, g, "x")


def whole_scale(nc, sem, bm, g, tag):
    part, reduced = sem(tag + "_max_part"), sem(tag + "_max_whole")
    with nc.Block() as block:
        @block.vector
        def _(dve):
            dve.tensor_reduce(g[:, 4:5], bm[:], AX.XY, ALU.max).then_inc(part, 1)
            link = Chain(dve, sem(tag + "_scale_link"))
            dve.wait_ge(reduced, 1)
            link(dve.tensor_scalar(g[:, 0:1], g[:, 5:6], 1.0 / (FP8_MAX * 6.0), LEAST, ALU.mult, ALU.max))
            link(dve.reciprocal(g[:, 1:2], g[:, 0:1]))
            link(dve.tensor_scalar(g[:, 2:3], g[:, 0:1], 0.5, None, ALU.mult))
            link(dve.tensor_scalar(g[:, 3:4], g[:, 2:3], g[:, 0:1], None, ALU.mult))

        @block.gpsimd
        def _(pool):
            pool.wait_ge(part, 1)
            pool.partition_all_reduce(g[:, 5:6], g[:, 4:5], P, bass.bass_isa.ReduceOp.max).then_inc(reduced, 1)


def block_scales(dve, link, bm, g, s, inv):
    link(dve.tensor_scalar(s, bm, g[:, 1:2], None, ALU.mult))
    link(dve.tensor_scalar(s, s, 1.0 / FP8_MAX, LEAST, ALU.mult, ALU.max))
    link(dve.reciprocal(inv, s))
    link(dve.tensor_scalar(inv, inv, g[:, 1:2], None, ALU.mult))


def ffn0_up(nc, sem, ps, ident, W, H, hb, xb, g):
    with ExitStack() as here:
        sb = sb_in_stack(nc, here)
        V, E, R, A = sb("u_V", [P, D]), sb("u_E", [P, D]), sb("u_R", [P, SELECT]), sb("u_A", [P, 2, D])
        sc, inv, bm = sb("u_sc", [P, D // BLK]), sb("u_inv", [P, D // BLK]), sb("u_bm", [P, 3, SELECT // BLK])
        ATh, ATl = sb("u_ATh", [P, 2, KC, P], F32R), sb("u_ATl", [P, 2, KC, P], F32R)
        T = sb("u_T", [P, I0])
        names = "a_ready at_psum at_hi at_lo gate_psum up_psum tanh_ready u_ready h_ready hb_ready"
        S = {n: sem("u_" + n) for n in names.split()}
        psA = lambda u: ps[:, u, :]
        gate = ps[:, 2:5, :].rearrange("p c n -> p (c n)")
        up = ps[:, 5:8, :].rearrange("p c n -> p (c n)")
        with nc.Block() as block:
            @block.tensor
            def _(pe):
                def turn(b, u):
                    pe.wait_ge(S["a_ready"], b + 1)
                    pe.wait_ge(S["at_lo"], b)
                    for k in range(KC):
                        last = pe.transpose(psA(u)[:, k * P:(k + 1) * P], A[:, u, k * P:(k + 1) * P], ident[:])
                    last.then_inc(S["at_psum"], 1)

                def product(out, u, w, pieces):
                    for c, n in pieces:
                        for k in range(KC):
                            last = mm3(pe, out[:, c:c + n], ATh[:, u, k], ATl[:, u, k], w[0][:, k, c:c + n],
                                       w[1][:, k, c:c + n], k == 0, k == KC - 1)
                    return last

                def body(pe, b, u, more):
                    pe.wait_ge(S["at_hi"], b + 1)
                    pe.wait_ge(S["at_lo"], b + 2)
                    need(pe, S["u_ready"], b)
                    product(gate, u, W[0], IC).then_inc(S["gate_psum"], 1)
                    need(pe, S["h_ready"], b)
                    product(up, u, W[1], IC[:-1])
                    if more:
                        turn(b + 1, 1 - u)
                    product(up, u, W[1], IC[-1:]).then_inc(S["up_psum"], 1)

                pe.sem_inc(S["at_lo"], 1)
                turn(0, 0)
                rows_loop(body)(pe)

            @block.scalar
            def _(act):
                def hi(b, u):
                    act.wait_ge(S["at_psum"], b + 1)
                    act.wait_ge(S["up_psum"], b)
                    act.activation(ATh[:, u], psA(u).rearrange("p (k n) -> p k n", k=KC), ACT.Copy).then_inc(S["at_hi"], 1)

                def body(act, b, u, more):
                    act.wait_ge(S["gate_psum"], b + 1)
                    need(act, S["h_ready"], b)
                    act.activation(T[:], gate[:, 0:I0], ACT.Tanh, scale=g[:, 2:3]).then_inc(S["tanh_ready"], 1)
                    if more:
                        hi(b + 1, 1 - u)

                act.sem_inc(S["up_psum"], 1)
                hi(0, 0)
                rows_loop(body)(act)

            @block.vector
            def _(dve):
                link = Chain(dve, sem("u_link"))

                def quantize(b, u):
                    link.row(b)
                    block_scales(dve, link, xb[:, b], g, sc[:], inv[:])
                    quantize_rows(dve, link, H[:, b, 0:D], inv[:], sc[:], V[:], E[:], R[:], A[:, u], bm, g[:, 1:2], D)\
                        .then_inc(S["a_ready"], 1)

                def lo(b, u):
                    dve.wait_ge(S["at_hi"], b + 1)
                    dve.tensor_tensor(ATl[:, u], psA(u).rearrange("p (k n) -> p k n", k=KC), ATh[:, u].bitcast(F32),
                                      ALU.subtract).then_inc(S["at_lo"], 1)

                def body(dve, b, u, more):
                    if more:
                        quantize(b + 1, 1 - u)
                    dve.wait_ge(S["tanh_ready"], b + 1)
                    dve.scalar_tensor_tensor(T[:], T[:], 1.0, gate[:, 0:I0], ALU.add, ALU.mult).then_inc(S["u_ready"], 1)
                    if more:
                        lo(b + 1, 1 - u)
                    dve.wait_ge(S["up_psum"], b + 2)
                    dve.wait_ge(S["u_ready"], b + 1)
                    dve.scalar_tensor_tensor(H[:, b], T[:], g[:, 3:4], up[:, 0:I0], ALU.mult, ALU.mult)\
                       .then_inc(S["h_ready"], 1)
                    dve.wait_ge(S["h_ready"], b + 1)
                    dve.tensor_reduce(hb[:, b], blocks(H[:, b]), AX.X, ALU.max, apply_absolute_value=True)\
                       .then_inc(S["hb_ready"], 1)

                quantize(0, 0)
                lo(0, 0)
                rows_loop(body)(dve)
    whole_scale(nc, sem, hb, g, "h")


def ffn0_down(nc, sem, ps, ident, scratch, X, stats, mv, H, hb, g):
    MT = len(IT)
    with ExitStack() as here:
        sb = sb_in_stack(nc, here)
        W = [sb(f"Wd{s}", [P, MT, D], F32R) for s in "hl"]
        sc, inv = sb("d_sc", [P, B, I0 // BLK]), sb("d_inv", [P, B, I0 // BLK])
        rows = sb("wdrows", [P, MT, D])
        V, E, R, A = sb("d_V", [P, 2, I0]), sb("d_E", [P, I0]), sb("d_R", [P, SELECT]), sb("d_A", [P, 2, I0])
        bm = sb("d_bm", [P, 3, SELECT // BLK])
        ATh, ATl = sb("d_ATh", [P, MT, P], F32R), sb("d_ATl", [P, MT, P], F32R)
        names = "w_loaded w_hi w_lo scales_ready v_scaled v_rounded normal_ready a_ready at_psum at_hi at_lo y_psum x_added stat_done"
        S = {n: sem("d_" + n) for n in names.split()}
        turned = lambda u: ps[:, 3 * u:3 * u + 3, :].rearrange("p c (m n) -> p (c m) n", n=P)
        y = lambda u: ps[:, 6 + u, :]
        full = I0 // P
        parts = [(P, slice(m, min(m + 4, full))) for m in range(0, full, 4)] + [(IT[-1][1], slice(full, MT))]
        NP = len(parts)
        N = I0 - SELECT
        with nc.Block() as block:
            @block.sync
            def _(sp):
                sp.dma_start(rows[:, 0:full], scratch["down"][0:full * P].rearrange("(m p) d -> p m d", p=P))\
                  .then_inc(S["w_loaded"], 16)
                sp.dma_start(rows[0:IT[-1][1], full], scratch["down"][full * P:I0]).then_inc(S["w_loaded"], 16)

            @block.tensor
            def _(pe):
                def body(pe, b, u, more):
                    pe.wait_ge(S["a_ready"], b + 1)
                    pe.wait_ge(S["normal_ready"], b + 1)
                    pe.wait_ge(S["at_lo"], NP * b)
                    for n, (m, w) in enumerate(IT):
                        last = pe.transpose(turned(u)[0:w, n], A[:, u, m:m + w], ident[:])
                    last.then_inc(S["at_psum"], 1)
                    pe.wait_ge(S["x_added"], b + 1)
                    if isinstance(b, int) and b == 0:
                        pe.wait_ge(S["w_lo"], MT)
                    for part, (w, m) in enumerate(parts):
                        pe.wait_ge(S["at_hi"], NP * b + part + 1)
                        pe.wait_ge(S["at_lo"], NP * (b + 1) + part + 1)
                        for n in range(m.start, m.stop):
                            last = mm3(pe, y(u), ATh[0:w, n], ATl[0:w, n], W[0][0:w, n], W[1][0:w, n], n == 0, n == MT - 1)
                    last.then_inc(S["y_psum"], 1)

                pe.sem_inc(S["at_lo"], NP)
                pe.sem_inc(S["x_added"], 2)
                rows_loop(body)(pe)

            @block.scalar
            def _(act):
                def body(act, b, u, more):
                    act.wait_ge(S["at_psum"], b + 1)
                    need(act, S["y_psum"], b)
                    for w, m in parts:
                        act.activation(ATh[0:w, m], turned(u)[0:w, m], ACT.Copy).then_inc(S["at_hi"], 1)

                act.wait_ge(S["w_loaded"], 32)
                for n, (_, w) in enumerate(IT):
                    act.activation(W[0][0:w, n], rows[0:w, n], ACT.Copy).then_inc(S["w_hi"], 1)
                rows_loop(body)(act)

            @block.gpsimd
            def _(pool):
                def scale_in(b, u):
                    if not isinstance(b, int) or b >= 2:
                        pool.wait_ge(S["a_ready"], b - 1)
                        pool.wait_ge(S["normal_ready"], b - 1)
                    pool.tensor_tensor(blocks(V[:, u]), blocks(H[:, b]), bcast(inv[:, b], BLK), ALU.mult)\
                        .then_inc(S["v_scaled"], 1)

                def scale_out(b, u):
                    pool.wait_ge(S["v_rounded"], b + 1)
                    if not isinstance(b, int) or b >= 2:
                        pool.wait_ge(S["at_psum"], b - 1)
                    pool.tensor_tensor(blocks(A[:, u, 0:N]), blocks(V[:, u, 0:N]), bcast(sc[:, b, 0:N // BLK], BLK),
                                       ALU.mult).then_inc(S["normal_ready"], 1)

                def body(pool, b, u, more):
                    if more:
                        scale_out(b + 1, 1 - u)
                    if more >= 3:
                        scale_in(b + 3, 1 - u)

                pool.wait_ge(S["scales_ready"], 1)
                scale_in(0, 0)
                pool.wait_ge(S["scales_ready"], 2)
                scale_in(1, 1)
                scale_out(0, 0)
                scale_in(2, 0)
                rows_loop(body, last=3)(pool)

            @block.vector
            def _(dve):
                link = Chain(dve, sem("d_link"))

                def normal(b, u):
                    link.row(b)
                    dve.wait_ge(S["v_scaled"], b + 1)
                    quantize_fp8(dve, link, V[:, u], E[:], EXPONENT)
                    dve.sem_inc(S["v_rounded"], 1)

                def outlier(b, u):
                    quantize_rest(dve, link, H[:, b, N:I0], sc[:, b, N // BLK:], V[:, u, N:I0], E[:, 0:SELECT], R[:],
                                  A[:, u, N:I0], bm, g[:, 1:2]).then_inc(S["a_ready"], 1)

                def body(dve, b, u, more):
                    if more:
                        normal(b + 1, 1 - u)
                    for part, (w, m) in enumerate(parts):
                        dve.wait_ge(S["at_hi"], NP * b + (part + 1 if part < NP - 2 else NP))
                        dve.tensor_tensor(ATl[0:w, m], turned(u)[0:w, m], ATh[0:w, m].bitcast(F32), ALU.subtract)\
                           .then_inc(S["at_lo"], 1)
                    if not isinstance(b, int) or b >= 1:
                        add(b - 1, 1 - u)
                    if more:
                        outlier(b + 1, 1 - u)

                def add(b, u):
                    dve.wait_ge(S["y_psum"], b + 1)
                    dve.scalar_tensor_tensor(X[:, b], y(u), g[:, 0:1], X[:, b], ALU.mult, ALU.add).then_inc(S["x_added"], 1)
                    dve.wait_ge(S["x_added"], b + 3)
                    dve.bn_stats(stats[:, b], X[:, b]).then_inc(S["stat_done"], 1)

                scales_link = Chain(dve, sem("d_scales_link"))
                for r in (slice(0, 1), slice(1, B)):
                    block_scales(dve, scales_link, hb[:, r], g, sc[:, r], inv[:, r])
                    dve.sem_inc(S["scales_ready"], 1)
                normal(0, 0)
                outlier(0, 0)
                for n, (_, w) in enumerate(IT):
                    dve.wait_ge(S["w_hi"], n + 1)
                    dve.tensor_tensor(W[1][0:w, n], rows[0:w, n], W[0][0:w, n].bitcast(F32), ALU.subtract)\
                       .then_inc(S["w_lo"], 1)
                rows_loop(body)(dve)
                add(B - 1, (B - 1) % 2)
                for b in range(B):
                    dve.wait_ge(S["stat_done"], b + 1)
                    dve.bn_aggr(mv[:, b], stats[:, b]).then_inc(S["stat_done"], 1)


def layer0_ffn(nc, t, sem, ps, ident, X, stats, mv, rstd, minus_half, scratch):
    with ExitStack() as here:
        sb = sb_in_stack(nc, here)
        H = sb("H", [P, B, I0])
        xb, hb, g = sb("xb", [P, B, D // BLK]), sb("hb", [P, B, I0 // BLK]), sb("g", [P, 6])
        with ExitStack() as weights:
            sbw = sb_in_stack(nc, weights)
            W = [[sbw(f"W{n}{s}", [P, KC, I0], F32R) for s in "hl"] for n in ("gate", "up")]
            with ExitStack() as reordering:
                pick = sb_in_stack(nc, reordering)("pick", [P, KC, D], F32R)
                work = H[:].rearrange("p b i -> p (b i)")
                ffn0_prepare_weights(nc, t, sem, ps, ident, scratch, work, pick, W)
                ffn0_gather_x(nc, sem, ps, ident, X, mv, rstd, minus_half, pick, H, xb, g)
            ffn0_up(nc, sem, ps, ident, W, H, hb, xb, g)
        ffn0_down(nc, sem, ps, ident, scratch, X, stats, mv, H, hb, g)

G1, J1, E1 = 8, 4, 128
W1 = J1 * E1
QK = W1 + E1
VE = E1 + 2
MULT = 0.08838834764831845
CAP = 30.0
MASKED = -1e30


def rope_tables():
    freq = (np.float32(1.0) / np.float32(10000.0) ** (np.arange(0, E1, 2, dtype=np.float32) / np.float32(E1))).astype(np.float32)
    phase = np.arange(P, dtype=np.float32)[:, None] * freq[None, :]
    c, s = np.cos(phase), np.sin(phase)
    return np.stack([np.concatenate([c, c], 1), np.concatenate([-s, s], 1)], 1).astype(np.float32)


def layer1_prepare(nc, t, S, sb, ps, ident, X, mv, rstd, minus_half, XTh, XTl, tables, bias, load_first, split_hi,
                   split_lo, slices, xh, rope, m, q_bias,
                   zero_weights, preset):
    m8, live = sb("m8", [P, P], mybir.dt.uint8), sb("live", [P, 1])
    psA = lambda u: ps[:, u, :]
    psM = ps[:, 2, 0:P]
    with nc.Block() as block:
        @block.sync
        def _(sp):
            sp.dma_start(rope, t["rope"]).then_inc(S["tables_loaded"], 16)
            sp.dma_start(m8[:], t["mask"]).then_inc(S["tables_loaded"], 16)
            load_first(sp)

        @block.gpsimd
        def _(pool):
            pool.wait_ge(S["eps_added"], 1)
            pool.tensor_tensor(rstd[:], rstd[:], minus_half[:], ALU.pow).then_inc(S["rstd_ready"], 1)
            for x in zero_weights:
                pool.memset(x[:].bitcast(F32), 0.0).then_inc(S["preset"], 1)
            for w in range(KC):
                split_lo(pool, 0, w, w + 1)

        @block.tensor
        def _(pe):
            def body(pe, b, u, more):
                pe.wait_ge(S["xh_ready"], b + 1)
                if not isinstance(b, int) or b >= 2:
                    pe.wait_ge(S["xt_lo"], b - 1)
                for k in range(KC):
                    last = pe.transpose(psA(u)[:, k * P:(k + 1) * P], xh[u][:, k * P:(k + 1) * P], ident[:])
                last.then_inc(S["xt_psum"], 1)

            rows_loop(body)(pe)
            pe.wait_ge(S["q_bias_steps"], 4)
            pe.transpose(psM, q_bias, ident[:]).then_inc(S["mask_turned"], 1)

        @block.scalar
        def _(act):
            def body(act, b, u, more):
                act.wait_ge(S["xt_psum"], b + 1)
                act.activation(XTh[:, b], psA(u).rearrange("p (k n) -> p k n", k=KC), ACT.Copy).then_inc(S["xt_hi"], 1)
                for w in beside.get(b, []) if isinstance(b, int) else []:
                    act.wait_ge(S["w_loaded"], 48)
                    split_hi(act, 0, w)

            beside = {0: [0, 1], B - 3: [2], B - 2: [3]}
            act.wait_ge(S["q_bias_steps"], 2)
            for n in range(2):
                for h in range(J1):
                    act.activation(tables[:, n, h], rope[:, n], ACT.Copy, scale=live[:])
                act.activation(tables[:, n, J1], rope[:, n], ACT.Copy)
            rows_loop(body, last=3)(act)
            act.wait_ge(S["wo_loaded"], 16)
            for w in range(KC, len(slices)):
                split_hi(act, 0, w)

        @block.vector
        def _(dve):
            dve.tensor_scalar(rstd[:], mv[:, :, 1:2], EPS, None, ALU.add).then_inc(S["eps_added"], 1)
            preset(dve)
            link = Chain(dve, S["q_bias_steps"])
            dve.wait_ge(S["tables_loaded"], 32)
            link(dve.tensor_copy(m, m8[:]))
            link(dve.tensor_reduce(live[:], m, AX.X, ALU.max))
            link(dve.tensor_scalar(q_bias, m, 1.0, live[:], ALU.subtract, ALU.mult))
            link(dve.tensor_scalar(q_bias, q_bias, -MASKED / CAP, None, ALU.mult))

            def unit(b, u):
                dve.tensor_scalar(xh[u], X[:, b], mv[:, b, 0:1], rstd[:, b], ALU.subtract, ALU.mult)\
                   .then_inc(S["xh_ready"], 1)

            def body(dve, b, u, more):
                dve.wait_ge(S["xt_hi"], b + 1)
                if more >= 2:
                    unit(b + 2, u)
                dve.tensor_tensor(XTl[:, b], psA(u).rearrange("p (k n) -> p k n", k=KC), XTh[:, b].bitcast(F32),
                                  ALU.subtract).then_inc(S["xt_lo"], 1)

            dve.wait_ge(S["rstd_ready"], 1)
            unit(0, 0)
            unit(1, 1)
            rows_loop(body, last=3)(dve)
            dve.wait_ge(S["mask_turned"], 1)
            dve.tensor_copy(bias[:], psM).then_inc(S["bias_ready"], 1)


def layer1_attention(nc, t, sem, ps, X, stats, mv, rstd, minus_half, ident, CTh, CTl, XTh, XTl, tables, bias):
    with ExitStack() as here:
        sb = sb_in_stack(nc, here)
        qkv_in = sb("qkv_in", [P, KC, QK + E1])
        o_in = qkv_in[:].rearrange("p k n -> p (k n)")[:, 0:J1 * D].rearrange("p (j n) -> p j n", n=D)
        Wi = [[sb(f"Wi{n}{s}", [P, KC, QK + E1], F32R) for s in "hl"] for n in range(2)]
        Wo = [[sb(f"Wo1{n}{s}", [P, J1, D], F32R) for s in "hl"] for n in range(2)]
        T1, T2 = sb("T1", [P, QK]), sb("T2", [P, QK])
        QTh, QTl = sb("QTh", [P, QK], F32R), sb("QTl", [P, QK], F32R)
        V = [sb(f"V1{s}", [P, 2, VE], F32R) for s in "hl"]
        E = sb("E", [P, W1])
        Ph, Pl = sb("Ph", [P, W1], F32R), sb("Pl", [P, W1], F32R)
        rden, A = sb("rden1", [P, J1]), sb("A1", [P, J1, E1])
        AT = [sb(f"AT{s}", [P, 2, J1, P], F32R) for s in "hl"]
        names = ("w_loaded wo_loaded w_hi w_lo q_psum kv_psum t_one t_two v_hi v_lo q_sum k_sum qk_psum qk_hi qk_lo s_psum tanh_ready masked "
                 "exp_ready p_hi p_lo pv_psum rden_ready a_ready at_psum at_hi at_lo y_psum x_added preset stat_done "
                 "tables_loaded eps_added rstd_ready xh_ready xt_psum xt_hi xt_lo q_bias_steps mask_turned bias_ready")
        S = {n: sem("s_" + n) for n in names.split()}
        qkv = ps[:, 0:2, :].rearrange("p c n -> p (c n)")
        turned = ps[:, 2:4, :].rearrange("p c n -> p (c n)")
        psS = ps[:, 4, :]
        psV = ps[:, 5:7, 0:2 * VE].rearrange("p c (j e) -> p c j e", e=VE)
        psA = ps[:, 5, :]
        psY = ps[:, 7, :]
        slices = [(True, k) for k in range(KC)] + [(False, j) for j in range(J1)]
        plan = {1: [0], 2: [1], 3: [2], 4: [3], 5: [4, 5], 6: [6, 7]}

        def steps(eng, body):
            with eng.Fori(0, G1 // 2) as i:
                for n in range(2):
                    for b in range(B):
                        body(i * 2 + n, n, b, i * (2 * B) + (n * B + b))

        def split_slice(n, w):
            inputs, k = slices[w]
            return (qkv_in[:, k], [x[:, k] for x in Wi[n]]) if inputs else (o_in[:, k], [x[:, k] for x in Wo[n]])

        def load(sp, g, n):
            if n:
                sp.wait_ge(S["w_lo"], n * len(slices))
            for dst, src in ((qkv_in[:, :, 0:W1], t["Wq1"][g]), (qkv_in[:, :, W1:QK], t["Wk1"][g]),
                             (qkv_in[:, :, QK:QK + E1], t["Wv1"][g])):
                sp.dma_start(dst, src).then_inc(S["w_loaded"], 16)
            sp.wait_ge(S["w_lo"], n * len(slices) + KC)
            sp.dma_start(o_in, t["Wo1"][g]).then_inc(S["wo_loaded"], 16)

        def split_hi(act, n, w):
            src, (hi, lo) = split_slice(n, w)
            act.activation(hi, src, ACT.Copy).then_inc(S["w_hi"], 1)

        def split_lo(pool, n, w, count):
            src, (hi, lo) = split_slice(n, w)
            pool.wait_ge(S["w_hi"], count)
            pool.tensor_tensor(lo, src, hi.bitcast(F32), ALU.subtract).then_inc(S["w_lo"], 1)

        def preset(dve):
            for u in range(2):
                dve.memset(V[0][:, u, E1:VE].bitcast(F32), 1.0).then_inc(S["preset"], 1)
                dve.memset(V[1][:, u, E1:VE].bitcast(F32), 0.0).then_inc(S["preset"], 1)
            for x in AT:
                dve.memset(x[:, 1].bitcast(F32), 0.0).then_inc(S["preset"], 1)

        with ExitStack() as preparing:
            layer1_prepare(nc, t, S, sb_in_stack(nc, preparing), ps, ident, X, mv, rstd, minus_half, XTh, XTl, tables,
                           bias, lambda sp: load(sp, 0, 0), split_hi, split_lo, slices,
                           [x[:, 0:D] for x in (T1, T2)], A[:, 0:2], A[:, 2], A[:, 3], Wo[1], preset)

        with nc.Block() as block:
            @block.sync
            def _(sp):
                for g in range(1, G1):
                    load(sp, g, g)
                load(sp, 0, G1)

            @block.gpsimd
            def _(pool):
                for w in range(KC, len(slices)):
                    split_lo(pool, 0, w, w + 1)

                def body(g, n, b, s):
                    for w in plan.get(b, []):
                        split_lo(pool, 1 - n, w, (g + 1) * len(slices) + w + 1)

                steps(pool, body)

            @block.tensor
            def _(pe):
                def project(n, b):
                    for k in range(KC):
                        last = mm3(pe, qkv[:, 0:W1], XTh[:, b, k], XTl[:, b, k], Wi[n][0][:, k, 0:W1],
                                   Wi[n][1][:, k, 0:W1], k == 0, k == KC - 1)
                    last.then_inc(S["q_psum"], 1)
                    for k in range(KC):
                        c = slice(b * P, (b + 1) * P)
                        last = mm3(pe, qkv[:, W1:QK + E1], CTh[:, k, c], CTl[:, k, c], Wi[n][0][:, k, W1:QK + E1],
                                   Wi[n][1][:, k, W1:QK + E1], k == 0, k == KC - 1)
                    last.then_inc(S["kv_psum"], 1)

                def turn(s):
                    pe.wait_ge(S["q_sum"], s + 1)
                    pe.wait_ge(S["k_sum"], s + 1)
                    for j in range(J1 + 1):
                        last = pe.transpose(turned[:, j * P:(j + 1) * P], T1[:, j * E1:(j + 1) * E1], ident[:])
                    last.then_inc(S["qk_psum"], 1)

                def output(n, u, heads):
                    for j in heads:
                        last = mm3(pe, psY, AT[0][:, u, j], AT[1][:, u, j], Wo[n][0][:, j], Wo[n][1][:, j],
                                   j == 0, j == J1 - 1)
                    return last

                def body(g, n, b, s):
                    u = b % 2
                    pe.wait_ge(S["qk_lo"], s + 1)
                    mm3(pe, psS, QTh[:, W1:QK], QTl[:, W1:QK], QTh[:, 0:W1], QTl[:, 0:W1], True, True)\
                        .then_inc(S["s_psum"], 1)
                    n2, b2 = (n, b + 1) if b + 1 < B else (1 - n, 0)
                    if b2 == 0:
                        pe.wait_ge(S["w_lo"], (g + 2) * len(slices))
                    pe.wait_ge(S["v_lo"], s + 1)
                    project(n2, b2)
                    pe.wait_ge(S["p_lo"], s + 1)
                    pe.wait_ge(S["at_lo"], s + 1)
                    for j in range(J1):
                        p = slice(j * P, (j + 1) * P)
                        last = mm3(pe, psV[:, j // 2, j % 2], Ph[:, p], Pl[:, p], V[0][:, u], V[1][:, u], True, True)
                    last.then_inc(S["pv_psum"], 1)
                    n0 = n if b else 1 - n
                    pe.wait_ge(S["x_added"], s + 1)
                    if b == 1:
                        pe.wait_ge(S["w_lo"], (g + 1) * len(slices))
                    output(n0, 1 - u, (0, 1))
                    turn(s + 1)
                    output(n0, 1 - u, (2,))
                    pe.wait_ge(S["a_ready"], s + 2)
                    for j in range(J1):
                        last = pe.transpose(psA[:, j * P:(j + 1) * P], A[:, j], ident[:])
                    last.then_inc(S["at_psum"], 1)
                    output(n0, 1 - u, (3,)).then_inc(S["y_psum"], 1)

                project(0, 0)
                turn(0)
                steps(pe, body)
                pe.wait_ge(S["at_lo"], G1 * B + 1)
                pe.wait_ge(S["x_added"], G1 * B + 1)
                output(1, 1, range(J1)).then_inc(S["y_psum"], 1)

            @block.scalar
            def _(act):
                def inputs(s, u):
                    act.wait_ge(S["kv_psum"], s + 1)
                    act.activation(V[0][:, u, 0:E1], qkv[:, QK:QK + E1], ACT.Copy).then_inc(S["v_hi"], 1)
                    act.wait_ge(S["qk_psum"], s + 1)
                    act.activation(QTh[:], turned[:, 0:QK], ACT.Copy).then_inc(S["qk_hi"], 1)

                inputs(0, 0)

                def body(g, n, b, s):
                    u = b % 2
                    act.wait_ge(S["s_psum"], s + 1)
                    act.activation(E[:], psS, ACT.Tanh, scale=MULT / CAP).then_inc(S["tanh_ready"], 1)
                    if b in plan:
                        if b == 1:
                            act.wait_ge(S["w_loaded"], (g + 2) * 48)
                        if b == 5:
                            act.wait_ge(S["wo_loaded"], (g + 2) * 16)
                        for w in plan[b]:
                            split_hi(act, 1 - n, w)
                    act.wait_ge(S["masked"], s + 1)
                    act.activation(E[:], E[:], ACT.Exp, scale=CAP).then_inc(S["exp_ready"], 1)
                    act.wait_ge(S["exp_ready"], s + 1)
                    act.activation(Ph[:], E[:], ACT.Copy).then_inc(S["p_hi"], 1)
                    inputs(s + 1, 1 - u)
                    act.wait_ge(S["at_psum"], s + 1)
                    act.activation(AT[0][:, u], psA.rearrange("p (j n) -> p j n", j=J1), ACT.Copy).then_inc(S["at_hi"], 1)

                steps(act, body)

            @block.vector
            def _(dve):
                def rotate(s, h):
                    split = lambda x: x.rearrange("p (h a e) -> p h a e", h=J1 + 1, a=2)[:, h]
                    half = lambda x: x[:, h].rearrange("p h (a e) -> p h a e", a=2)
                    src = split(qkv[:, 0:QK])
                    dve.tensor_tensor(split(T1[:]), src, half(tables[:, 0]), ALU.mult).then_inc(S["t_one"], 1)
                    dve.tensor_tensor(split(T2[:]), src[:, :, ::-1], half(tables[:, 1]), ALU.mult)\
                       .then_inc(S["t_two"], 1)

                def rope_q(s):
                    dve.wait_ge(S["q_psum"], s + 1)
                    rotate(s, slice(0, J1))
                    dve.wait_ge(S["t_one"], 2 * s + 1)
                    dve.wait_ge(S["t_two"], 2 * s + 1)
                    dve.tensor_tensor(T1[:, 0:W1], T1[:, 0:W1], T2[:, 0:W1], ALU.add).then_inc(S["q_sum"], 1)

                def rope_k(s, u):
                    dve.wait_ge(S["v_hi"], s + 1)
                    rotate(s, slice(J1, J1 + 1))
                    dve.tensor_tensor(V[1][:, u, 0:E1], qkv[:, QK:QK + E1], V[0][:, u, 0:E1].bitcast(F32), ALU.subtract)\
                       .then_inc(S["v_lo"], 1)
                    dve.wait_ge(S["t_one"], 2 * s + 2)
                    dve.wait_ge(S["t_two"], 2 * s + 2)
                    dve.tensor_tensor(T1[:, W1:QK], T1[:, W1:QK], T2[:, W1:QK], ALU.add).then_inc(S["k_sum"], 1)

                def low(s):
                    dve.wait_ge(S["qk_hi"], s + 1)
                    dve.tensor_tensor(QTl[:], turned[:, 0:QK], QTh[:].bitcast(F32), ALU.subtract).then_inc(S["qk_lo"], 1)

                def add(s, b):
                    dve.wait_ge(S["y_psum"], s)
                    dve.tensor_tensor(X[:, b], psY, X[:, b], ALU.add).then_inc(S["x_added"], 1)

                def statistics(s, b):
                    dve.wait_ge(S["x_added"], s)
                    dve.bn_stats(stats[:, b], X[:, b]).then_inc(S["stat_done"], 1)

                for name in ("at_lo", "a_ready", "x_added"):
                    dve.sem_inc(S[name], 1)
                rope_q(0)
                rope_k(0, 0)
                low(0)

                def body(g, n, b, s):
                    u = b % 2
                    dve.wait_ge(S["tanh_ready"], s + 1)
                    dve.tensor_tensor(E[:].rearrange("p (j q) -> p j q", j=J1), E[:].rearrange("p (j q) -> p j q", j=J1),
                                      bias[:].unsqueeze(1).broadcast_to([P, J1, P]), ALU.add).then_inc(S["masked"], 1)
                    statistics(s + 1, (b - 2) % B)
                    dve.wait_ge(S["p_hi"], s + 1)
                    dve.tensor_tensor(Pl[:], E[:], Ph[:].bitcast(F32), ALU.subtract).then_inc(S["p_lo"], 1)
                    rope_q(s + 1)
                    rope_k(s + 1, 1 - u)
                    dve.wait_ge(S["pv_psum"], s + 1)
                    r = rden[:].rearrange("p (c j) -> p c j", c=2)
                    dve.reciprocal(r, psV[:, :, :, E1]).then_inc(S["rden_ready"], 1)
                    dve.wait_ge(S["rden_ready"], s + 1)
                    dve.tensor_tensor(A[:].rearrange("p (c j) e -> p c j e", c=2), psV[:, :, :, 0:E1], bcast(r, E1),
                                      ALU.mult).then_inc(S["a_ready"], 1)
                    low(s + 1)
                    dve.wait_ge(S["at_hi"], s + 1)
                    dve.tensor_tensor(AT[1][:, u], psA.rearrange("p (j n) -> p j n", j=J1), AT[0][:, u].bitcast(F32),
                                      ALU.subtract).then_inc(S["at_lo"], 1)
                    add(s + 1, (b - 1) % B)

                steps(dve, body)
                add(G1 * B + 1, B - 1)
                statistics(G1 * B + 1, B - 2)
                statistics(G1 * B + 2, B - 1)
                dve.wait_ge(S["stat_done"], G1 * B + 2)
                for b in range(B):
                    dve.bn_aggr(mv[:, b], stats[:, b]).then_inc(S["stat_done"], 1)


def layer1_ffn(nc, t, sem, ps, ident, X, mv, rstd, minus_half):
    IB = 32
    OC = D // P
    with ExitStack() as here:
        sb = sb_in_stack(nc, here)
        WT = [sb(f"WT{s}", [P, KC, D], F32R) for s in "hl"]
        add_bias = sb("add_bias", [P, D])
        packed = sb("packed", [P, OC, D // 2], I32)
        q = sb("q", [P, OC, D // 2, 2], I32)
        W = sb("W1f", [P, OC, D])
        s16, v8 = sb("s16", [P, OC, D // IB], mybir.dt.float16), sb("v8", [P, OC, D // IB], mybir.dt.uint8)
        sc, half = sb("sc1", [P, OC, D // IB]), sb("half1", [P, OC, D // IB])
        xh = sb("f_xh", [P, 2, D])
        XTh, XTl = sb("f_XTh", [P, 2, KC, P], F32R), sb("f_XTl", [P, 2, KC, P], F32R)
        names = ("loaded bias_loaded unpack_link w_done w_turned w_hi w_lo eps_added rstd_ready xh_ready xt_psum xt_hi xt_lo "
                 "y_psum biased out_ready stored")
        S = {n: sem("f_" + n) for n in names.split()}
        psA = lambda u: ps[:, u, :]
        psY = lambda u: ps[:, 2 + u, :]
        psW = lambda k: ps[:, 4 + k, :]
        out = t["out"].rearrange("b p d -> p b d")
        with nc.Block() as block:
            @block.gpsimd
            def _(pool):
                pool.wait_ge(S["eps_added"], 1)
                pool.tensor_tensor(rstd[:], rstd[:], minus_half[:], ALU.pow).then_inc(S["rstd_ready"], 1)
                pool.wait_ge(S["bias_loaded"], 16)

                def body(pool, b, u, more):
                    pool.wait_ge(S["xh_ready"], b + 1)
                    pool.tensor_tensor(X[:, b], X[:, b], add_bias[:], ALU.add).then_inc(S["biased"], 1)

                rows_loop(body)(pool)

            @block.tensor
            def _(pe):
                def turn(b, u):
                    pe.wait_ge(S["xh_ready"], b + 1)
                    pe.wait_ge(S["xt_lo"], b)
                    for k in range(KC):
                        last = pe.transpose(psA(u)[:, k * P:(k + 1) * P], xh[:, u, k * P:(k + 1) * P], ident[:])
                    last.then_inc(S["xt_psum"], 1)

                def body(pe, b, u, more):
                    if more:
                        turn(b + 1, 1 - u)
                    pe.wait_ge(S["xt_hi"], b + 1)
                    pe.wait_ge(S["xt_lo"], b + 2)
                    pe.wait_ge(S["out_ready"], b + 1)
                    for k in range(KC):
                        last = mm3(pe, psY(u), XTh[:, u, k], XTl[:, u, k], WT[0][:, k], WT[1][:, k], k == 0, k == KC - 1)
                    last.then_inc(S["y_psum"], 1)

                pe.sem_inc(S["xt_lo"], 1)
                pe.sem_inc(S["out_ready"], 2)
                turn(0, 0)
                for o in range(OC):
                    pe.wait_ge(S["w_done"], o + 1)
                    for k in range(KC):
                        last = pe.transpose(psW(k)[:, o * P:(o + 1) * P], W[:, o, k * P:(k + 1) * P], ident[:])
                        if o == OC - 1:
                            last.then_inc(S["w_turned"], 1)
                pe.wait_ge(S["w_hi"], KC)
                pe.wait_ge(S["w_lo"], KC)
                rows_loop(body)(pe)

            @block.scalar
            def _(act):
                def x_hi(b, u):
                    act.wait_ge(S["xt_psum"], b + 1)
                    act.wait_ge(S["out_ready"], b + 1)
                    act.activation(XTh[:, u], psA(u).rearrange("p (k n) -> p k n", k=KC), ACT.Copy).then_inc(S["xt_hi"], 1)

                def body(act, b, u, more):
                    if more:
                        x_hi(b + 1, 1 - u)

                x_hi(0, 0)
                for k in range(KC):
                    act.wait_ge(S["w_turned"], k + 1)
                    act.activation(WT[0][:, k], psW(k), ACT.Copy).then_inc(S["w_hi"], 1)
                rows_loop(body)(act)

            @block.vector
            def _(dve):
                dve.tensor_scalar(rstd[:], mv[:, :, 1:2], EPS, None, ALU.add).then_inc(S["eps_added"], 1)

                def normalize(b, u):
                    dve.tensor_scalar(xh[:, u], X[:, b], mv[:, b, 0:1], rstd[:, b], ALU.subtract, ALU.mult)\
                       .then_inc(S["xh_ready"], 1)

                def split(b, u):
                    dve.wait_ge(S["xt_hi"], b + 1)
                    dve.tensor_tensor(XTl[:, u], psA(u).rearrange("p (k n) -> p k n", k=KC), XTh[:, u].bitcast(F32),
                                      ALU.subtract).then_inc(S["xt_lo"], 1)

                def body(dve, b, u, more):
                    if more:
                        split(b + 1, 1 - u)
                    if more >= 2:
                        normalize(b + 2, u)
                    dve.wait_ge(S["y_psum"], b + 1)
                    dve.wait_ge(S["biased"], b + 1)
                    dve.tensor_tensor(X[:, b], psY(u), X[:, b], ALU.add).then_inc(S["out_ready"], 1)

                dve.wait_ge(S["rstd_ready"], 1)
                normalize(0, 0)
                normalize(1, 1)
                split(0, 0)
                link = Chain(dve, S["unpack_link"])
                dve.wait_ge(S["loaded"], 48)
                link(dve.tensor_scalar(q[:, :, :, 0], packed[:], 15, None, ALU.bitwise_and))
                link(dve.tensor_scalar(q[:, :, :, 1], packed[:], 4, 15, ALU.logical_shift_right, ALU.bitwise_and))
                link(dve.tensor_scalar(half[:], v8[:], 0.5, 0.5, ALU.mult, ALU.add))
                link(dve.tensor_tensor(sc[:], half[:], s16[:], ALU.mult))
                for o in range(OC):
                    dve.scalar_tensor_tensor(W[:, o].rearrange("p (b e) -> p b e", e=IB),
                                             q[:, o].rearrange("p (b e) c -> p b (e c)", b=D // IB), -8.0,
                                             bcast(sc[:, o], IB), ALU.add, ALU.mult).then_inc(S["w_done"], 1)
                for k in range(KC):
                    dve.wait_ge(S["w_hi"], k + 1)
                    dve.tensor_tensor(WT[1][:, k], psW(k), WT[0][:, k].bitcast(F32), ALU.subtract).then_inc(S["w_lo"], 1)
                rows_loop(body, last=3)(dve)

            @block.sync
            def _(sp):
                def body(sp, b, u, more):
                    sp.wait_ge(S["out_ready"], b + 3)
                    sp.dma_start(out[:, b], X[:, b]).then_inc(S["stored"], 16)

                sp.dma_start(packed[:], t["packed"]).then_inc(S["loaded"], 16)
                sp.dma_start(s16[:], t["scale"]).then_inc(S["loaded"], 16)
                sp.dma_start(v8[:], t["var_mask"]).then_inc(S["loaded"], 16)
                sp.dma_start(add_bias[:], t["L1_ffn_bias"].partition_broadcast(P)).then_inc(S["bias_loaded"], 16)
                rows_loop(body)(sp)
                sp.wait_ge(S["stored"], 16 * B)


_INS = ["x", "ctx_4096", "L0_xattn_Wq", "L0_xattn_Wk", "L0_xattn_Wv", "L0_xattn_Wo",
        "L0_ffn_w_gate", "L0_ffn_w_up", "L0_ffn_w_down", "L0_ffn_ri_in", "L1_ffn_bias"]
STOP = 4


def kernel(**inputs):
    import concourse.bacc as bacc
    from concourse.bass_utils import run_bass_kernel_spmd as run

    nc = bacc.Bacc("TRN2", target_bir_lowering=False, num_devices=1)
    arrays, t = {}, {}
    ri_in, ri_mid = np.asarray(inputs["L0_ffn_ri_in"]), np.asarray(inputs["L0_ffn_ri_mid"])
    full = I0 // P * P
    inputs = {**inputs, "ri_in_columns": ri_in.reshape(KC, P).T, "ri_mid_columns": ri_mid[:full].reshape(-1, P).T,
              "ri_mid_rest": ri_mid[full:].reshape(-1, 1)}
    get = lambda name: np.asarray(inputs[name])
    inputs["Wq1"] = get("L1_xattn_Wq").reshape(KC, P, G1, W1).transpose(2, 1, 0, 3)
    inputs["Wk1"] = get("L1_xattn_Wk").reshape(KC, P, G1, E1).transpose(2, 1, 0, 3)
    inputs["Wv1"] = get("L1_xattn_Wv").reshape(KC, P, G1, E1).transpose(2, 1, 0, 3)
    inputs["Wo1"] = get("L1_xattn_Wo").reshape(G1, J1, P, D).transpose(0, 2, 1, 3)
    inputs["rope"] = rope_tables()
    inputs["mask"] = get("mask_1x1xSxS2_bk0").reshape(P, P)
    inputs["packed"] = get("L1_ffn_weight_packed").reshape(D // P, P, D // 2).transpose(1, 0, 2)
    inputs["scale"] = get("L1_ffn_weight_scale").reshape(D // P, P, -1).transpose(1, 0, 2)
    inputs["var_mask"] = get("L1_ffn_weight_var_mask").reshape(D // P, P, -1).transpose(1, 0, 2)
    made = ["ri_in_columns", "ri_mid_columns", "ri_mid_rest", "Wq1", "Wk1", "Wv1", "Wo1", "rope", "mask", "packed",
            "scale", "var_mask"]
    for name in _INS + made:
        a = np.asarray(inputs[name])
        if name == "L0_xattn_Wq":
            a = a.reshape(D, PAIRS, 2, J0, E0).transpose(0, 1, 3, 2, 4).reshape(D, D)
        if name == "L0_ffn_w_down":
            a = a.T
        a = np.ascontiguousarray(a)
        arrays["in_" + name] = a
        t[name] = nc.dram_tensor("in_" + name, a.shape, mybir.dt.from_np(a.dtype), kind="ExternalInput").ap()
    t["out"] = nc.dram_tensor("out_x", (B, P, D), F32, kind="ExternalOutput").ap()
    program(nc, t, STOP)
    return run(nc, [arrays], core_ids=[0]).results[0]["out_x"]
```
